# Optimizing a Trainium2 kernel written in Bass

```python
import numpy as np
import jax
import jax.numpy as jnp

def _softmax(x, axis=-1):
    return jax.nn.softmax(x, axis=axis)

def _gelu(x):
    return jax.nn.gelu(x, approximate=True)

def _silu(x):
    return jax.nn.silu(x)

def _sigmoid(x):
    return jax.nn.sigmoid(x)

def _layernorm(x, axis=-1, eps=1e-05):
    m = jnp.mean(x, axis=axis, keepdims=True)
    v = jnp.var(x, axis=axis, keepdims=True)
    return (x - m) / jnp.sqrt(v + eps)

def _scatter_add(tgt, idx, src, axis=0):
    return tgt.at[idx].add(src)

def _segment_sum(src, seg, n):
    return jax.ops.segment_sum(src, seg, n)
kernel_name = 'mk_decoder_preln_d1_seqx_r4_98bcc9'

def setup_inputs(seed: int=0):
    np.random.seed(seed)
    _w = jnp.asarray

    def _rec_inputs():
        import jax
        import jax.numpy as jnp
        _rk = jax.random.key(seed)
        x = 7.22e-05 + 1 * jax.random.normal(jax.random.fold_in(_rk, 1), (1, 2048, 256), jnp.float32)
        _lenS = 2048 - jax.random.randint(jax.random.fold_in(_rk, 7), (1,), 0, max(1, 2048 // 4) + 1, jnp.int32)
        _lenS2 = 1601 - jax.random.randint(jax.random.fold_in(_rk, 8), (1,), 0, max(1, 1601 // 4) + 1, jnp.int32)
        _ctx_1024P = jax.random.normal(jax.random.fold_in(_rk, 11), (1, 16, 256), jnp.float32)
        _ctx_1024c = jax.random.dirichlet(jax.random.fold_in(_rk, 511), 0.3 * jnp.ones((16,), jnp.float32), (1, 1601))
        _ctx_1024t = jnp.einsum('bsk,bkd->bsd', _ctx_1024c, _ctx_1024P)
        _ctx_1024t = _ctx_1024t * jax.lax.rsqrt(jnp.mean(jnp.square(_ctx_1024t)) + 1e-12) * 0.953939
        ctx_1024 = 4.13588e-05 + 0.999923 * (_ctx_1024t + 0.3 * jax.random.normal(jax.random.fold_in(_rk, 611), (1, 1601, 256), jnp.float32))
        return (x, ctx_1024)
    x, ctx_1024 = _rec_inputs()

    def _L0_attn_setup():
        import jax, jax.numpy as jnp
        import numpy as np
        B, N, D, H = (4, 512, 256, 16)
        HD = D // H
        CHUNK = 64
        BASE = 10000.0
        EPS = 1e-06

        def _lrpe(x, theta):
            c = jnp.cos(theta)[None, :, None, :]
            s = jnp.sin(theta)[None, :, None, :]
            return jnp.concatenate([x * c, x * s], axis=-1)

        def _chunk_gla(q, k, v, g):
            b, n, h, dk = q.shape
            dv = v.shape[-1]
            nc = n // CHUNK

            def to_chunks(t):
                return t.reshape(b, nc, CHUNK, t.shape[2], t.shape[3]).transpose(1, 0, 2, 3, 4)
            qc, kc, vc, gc = map(to_chunks, (q, k, v, g))
            mask = jnp.tril(jnp.ones((CHUNK, CHUNK), bool))

            def step(S, inp):
                qi, ki, vi, gi = inp
                G = jnp.cumsum(gi, axis=1)
                q_g = qi * jnp.exp(G)
                k_g = ki * jnp.exp(-G)
                o_inter = jnp.einsum('bchk,bhkv->bchv', q_g, S)
                A = jnp.einsum('bchk,bshk->bhcs', q_g, k_g)
                A = jnp.where(mask[None, None], A, 0.0)
                o_intra = jnp.einsum('bhcs,bshv->bchv', A, vi)
                G_last = G[:, -1:]
                S = S * jnp.exp(G_last[:, 0])[..., None] + jnp.einsum('bchk,bchv->bhkv', ki * jnp.exp(G_last - G), vi)
                return (S, o_inter + o_intra)
            S0 = jnp.zeros((b, h, dk, dv), q.dtype)
            _, o = jax.lax.scan(step, S0, (qc, kc, vc, gc))
            return o.transpose(1, 0, 2, 3, 4).reshape(b, n, h, dv)
        key = jax.random.key(seed)
        ks = jax.random.split(key, 8)
        s = 0.02
        return {'x': jax.random.normal(ks[0], (B, N, D), jnp.float32), 'Wq': jax.random.normal(ks[1], (D, D), jnp.float32) * s, 'Wk': jax.random.normal(ks[2], (D, D), jnp.float32) * s, 'Wv': jax.random.normal(ks[3], (D, D), jnp.float32) * s, 'Wo': jax.random.normal(ks[4], (D, D), jnp.float32) * s, 'Wg1': jax.random.normal(ks[5], (D, H), jnp.float32) * s, 'Wg2': jax.random.normal(ks[6], (H, D), jnp.float32) * s, 'norm_w': jnp.ones((D,), jnp.float32)}
    _L0_attn_all = _L0_attn_setup()
    _L0_attn_in = {k: v for k, v in _L0_attn_all.items() if k in ('Wq', 'Wk', 'Wv', 'Wo', 'Wg1', 'Wg2', 'norm_w')}
    del _L0_attn_all

    def _L0_xattn_setup():
        import jax, jax.numpy as jnp
        import numpy as np
        D_MODEL = 256
        N_HEADS = 16
        D_K = D_MODEL // N_HEADS
        B, S = (4, 512)

        def _xavier(key, out_dim, in_dim):
            limit = float(np.sqrt(6.0 / (in_dim + out_dim)))
            return jax.random.uniform(key, (out_dim, in_dim), jnp.float32, -limit, limit)
        key = jax.random.key(seed)
        ks = jax.random.split(key, 7)
        return {'query': jax.random.normal(ks[0], (B, S, D_MODEL), jnp.float32), 'key': jax.random.normal(ks[1], (B, S, D_MODEL), jnp.float32), 'value': jax.random.normal(ks[2], (B, S, D_MODEL), jnp.float32), 'W_q': _xavier(ks[3], D_MODEL, D_MODEL), 'b_q': jnp.zeros((D_MODEL,), jnp.float32), 'W_k': _xavier(ks[4], D_MODEL, D_MODEL), 'b_k': jnp.zeros((D_MODEL,), jnp.float32), 'W_v': _xavier(ks[5], D_MODEL, D_MODEL), 'b_v': jnp.zeros((D_MODEL,), jnp.float32), 'W_o': _xavier(ks[6], D_MODEL, D_MODEL), 'b_o': jnp.zeros((D_MODEL,), jnp.float32)}
    _L0_xattn_all = _L0_xattn_setup()
    _L0_xattn_in = {k: v for k, v in _L0_xattn_all.items() if k in ('W_q', 'b_q', 'W_k', 'b_k', 'W_v', 'b_v', 'W_o', 'b_o')}
    del _L0_xattn_all

    def _L0_ffn_setup():
        import jax, jax.numpy as jnp
        import numpy as np
        B, L, D = (4, 128, 256)
        E, TOP_K = (16, 4)
        F = 4 * D
        key = jax.random.key(seed)
        ks = jax.random.split(key, 6)
        scale = 0.02
        return {'x': jax.random.normal(ks[0], (B, L, D), jnp.float32), 'keys': jax.random.normal(ks[1], (E, D), jnp.float32), 'w1': jax.random.normal(ks[2], (E, F, D), jnp.float32) * scale, 'b1': jnp.zeros((E, F), jnp.float32), 'w2': jax.random.normal(ks[3], (E, D, F), jnp.float32) * scale, 'b2': jnp.zeros((E, D), jnp.float32), 'rw': jax.random.normal(ks[4], (E, D), jnp.float32) * scale, 'rb': jnp.zeros((E,), jnp.float32)}
    _L0_ffn_all = _L0_ffn_setup()
    _L0_ffn_in = {k: v for k, v in _L0_ffn_all.items() if k in ('keys', 'w1', 'b1', 'w2', 'b2', 'rw', 'rb')}
    del _L0_ffn_all
    return {'x': x, 'ctx_1024': ctx_1024, 'L0_attn_Wq': _L0_attn_in['Wq'], 'L0_attn_Wk': _L0_attn_in['Wk'], 'L0_attn_Wv': _L0_attn_in['Wv'], 'L0_attn_Wo': _L0_attn_in['Wo'], 'L0_attn_Wg1': _L0_attn_in['Wg1'], 'L0_attn_Wg2': _L0_attn_in['Wg2'], 'L0_attn_norm_w': _L0_attn_in['norm_w'], 'L0_xattn_W_q': _L0_xattn_in['W_q'], 'L0_xattn_b_q': _L0_xattn_in['b_q'], 'L0_xattn_W_k': _L0_xattn_in['W_k'], 'L0_xattn_b_k': _L0_xattn_in['b_k'], 'L0_xattn_W_v': _L0_xattn_in['W_v'], 'L0_xattn_b_v': _L0_xattn_in['b_v'], 'L0_xattn_W_o': _L0_xattn_in['W_o'], 'L0_xattn_b_o': _L0_xattn_in['b_o'], 'L0_ffn_keys': _L0_ffn_in['keys'], 'L0_ffn_w1': _L0_ffn_in['w1'], 'L0_ffn_b1': _L0_ffn_in['b1'], 'L0_ffn_w2': _L0_ffn_in['w2'], 'L0_ffn_b2': _L0_ffn_in['b2'], 'L0_ffn_rw': _L0_ffn_in['rw'], 'L0_ffn_rb': _L0_ffn_in['rb']}

def reference(x, ctx_1024, L0_attn_Wq, L0_attn_Wk, L0_attn_Wv, L0_attn_Wo, L0_attn_Wg1, L0_attn_Wg2, L0_attn_norm_w, L0_xattn_W_q, L0_xattn_b_q, L0_xattn_W_k, L0_xattn_b_k, L0_xattn_W_v, L0_xattn_b_v, L0_xattn_W_o, L0_xattn_b_o, L0_ffn_keys, L0_ffn_w1, L0_ffn_b1, L0_ffn_w2, L0_ffn_b2, L0_ffn_rw, L0_ffn_rb):
    import jax
    import jax.numpy as jnp

    def _L0_attn_ref(x, Wq, Wk, Wv, Wo, Wg1, Wg2, norm_w):
        import jax, jax.numpy as jnp
        import numpy as np
        B, N, D, H = (4, 512, 256, 16)
        HD = D // H
        CHUNK = 64
        BASE = 10000.0
        EPS = 1e-06

        def _lrpe(x, theta):
            c = jnp.cos(theta)[None, :, None, :]
            s = jnp.sin(theta)[None, :, None, :]
            return jnp.concatenate([x * c, x * s], axis=-1)

        def _chunk_gla(q, k, v, g):
            b, n, h, dk = q.shape
            dv = v.shape[-1]
            nc = n // CHUNK

            def to_chunks(t):
                return t.reshape(b, nc, CHUNK, t.shape[2], t.shape[3]).transpose(1, 0, 2, 3, 4)
            qc, kc, vc, gc = map(to_chunks, (q, k, v, g))
            mask = jnp.tril(jnp.ones((CHUNK, CHUNK), bool))

            def step(S, inp):
                qi, ki, vi, gi = inp
                G = jnp.cumsum(gi, axis=1)
                q_g = qi * jnp.exp(G)
                k_g = ki * jnp.exp(-G)
                o_inter = jnp.einsum('bchk,bhkv->bchv', q_g, S)
                A = jnp.einsum('bchk,bshk->bhcs', q_g, k_g)
                A = jnp.where(mask[None, None], A, 0.0)
                o_intra = jnp.einsum('bhcs,bshv->bchv', A, vi)
                G_last = G[:, -1:]
                S = S * jnp.exp(G_last[:, 0])[..., None] + jnp.einsum('bchk,bchv->bhkv', ki * jnp.exp(G_last - G), vi)
                return (S, o_inter + o_intra)
            S0 = jnp.zeros((b, h, dk, dv), q.dtype)
            _, o = jax.lax.scan(step, S0, (qc, kc, vc, gc))
            return o.transpose(1, 0, 2, 3, 4).reshape(b, n, h, dv)
        b, n, d = x.shape
        q = jax.nn.silu(x @ Wq).reshape(b, n, H, HD)
        k_raw = (x @ Wk).reshape(b, n, H, HD)
        v = (x @ Wv).reshape(b, n, H, HD)
        f = jnp.concatenate([jnp.zeros((b, 1, H, HD), jnp.float32), k_raw.astype(jnp.float32)], axis=1)
        z = jax.lax.cumlogsumexp(f, axis=1)
        log_f = z[:, :-1] - z[:, 1:]
        k = jnp.exp(k_raw - z[:, 1:])
        theta = jnp.arange(n, dtype=jnp.float32)[:, None] * (BASE ** (-2.0 * jnp.arange(HD, dtype=jnp.float32) / HD))[None]
        q = _lrpe(q, theta)
        k = _lrpe(k, theta)
        g = jnp.concatenate([log_f, log_f], axis=-1)
        o = _chunk_gla(q, k, v, g)
        o = o.reshape(b, n, d)
        gate = jax.nn.sigmoid(x @ Wg1 @ Wg2)
        o = o * gate
        o = o * jax.lax.rsqrt(jnp.mean(o * o, axis=-1, keepdims=True) + EPS) * norm_w
        return o @ Wo

    def _L0_xattn_ref(query, key, value, W_q, b_q, W_k, b_k, W_v, b_v, W_o, b_o):
        import jax, jax.numpy as jnp
        import numpy as np
        D_MODEL = 256
        N_HEADS = 16
        D_K = D_MODEL // N_HEADS
        B, S = (4, 512)

        def _xavier(key, out_dim, in_dim):
            limit = float(np.sqrt(6.0 / (in_dim + out_dim)))
            return jax.random.uniform(key, (out_dim, in_dim), jnp.float32, -limit, limit)
        b, sq, _ = query.shape
        sk = key.shape[1]
        Q = (query @ W_q.T + b_q).reshape(b, sq, N_HEADS, D_K).transpose(0, 2, 1, 3)
        K = (key @ W_k.T + b_k).reshape(b, sk, N_HEADS, D_K).transpose(0, 2, 1, 3)
        V = (value @ W_v.T + b_v).reshape(b, sk, N_HEADS, D_K).transpose(0, 2, 1, 3)
        scores = jnp.einsum('bhqd,bhkd->bhqk', Q, K) / jnp.sqrt(jnp.float32(D_K))
        attn = jax.nn.softmax(scores, axis=-1)
        out = jnp.einsum('bhqk,bhkd->bhqd', attn, V)
        out = out.transpose(0, 2, 1, 3).reshape(b, sq, D_MODEL)
        return out @ W_o.T + b_o

    def _L0_ffn_ref(x, keys, w1, b1, w2, b2, rw, rb):
        import jax, jax.numpy as jnp
        import numpy as np
        B, L, D = (4, 128, 256)
        E, TOP_K = (16, 4)
        F = 4 * D
        diff = x[:, :, None, :] - keys
        dist2 = jnp.sum(diff * diff, axis=-1)
        logits = -dist2 + jnp.einsum('bld,ed->ble', x, rw) + rb
        topv, topi = jax.lax.top_k(logits, TOP_K)
        w = jax.nn.softmax(topv, axis=-1)
        hidden = jax.nn.gelu(jnp.einsum('bld,efd->blef', x, w1) + b1, approximate=False)
        exp_out = jnp.einsum('blef,edf->bled', hidden, w2) + b2
        sel = jnp.take_along_axis(exp_out, topi[..., None], axis=2)
        fused = jnp.sum(w[..., None] * sel, axis=2)
        return fused
    x = x + _L0_attn_ref(_layernorm(x, axis=-1), L0_attn_Wq, L0_attn_Wk, L0_attn_Wv, L0_attn_Wo, L0_attn_Wg1, L0_attn_Wg2, L0_attn_norm_w)
    x = x + _L0_xattn_ref(_layernorm(x, axis=-1), ctx_1024, ctx_1024, L0_xattn_W_q, L0_xattn_b_q, L0_xattn_W_k, L0_xattn_b_k, L0_xattn_W_v, L0_xattn_b_v, L0_xattn_W_o, L0_xattn_b_o)
    x = x + _L0_ffn_ref(_layernorm(x, axis=-1), L0_ffn_keys, L0_ffn_w1, L0_ffn_b1, L0_ffn_w2, L0_ffn_b2, L0_ffn_rw, L0_ffn_rb)
    return x

_drawn_inputs = setup_inputs


def setup_inputs(seed=0):
    import zlib

    import numpy as np

    out = dict(_drawn_inputs(seed))
    spreads = {'L0_attn_norm_w': (1.0, 0.2),
     'L0_xattn_b_q': (0.0, 0.453),
     'L0_xattn_b_k': (0.0, 0.8),
     'L0_xattn_b_v': (0.0, 0.1),
     'L0_xattn_b_o': (0.0, 0.1),
     'L0_ffn_b1': (0.0, 0.273),
     'L0_ffn_b2': (0.0, 0.1),
     'L0_ffn_rb': (0.0, 0.8)}
    factors = {'L0_attn_Wg1': 8.0, 'L0_attn_Wg2': 8.0, 'L0_ffn_rw': 8.0}
    for name, (base, spread) in spreads.items():
        noise = np.random.default_rng([zlib.crc32(name.encode()), seed]).standard_normal(out[name].shape)
        drawn = base * np.exp(spread * noise) if base else spread * noise
        out[name] = jnp.asarray(drawn.astype(out[name].dtype))
    for name, factor in factors.items():
        out[name] = (out[name] * factor).astype(out[name].dtype)
    return out
```

```python
from contextlib import ExitStack

import numpy as np

import concourse.bass as bass
from concourse import mybir

ALU = mybir.AluOpType
ACT = mybir.ActivationFunctionType
F32 = mybir.dt.float32
BF16 = mybir.dt.bfloat16
U32 = mybir.dt.uint32
I32 = mybir.dt.int32
AX_X = mybir.AxisListType.X

P = 128
N = 2048
D = 256
KD = D // P
H = 16
HD = D // H
BLK = 512
NB = N // BLK
CH = 128
NC = BLK // CH
FT = 2 * D // P
HPT = H // FT
KEYS = 1601
KT = -(-KEYS // P)
KEYP = KT * P
KPART = KEYP // 4
EXP = 16
TOPK = 4
F = 1024
FF = F // P
TT = N // P
TILES = N * TOPK // P + EXP
NEG_LN_EPS = 1e-05
RMS_EPS = 1e-06


def constants():
    j = np.arange(HD, dtype=np.float32)
    freq = np.power(np.float32(10000.0), (np.float32(-2.0) * j / np.float32(HD)).astype(np.float32)).astype(np.float32)
    theta = (np.arange(N, dtype=np.float32)[:, None] * freq[None]).astype(np.float32)
    both = np.concatenate([np.cos(theta), np.sin(theta)], axis=1).T
    rope = np.ascontiguousarray(np.tile(both, (HPT, 1)).astype(np.float32))
    p = np.arange(P)
    const = np.zeros((P, 5, P), np.float32)
    const[:, 0, :] = 1.0 / D
    const[:, 1, :] = p[:, None] == p[None, :]
    const[:, 2, :] = p[:, None] <= p[None, :]
    const[:, 3, 0:64] = (p[:, None] // 32) == (np.arange(64)[None, :] // HD)
    const[:, 3, 64:64 + EXP] = np.arange(EXP)[None, :]
    const[:, 3, 96:96 + HPT] = (p[:, None] // 32) == np.arange(HPT)[None, :]
    const[:, 4, :] = (p[:, None] % 32 == HD) & (p[:, None] // 32 == p[None, :] // 32)
    return rope, const


def routing_constants():
    table = np.zeros((P, TT * EXP + TILES + TT + 1), np.float32)
    table[:, 0:TT * EXP] = np.tile(np.arange(TT) > 0, EXP)[None]
    table[:, TT * EXP:TT * EXP + TILES] = np.arange(TILES)[None]
    table[:, TT * EXP + TILES:] = np.arange(TT + 1)[None] * P + np.arange(P)[:, None]
    return table


def decoder_layer(nc, d):
    with ExitStack() as ctx:
        def sb(name, shape, dt=F32):
            return ctx.enter_context(nc.sbuf_tensor(name, shape, dt))

        def sem(name):
            return ctx.enter_context(nc.semaphore(name))

        psum = ctx.enter_context(nc.psum_tensor("psum", [P, 8, BLK], F32))

        x_t = sb("x_t", [P, KD, N])
        const = sb("const", [P, 5, P])
        rope = sb("rope", [P, N])
        mean_w, ident, causal = const[:, 0, :], const[:, 1, :], const[:, 2, :]
        own_state, expert_no, head_rows, den_sel = const[:, 3, 0:64], const[:, 3, 64:64 + EXP], const[:, 3, 96:96 + HPT], const[:, 4, :]

        eps_ln = sb("eps_ln", [P, 1])
        eps_rms = sb("eps_rms", [P, 1])
        ones = sb("ones", [P, BLK])

        a_wq = sb("a_wq", [P, KD, 2 * D])
        a_wk = sb("a_wk", [P, KD, 2 * D])
        a_wv = sb("a_wv", [P, KD, D])
        a_wo = sb("a_wo", [P, KD, D])
        a_wg1 = sb("a_wg1", [P, KD, H])
        a_wg2 = sb("a_wg2", [H, D])
        a_nw = sb("a_nw", [P, KD])
        cent = sb("cent", [P, KD, BLK])
        sq = sb("sq", [P, KD, BLK])
        lnv = sb("lnv", [P, BLK])
        rstd = sb("rstd", [P, BLK])
        xn = sb("xn", [P, KD, BLK])

        ld_x, ld_const, ld_rope, ld_aw, ld_xw, ld_ctx, out_done = (sem(s) for s in (
            "ld_x", "ld_const", "ld_rope", "ld_aw", "ld_xw", "ld_ctx", "out_done"))
        set_up = sem("set_up")

        with ExitStack() as st, nc.Block() as block:
            def sba(name, shape, dt=F32):
                return st.enter_context(nc.sbuf_tensor(name, shape, dt))

            def sema(name):
                return sem("a_" + name)

            ek = sba("ek", [P, FT, BLK])
            zz = sba("zz", [P, FT, BLK])
            kf = sba("kf", [P, FT, BLK])
            eq = sba("eq", [P, FT, BLK])
            qc = sba("qc", [P, FT, BLK])
            qx = sba("qx", [P, FT, NC, HPT, CH])
            v_pl = sba("v_pl", [P, NC, D + 64])
            v_hd = sba("v_hd", [P, NC, H, 32])
            g1 = sba("g1", [H, BLK])
            gs = sba("gs", [P, KD, BLK])
            kft = sba("kft", [P, 2, FT, P])
            am = sba("am", [P, 2, HPT, CH])
            st8 = sba("st8", [P, 2, FT, 64])
            st_d = sba("st_d", [P, FT, 64])
            og = sba("og", [P, KD, BLK])
            nbm = sba("nbm", [P, FT])
            ngm = sba("ngm", [P, FT])
            dmx = sba("dmx", [P, FT])
            alp = sba("alp", [P, FT])
            z0 = sba("z0", [P, FT])
            a_wos = sba("a_wos", [P, KD, D])

            s_wos = sema("wos")
            s_mean = sema("mean"); s_cent = sema("cent"); s_sq = sema("sq"); s_var = sema("var")
            s_lnv = sema("lnv"); s_rstd = sema("rstd"); s_xn = sema("xn")
            s_kps = sema("kps"); s_nbm = sema("nbm"); s_dmx = sema("dmx"); s_ngm = sema("ngm")
            s_ek = sema("ek"); s_alp = sema("alp"); s_z0 = sema("z0"); s_zz = sema("zz"); s_kf = sema("kf")
            s_qps = sema("qps"); s_eq = sema("eq"); s_qc = sema("qc"); s_rq = sema("rq"); s_rr = sema("rr")
            s_qf = sema("qf"); s_qx = sema("qx")
            s_vps = sema("vps"); s_vpl = sema("vpl"); s_vhd = sema("vhd")
            s_h1 = sema("h1"); s_g1 = sema("g1"); s_gps = sema("gps"); s_eg = sema("eg"); s_g2 = sema("g2"); s_gs = sema("gs")
            s_ktp = sema("ktp"); s_kft = sema("kft"); s_aps = sema("aps"); s_am = sema("am")
            s_avr = sema("avr"); s_out = sema("out"); s_std = sema("std"); s_st = sema("st"); s_og = sema("og")
            s_osq = sema("osq"); s_ss = sema("ss"); s_lno = sema("lno"); s_ro = sema("ro"); s_on = sema("on")
            s_wps = sema("wps"); s_x1 = sema("x1")

            @block.sync
            def _(sp):
                sp.dma_start(x_t[:, :, :], d["x_t"]).then_inc(ld_x, 16)
                sp.dma_start(const[:, :, :], d["const"]).then_inc(ld_const, 16)
                for dst, name in ((a_wk, "a_wk"), (a_wq, "a_wq"), (a_wv, "a_wv"), (a_wo, "a_wo"), (a_wg1, "a_wg1"),
                                  (a_wg2, "a_wg2"), (a_nw, "a_nw")):
                    sp.dma_start(dst[:], d[name]).then_inc(ld_aw, 16)
                sp.dma_start(rope[:, :], d["rope"]).then_inc(ld_rope, 16)

            @block.gpsimd
            def _(pool):
                pool.memset(v_hd[:], 0.0).then_inc(set_up, 1)
                pool.wait_ge(ld_const, 16)
                pool.wait_ge(ld_rope, 16)
                with pool.Fori(0, NB) as i:
                    for f in range(FT):
                        count = pool.to_reg(FT * i + f + 1)
                        pool.wait_ge(ld_rope, 16)
                        pool.wait_ge(s_ek, count)
                        if f == 0:
                            pool.wait_ge(s_avr, NC * FT * i)
                        pool.tensor_tensor(kf[:, f, :], ek[:, f, :], rope[:, bass.ds(i * BLK, BLK)], ALU.mult).then_inc(s_kf, 1)
                    for u in range(2):
                        count = pool.to_reg(2 * i + u + 1)
                        pool.wait_ge(ld_const, 16)
                        pool.wait_ge(s_vpl, count)
                        src = v_pl[:, 2 * u:2 * u + 2, 0:D].rearrange("p c (h e d) -> p c h e d", e=2, d=HD)
                        for e in range(2):
                            for c in range(2):
                                dst = v_hd[:, 2 * u + c].rearrange("p (h e) d -> p h e d", e=2)
                                pool.tensor_scalar(dst[:, :, e, HD * e:HD * e + HD], src[:, c, :, e, :], 1.0, 1.0,
                                                   ALU.mult, ALU.mult).then_inc(s_vhd, 1)
                    for f in range(FT):
                        count = pool.to_reg(FT * i + f + 1)
                        pool.wait_ge(ld_const, 16)
                        pool.wait_ge(s_qf, count)
                        for g in range(HPT):
                            pool.tensor_scalar(qx[:, f, :, g, :], qc[:, f, :].rearrange("p (c t) -> p c t", c=NC),
                                               head_rows[:, g:g + 1], 1.0, ALU.mult, ALU.mult).then_inc(s_qx, 1)

            @block.scalar
            def _(act):
                act.preload_act_table_set("natural_log_exp_and_others")
                act.wait_ge(set_up, 6)
                with act.Fori(0, NB) as i:
                    act.wait_ge(s_cent, i + 1)
                    act.activation(sq[:], cent[:], ACT.Square).then_inc(s_sq, 1)
                    act.wait_ge(s_var, i + 1)
                    act.activation(lnv[:], psum[:, 0, :], ACT.Ln, bias=eps_ln[:, 0:1]).then_inc(s_lnv, 1)
                    act.wait_ge(s_lnv, i + 1)
                    act.activation(rstd[:], lnv[:], ACT.Exp, scale=-0.5).then_inc(s_rstd, 1)
                    for f in range(FT):
                        act.wait_ge(s_ngm, FT * i + f + 1)
                        if f == 0:
                            act.wait_ge(s_zz, FT * i)
                            act.wait_ge(s_kf, FT * i)
                        act.activation(ek[:, f, :], psum[:, 1 + f % 2, :], ACT.Exp, bias=ngm[:, f:f + 1]).then_inc(s_ek, 1)
                    act.activation(alp[:], dmx[:], ACT.Exp).then_inc(s_alp, 1)
                    for f in range(FT):
                        act.wait_ge(s_qps, FT * i + f + 1)
                        act.activation(eq[:, f, :], psum[:, 1 + f % 2, :], ACT.Exp, scale=-1.0).then_inc(s_eq, 1)
                    for u in range(2):
                        act.wait_ge(s_vps, 2 * i + u + 1)
                        act.activation(v_pl[:, 2 * u:2 * u + 2, 0:D], psum[:, 1 + u, :].rearrange("p (c n) -> p c n", c=2),
                                       ACT.Copy).then_inc(s_vpl, 1)
                    act.wait_ge(s_h1, i + 1)
                    act.activation(g1[:], psum[0:H, 1, :], ACT.Copy).then_inc(s_g1, 1)
                    for t in range(KD):
                        act.wait_ge(s_gps, KD * i + t + 1)
                        if t == 0:
                            act.wait_ge(s_og, NC * i)
                        act.activation(gs[:, t, :], psum[:, 2 - t, :], ACT.Exp, scale=-1.0).then_inc(s_eg, 1)
                    for c in range(NC):
                        act.wait_ge(s_ktp, NC * i + c + 1)
                        if c < 2:
                            act.wait_ge(s_out, NC * i)
                        else:
                            act.wait_ge(s_out, NC * i + c - 1)
                        act.activation(kft[:, c % 2], psum[:, 7, :].rearrange("p (f t) -> p f t", f=FT),
                                       ACT.Copy).then_inc(s_kft, 1)
                    act.wait_ge(s_og, NC * i + NC)
                    act.activation(sq[:], og[:], ACT.Square).then_inc(s_osq, 1)
                    act.wait_ge(s_ss, i + 1)
                    act.activation(lnv[:], psum[:, 0, :], ACT.Ln, bias=eps_rms[:, 0:1]).then_inc(s_lno, 1)
                    act.wait_ge(s_lno, i + 1)
                    act.activation(rstd[:], lnv[:], ACT.Exp, scale=-0.5).then_inc(s_ro, 1)

            @block.vector
            def _(dve):
                dve.memset(eps_ln[:], NEG_LN_EPS).then_inc(set_up, 1)
                dve.memset(eps_rms[:], RMS_EPS).then_inc(set_up, 1)
                dve.memset(ones[:], 1.0).then_inc(set_up, 1)
                dve.memset(ngm[:], 0.0).then_inc(set_up, 1)
                dve.memset(zz[:, :, BLK - 1:BLK], 1.0).then_inc(set_up, 1)
                dve.wait_ge(set_up, 6)
                dve.memset(st8[:], 0.0).then_inc(s_wos, 1)
                dve.memset(v_pl[:, :, D:D + 64], 0.0).then_inc(s_wos, 1)
                dve.wait_ge(ld_aw, 16 * 7)
                for k in range(KD):
                    dve.tensor_scalar(a_wos[:, k, :], a_wo[:, k, :], a_nw[:, k:k + 1], None, ALU.mult).then_inc(s_wos, 1)
                dve.wait_ge(s_wos, 2 + KD)
                dve.wait_ge(ld_rope, 16)
                dve.wait_ge(ld_x, 16)
                dve.wait_ge(ld_const, 16)
                with dve.Fori(0, NB) as i:
                    now = bass.ds(i * BLK, BLK)
                    dve.wait_ge(s_mean, i + 1)
                    dve.tensor_tensor(cent[:], x_t[:, :, now], psum[:, 0:1, :].to_broadcast([P, KD, BLK]),
                                      ALU.subtract).then_inc(s_cent, 1)
                    dve.wait_ge(s_rstd, i + 1)
                    dve.wait_ge(s_cent, i + 1)
                    dve.tensor_tensor(xn[:], cent[:], rstd[:].unsqueeze(1).to_broadcast([P, KD, BLK]), ALU.mult).then_inc(s_xn, 1)
                    for f in range(FT):
                        n = FT * i + f + 1
                        dve.wait_ge(s_kps, n)
                        dve.tensor_reduce(nbm[:, f:f + 1], psum[:, 1 + f % 2, :], AX_X, ALU.max, negate=True).then_inc(s_nbm, 1)
                        dve.wait_ge(s_nbm, n)
                        dve.tensor_scalar(dmx[:, f:f + 1], nbm[:, f:f + 1], ngm[:, f:f + 1], 0.0, ALU.subtract,
                                          ALU.min).then_inc(s_dmx, 1)
                        dve.wait_ge(s_dmx, n)
                        dve.tensor_tensor(ngm[:, f:f + 1], nbm[:, f:f + 1], ngm[:, f:f + 1], ALU.min).then_inc(s_ngm, 1)
                    for f in range(FT):
                        dve.wait_ge(s_eq, FT * i + f + 1)
                        if f == 0:
                            dve.wait_ge(s_avr, NC * FT * i)
                            dve.wait_ge(s_qx, FT * HPT * i)
                        dve.tensor_tensor(qc[:, f, :], psum[:, 1 + f % 2, :], rope[:, now], ALU.mult).then_inc(s_qc, 1)
                    dve.wait_ge(s_alp, i + 1)
                    dve.wait_ge(s_zz, FT * i)
                    dve.tensor_tensor(z0[:], zz[:, :, BLK - 1], alp[:], ALU.mult).then_inc(s_z0, 1)
                    dve.wait_ge(s_z0, i + 1)
                    for f in range(FT):
                        dve.wait_ge(s_ek, FT * i + f + 1)
                        dve.tensor_tensor_scan(zz[:, f, :], ones[:], ek[:, f, :], z0[:, f:f + 1], ALU.mult, ALU.add).then_inc(s_zz, 1)
                    dve.tensor_tensor(st8[:, 0], st8[:, 0], alp[:].unsqueeze(2).to_broadcast([P, FT, 64]), ALU.mult).then_inc(s_st, 1)
                    for f in range(FT):
                        n = FT * i + f + 1
                        dve.wait_ge(s_eq, n)
                        dve.wait_ge(s_zz, n)
                        dve.scalar_tensor_tensor(out=eq[:, f, :], in0=eq[:, f, :], scalar=1.0, in1=zz[:, f, :],
                                                 op0=ALU.add, op1=ALU.mult).then_inc(s_rq, 1)
                        dve.wait_ge(s_rq, n)
                        dve.reciprocal(eq[:, f, :], eq[:, f, :]).then_inc(s_rr, 1)
                        dve.wait_ge(s_rr, n)
                        dve.wait_ge(s_qc, n)
                        dve.tensor_tensor(qc[:, f, :], qc[:, f, :], eq[:, f, :], ALU.mult).then_inc(s_qf, 1)
                    dve.wait_ge(s_eg, KD * i + KD)
                    dve.tensor_scalar(gs[:], gs[:], 1.0, None, ALU.add).then_inc(s_g2, 1)
                    dve.wait_ge(s_g2, i + 1)
                    dve.reciprocal(gs[:], gs[:]).then_inc(s_gs, 1)
                    for u in range(NC * FT):
                        c, f = divmod(u, FT)
                        dve.wait_ge(s_aps, NC * FT * i + u + 1)
                        dve.wait_ge(s_avr, NC * FT * i + max(u - 1, 0))
                        dve.tensor_tensor(am[:, u % 2], psum[:, 3 + u % 2, :].rearrange("p (g t) -> p g t", g=HPT),
                                          causal.unsqueeze(1).to_broadcast([P, HPT, CH]), ALU.mult).then_inc(s_am, 1)
                        if f == FT - 1:
                            n = NC * i + c + 1
                            dve.wait_ge(s_out, n)
                            dve.tensor_tensor(st_d[:], psum[:, 0, :].rearrange("p (f n) -> p f n", f=FT)[:, :, 0:64],
                                              own_state.unsqueeze(1).to_broadcast([P, FT, 64]), ALU.mult).then_inc(s_std, 1)
                            dve.wait_ge(s_std, n)
                            dve.wait_ge(s_st, (NC + 1) * i + c + 1)
                            dve.tensor_tensor(st8[:, (c + 1) % 2], st8[:, c % 2], st_d[:], ALU.add).then_inc(s_st, 1)
                            dve.wait_ge(s_avr, NC * FT * i + FT * (c + 1))
                            dve.wait_ge(s_gs, i + 1)
                            if c == 0:
                                dve.wait_ge(s_osq, i)
                            dve.tensor_tensor(og[:, :, c * CH:(c + 1) * CH],
                                              psum[:, 5 + c % 2, 0:KD * CH].rearrange("p (k t) -> p k t", k=KD),
                                              gs[:, :, c * CH:(c + 1) * CH], ALU.mult).then_inc(s_og, 1)
                    dve.wait_ge(s_ro, i + 1)
                    dve.wait_ge(s_og, NC * i + NC)
                    dve.tensor_tensor(og[:], og[:], rstd[:].unsqueeze(1).to_broadcast([P, KD, BLK]), ALU.mult).then_inc(s_on, 1)
                    for t in range(KD):
                        dve.wait_ge(s_wps, KD * i + t + 1)
                        dve.tensor_tensor(x_t[:, t, now], psum[:, 2 - t, :], x_t[:, t, now], ALU.add).then_inc(s_x1, 1)

            @block.tensor
            def _(pe):
                pe.wait_ge(ld_const, 16)
                pe.wait_ge(ld_x, 16)
                pe.wait_ge(s_wos, 2 + KD)
                pe.wait_ge(set_up, 6)
                with pe.Fori(0, NB) as i:
                    now = bass.ds(i * BLK, BLK)
                    pe.wait_ge(s_x1, KD * i)
                    for k in range(KD):
                        mm = pe.matmul(psum[:, 0, :], mean_w, x_t[:, k, now], start=k == 0, stop=k == KD - 1)
                    mm.then_inc(s_mean, 1)
                    pe.wait_ge(s_sq, i + 1)
                    for k in range(KD):
                        mm = pe.matmul(psum[:, 0, :], mean_w, sq[:, k, :], start=k == 0, stop=k == KD - 1)
                    mm.then_inc(s_var, 1)
                    pe.wait_ge(s_xn, i + 1)
                    for f in range(FT):
                        if f >= 2:
                            pe.wait_ge(s_ek, FT * i + f - 1)
                        for k in range(KD):
                            mm = pe.matmul(psum[:, 1 + f % 2, :], a_wk[:, k, f * P:(f + 1) * P], xn[:, k, :], start=k == 0, stop=k == KD - 1)
                        mm.then_inc(s_kps, 1)
                    for f in range(FT):
                        if f < 2:
                            pe.wait_ge(s_ek, FT * i + f + 3)
                        else:
                            pe.wait_ge(s_eq, FT * i + f - 1)
                            pe.wait_ge(s_qc, FT * i + f - 1)
                        for k in range(KD):
                            mm = pe.matmul(psum[:, 1 + f % 2, :], a_wq[:, k, f * P:(f + 1) * P], xn[:, k, :], start=k == 0, stop=k == KD - 1)
                        mm.then_inc(s_qps, 1)
                    for u in range(2):
                        pe.wait_ge(s_eq, FT * i + 3 + u)
                        pe.wait_ge(s_qc, FT * i + 3 + u)
                        for c in range(2):
                            for k in range(KD):
                                mm = pe.matmul(psum[:, 1 + u, c * D:(c + 1) * D], xn[:, k, (2 * u + c) * CH:(2 * u + c + 1) * CH],
                                               a_wv[:, k, :], start=k == 0, stop=k == KD - 1)
                        mm.then_inc(s_vps, 1)
                    pe.wait_ge(s_vpl, 2 * i + 1)
                    for k in range(KD):
                        mm = pe.matmul(psum[0:H, 1, :], a_wg1[:, k, :], xn[:, k, :], start=k == 0, stop=k == KD - 1)
                    mm.then_inc(s_h1, 1)
                    pe.wait_ge(s_vpl, 2 * i + 2)
                    pe.wait_ge(s_g1, i + 1)
                    for t in range(KD):
                        pe.matmul(psum[:, 2 - t, :], a_wg2[:, t * P:(t + 1) * P], g1[:], start=True, stop=True).then_inc(s_gps, 1)

                    def values(u):
                        c, f = divmod(u, FT)
                        o = 5 + c % 2
                        if f == 0:
                            pe.wait_ge(s_st, (NC + 1) * i + c + 1)
                            if c >= 2:
                                pe.wait_ge(s_og, NC * i + c - 1)
                            else:
                                pe.wait_ge(s_og, NC * i)
                            pe.wait_ge(s_qf, FT * i + FT)
                            for ff in range(FT):
                                at = 64 * (ff % 2)
                                pe.matmul(psum[at:at + 64, o, (ff // 2) * CH:(ff // 2 + 1) * CH], st8[:, c % 2, ff, :],
                                          qc[:, ff, c * CH:(c + 1) * CH], start=ff < 2, stop=False, skip_group_check=True)
                            pe.wait_ge(s_vhd, 8 * i + 4 * (c // 2) + 4)
                        pe.wait_ge(s_am, NC * FT * i + u + 1)
                        for g in range(HPT):
                            h = HPT * f + g
                            at = 32 * (h // 2 % 4)
                            mm = pe.matmul(psum[at:at + 32, o, (h // 8) * CH:(h // 8 + 1) * CH], v_hd[:, c, h, :], am[:, u % 2, g, :],
                                           start=False, stop=f == FT - 1, skip_group_check=True)
                        mm.then_inc(s_avr, 1)

                    for u in range(NC * FT):
                        c, f = divmod(u, FT)
                        if f == 0:
                            pe.wait_ge(s_kf, FT * i + FT)
                            pe.wait_ge(s_kft, NC * i + c)
                            for ff in range(FT):
                                mm = pe.transpose(psum[:, 7, ff * P:(ff + 1) * P], kf[:, ff, c * CH:(c + 1) * CH], ident)
                            mm.then_inc(s_ktp, 1)
                        if c == 0:
                            pe.wait_ge(s_qx, FT * HPT * i + HPT * (f + 1))
                        pe.wait_ge(s_am, NC * FT * i + max(u - 1, 0))
                        pe.matmul(psum[:, 3 + u % 2, :], kf[:, f, c * CH:(c + 1) * CH],
                                  qx[:, f, c].rearrange("p g t -> p (g t)"), start=True, stop=True).then_inc(s_aps, 1)
                        if u > 0:
                            values(u - 1)
                        if f == 2:
                            pe.wait_ge(s_kft, NC * i + c + 1)
                            pe.wait_ge(s_st, (NC + 1) * i + c + 1)
                            for ff in range(FT):
                                mm = pe.matmul(psum[:, 0, ff * P:(ff + 1) * P], kft[:, c % 2, ff, :], v_pl[:, c, 64 * ff:64 * ff + P],
                                               start=True, stop=True)
                            mm.then_inc(s_out, 1)
                    values(NC * FT - 1)
                    pe.wait_ge(s_osq, i + 1)
                    for k in range(KD):
                        mm = pe.matmul(psum[:, 0, :], mean_w, sq[:, k, :], start=k == 0, stop=k == KD - 1)
                    mm.then_inc(s_ss, 1)
                    pe.wait_ge(s_on, i + 1)
                    for t in range(KD):
                        for k in range(KD):
                            mm = pe.matmul(psum[:, 2 - t, :], a_wos[:, k, t * P:(t + 1) * P], og[:, k, :], start=k == 0, stop=k == KD - 1)
                        mm.then_inc(s_wps, 1)


        k_op = sb("k_op", [P, H, KEYS], BF16)
        v_pad = sb("v_pad", [P, KT, H, 32])
        x_wo = sb("x_wo", [P, H // 4, D])
        x_wq = sb("x_wq", [P, KD, D])
        x_bq = sb("x_bq", [P, KD])
        x_bo = sb("x_bo", [P, KD])
        k_dram = nc.dram_tensor("k_parts", (3, D, KEYP), BF16, kind="Internal").ap()
        q_dram = nc.dram_tensor("q_parts", (3, D, N), BF16, kind="Internal").ap()
        m_dram = nc.dram_tensor("shifts", (NB, H, BLK), BF16, kind="Internal").ap()
        Q_PART, K_PART = (0, 0, 1, 1, 0, 2), (0, 1, 0, 1, 2, 0)
        NPR = len(Q_PART)
        SHIFT = NPR * HD
        assert SHIFT == 96

        with ExitStack() as st, nc.Block() as block:
            ctx_t = st.enter_context(nc.sbuf_tensor("ctx_t", [P, KD, KEYP], F32))
            x_wk = st.enter_context(nc.sbuf_tensor("x_wk", [P, KD, D], F32))
            x_wv = st.enter_context(nc.sbuf_tensor("x_wv", [P, KD, D], F32))
            x_bk = st.enter_context(nc.sbuf_tensor("x_bk", [P, KD], F32))
            x_bv = st.enter_context(nc.sbuf_tensor("x_bv", [P, D], F32))
            kk = st.enter_context(nc.sbuf_tensor("kk", [P, KD, KPART], F32))
            kp = st.enter_context(nc.sbuf_tensor("kp", [P, 3, KD, KPART], BF16))
            kps, kk_in, kp0, kr0, kp1, kp2, k_out, k_row, vps, v_in, v_set = (sem("k_" + n) for n in (
                "kps", "kk_in", "kp0", "kr0", "kp1", "kp2", "out", "row", "vps", "v_in", "v_set"))

            @block.sync
            def _(sp):
                for dst, name in ((ctx_t, "ctx_t"), (x_wk, "x_wk"), (x_bk, "x_bk"), (x_wv, "x_wv")):
                    sp.dma_start(dst[:], d[name]).then_inc(ld_ctx, 16)
                sp.dma_start(x_bv[:], d["x_bv"].partition_broadcast(P)).then_inc(ld_ctx, 16)
                for dst, name in ((x_wo, "x_wo"), (x_wq, "x_wq"), (x_bq, "x_bq"), (x_bo, "x_bo")):
                    sp.dma_start(dst[:], d[name]).then_inc(ld_xw, 16)
                with sp.Fori(0, 4) as i:
                    sp.wait_ge(kp2, i + 1)
                    sp.wait_ge(kp1, i + 1)
                    for n in range(3):
                        sp.dma_start(k_dram[n].rearrange("(t p) n -> p t n", p=P)[:, :, bass.ds(i * KPART, KPART)],
                                     kp[:, n]).then_inc(k_out, 16)
                sp.wait_ge(k_out, 16 * 12)
                for r, n in enumerate(K_PART):
                    sp.dma_start(k_op[r * HD:(r + 1) * HD], k_dram[n].rearrange("(h j) n -> j h n", j=HD)[:, :, 0:KEYS]).then_inc(k_row, 16)

            @block.gpsimd
            def _(pool):
                pool.memset(k_op[96:97], 1.0).then_inc(v_set, 1)
                pool.wait_ge(v_set, 1)
                pool.memset(v_pad[:], 0.0).then_inc(v_set, 1)
                pool.wait_ge(v_set, 2)
                pool.memset(v_pad[:, :, :, HD:HD + 1], 1.0).then_inc(v_set, 1)

            @block.scalar
            def _(act):
                act.wait_ge(ld_ctx, 16 * 5)
                with act.Fori(0, 4) as i:
                    for t in range(KD):
                        act.wait_ge(kps, KD * i + t + 1)
                        if t == 0:
                            act.wait_ge(kp2, i)
                        act.activation(kk[:, t, :], psum[:, t, 0:KPART], ACT.Identity, bias=x_bk[:, t:t + 1]).then_inc(kk_in, 1)

            @block.vector
            def _(dve):
                dve.wait_ge(ld_ctx, 16 * 5)
                dve.wait_ge(v_set, 3)
                for kt in range(KT):
                    rows = min(P, KEYS - kt * P)
                    dve.wait_ge(vps, kt + 1)
                    dve.tensor_tensor(v_pad[0:rows, kt, :, 0:HD], psum[0:rows, 4 + kt % 2, 0:D].rearrange("p (h d) -> p h d", h=H),
                                      x_bv[0:rows].rearrange("p (h d) -> p h d", h=H), ALU.add).then_inc(v_in, 1)
                with dve.Fori(0, 4) as i:
                    dve.wait_ge(kk_in, KD * i + KD)
                    dve.wait_ge(k_out, 48 * i)
                    dve.tensor_copy(kp[:, 0], kk[:]).then_inc(kp0, 1)
                    dve.wait_ge(kp0, i + 1)
                    dve.tensor_tensor(kk[:], kk[:], kp[:, 0], ALU.subtract).then_inc(kr0, 1)
                    dve.wait_ge(kr0, i + 1)
                    dve.tensor_copy(kp[:, 1], kk[:]).then_inc(kp1, 1)
                    dve.wait_ge(kp1, i + 1)
                    dve.tensor_tensor(kp[:, 2], kk[:], kp[:, 1], ALU.subtract).then_inc(kp2, 1)

            @block.tensor
            def _(pe):
                pe.wait_ge(ld_ctx, 16 * 5)
                for kt in range(KT):
                    rows = min(P, KEYS - kt * P)
                    if kt >= 2:
                        pe.wait_ge(v_in, kt - 1)
                    for k in range(KD):
                        mm = pe.matmul(psum[0:rows, 4 + kt % 2, 0:D], ctx_t[:, k, kt * P:kt * P + rows], x_wv[:, k, :],
                                       start=k == 0, stop=k == KD - 1)
                    mm.then_inc(vps, 1)
                with pe.Fori(0, 4) as i:
                    for t in range(KD):
                        pe.wait_ge(kk_in, KD * i)
                        for k in range(KD):
                            mm = pe.matmul(psum[:, t, 0:KPART], x_wk[:, k, t * P:(t + 1) * P], ctx_t[:, k, bass.ds(i * KPART, KPART)],
                                           start=k == 0, stop=k == KD - 1)
                        mm.then_inc(kps, 1)

        with ExitStack() as st, nc.Block() as block:
            def sbb(name, shape, dt=F32):
                return st.enter_context(nc.sbuf_tensor(name, shape, dt))

            qq = sbb("qq", [P, KD, BLK])
            qp = sbb("qp", [P, 3, KD, BLK], BF16)
            q_op = sbb("q_op", [P, H, BLK], BF16)
            nmx = sbb("nmx", [P, NC, H])
            nmt = sbb("nmt", [H, BLK], BF16)
            pr = sbb("pr", [P, 3, 4, BLK])
            osb = sbb("osb", [P, 2, BLK])
            rden = sbb("rden", [P, BLK])
            on = sbb("on", [P, 4, BLK])
            GR = KT * 4
            s_mean, s_cent, s_sq, s_var, s_lnv, s_rstd, s_xn = (sem("b_" + n) for n in ("mean", "cent", "sq", "var", "lnv", "rstd", "xn"))
            s_qps, s_qq, s_qp0, s_qr0, s_qp1, s_qp2, s_qout, s_qop = (sem("b_" + n) for n in ("qps", "qq", "qp0", "qr0", "qp1", "qp2", "qout", "qop"))
            s_ms, s_mx, s_mt, s_mn, s_mout, s_mrow = (sem("b_" + n) for n in ("ms", "mx", "mt", "mn", "mout", "mrow"))
            s_sc, s_ex, s_pv, s_os, s_dn, s_rd, s_on, s_wps, s_x2 = (sem("b_" + n) for n in ("sc", "ex", "pv", "os", "dn", "rd", "on", "wps", "x2"))

            @block.sync
            def _(sp):
                with sp.Fori(0, NB) as i:
                    now = bass.ds(i * BLK, BLK)
                    sp.wait_ge(s_qp1, i + 1)
                    sp.wait_ge(s_qp2, i + 1)
                    for n in range(3):
                        sp.dma_start(q_dram[n].rearrange("(t p) n -> p t n", p=P)[:, :, now], qp[:, n]).then_inc(s_qout, 16)
                    scored = sp.to_reg(2 * GR * i)
                    sp.wait_ge(s_qout, 48 * i + 48)
                    sp.wait_ge(s_sc, scored)
                    for r, n in enumerate(Q_PART):
                        sp.dma_start(q_op[r * HD:(r + 1) * HD], q_dram[n].rearrange("(h j) n -> j h n", j=HD)[:, :, now]).then_inc(s_qop, 16)
                    sp.wait_ge(s_mn, i + 1)
                    sp.dma_start(m_dram[bass.ds(i, 1)].rearrange("o h n -> (o h) n"), nmt[:]).then_inc(s_mout, 16)
                    sp.wait_ge(s_mout, 16 * i + 16)
                    sp.dma_start(q_op[SHIFT:SHIFT + 1], m_dram[bass.ds(i, 1)]).then_inc(s_mrow, 16)

            @block.scalar
            def _(act):
                with act.Fori(0, NB) as i:
                    act.wait_ge(s_cent, i + 1)
                    act.activation(sq[:], cent[:], ACT.Square).then_inc(s_sq, 1)
                    act.wait_ge(s_var, i + 1)
                    act.activation(lnv[:], psum[:, 0, :], ACT.Ln, bias=eps_ln[:, 0:1]).then_inc(s_lnv, 1)
                    act.wait_ge(s_lnv, i + 1)
                    act.activation(rstd[:], lnv[:], ACT.Exp, scale=-0.5).then_inc(s_rstd, 1)
                    act.wait_ge(s_mt, i + 1)
                    act.activation(nmt[:], psum[0:H, 7, :], ACT.Copy).then_inc(s_mn, 1)
                    for n in range(GR):
                        for e in range(2):
                            p = 2 * n + e
                            act.wait_ge(s_sc, 2 * GR * i + p + 1)
                            if n >= 3:
                                act.wait_ge(s_pv, GR * i + n - 2)
                            else:
                                act.wait_ge(s_pv, GR * i)
                            rows = min(P, KEYS - (n % KT) * P)
                            b = 2 * (p % 3)
                            act.activation(pr[0:rows, n % 3, 2 * e:2 * e + 2, :], psum[0:rows, b:b + 2, :], ACT.Exp).then_inc(s_ex, 1)

            @block.vector
            def _(dve):
                dve.wait_ge(ld_xw, 16 * 4)
                with dve.Fori(0, NB) as i:
                    now = bass.ds(i * BLK, BLK)
                    dve.wait_ge(s_mean, i + 1)
                    dve.tensor_tensor(cent[:], x_t[:, :, now], psum[:, 0:1, :].to_broadcast([P, KD, BLK]), ALU.subtract).then_inc(s_cent, 1)
                    dve.wait_ge(s_rstd, i + 1)
                    dve.wait_ge(s_cent, i + 1)
                    dve.tensor_tensor(xn[:], cent[:], rstd[:].unsqueeze(1).to_broadcast([P, KD, BLK]), ALU.mult).then_inc(s_xn, 1)
                    for t in range(KD):
                        dve.wait_ge(s_qps, KD * i + t + 1)
                        dve.tensor_scalar(qq[:, t, :], psum[:, 1 + t, :], x_bq[:, t:t + 1], float(HD) ** -0.5, ALU.add,
                                          ALU.mult).then_inc(s_qq, 1)
                    dve.wait_ge(s_qq, KD * i + KD)
                    dve.wait_ge(s_qout, 48 * i)
                    dve.tensor_copy(qp[:, 0], qq[:]).then_inc(s_qp0, 1)
                    dve.wait_ge(s_qp0, i + 1)
                    dve.tensor_tensor(qq[:], qq[:], qp[:, 0], ALU.subtract).then_inc(s_qr0, 1)
                    dve.wait_ge(s_qr0, i + 1)
                    dve.tensor_copy(qp[:, 1], qq[:]).then_inc(s_qp1, 1)
                    dve.wait_ge(s_qp1, i + 1)
                    dve.tensor_tensor(qp[:, 2], qq[:], qp[:, 1], ALU.subtract).then_inc(s_qp2, 1)
                    with dve.Fori(0, H // 2) as h2:
                        for w in range(2 * NC):
                            e, c = divmod(w, NC)
                            dve.wait_ge(s_ms, H * NC * i + 2 * NC * h2 + w + 1)
                            dve.tensor_reduce(nmx[:, c, bass.ds(2 * h2 + e, 1)],
                                              psum[:, 4 * (w % 2):4 * (w % 2) + 4, :].rearrange("p b n -> p (b n)")[:, 0:KEYS],
                                              AX_X, ALU.max, negate=True).then_inc(s_mx, 1)
                    for g in range(4):
                        dve.wait_ge(s_pv, GR * i + KT * (g + 1))
                        dve.tensor_copy(osb[:, g % 2, :], psum[:, 6, :]).then_inc(s_os, 1)
                        dve.wait_ge(s_dn, 4 * i + g + 1)
                        dve.reciprocal(rden[:], psum[:, 7, :]).then_inc(s_rd, 1)
                        dve.wait_ge(s_rd, 4 * i + g + 1)
                        dve.wait_ge(s_os, 4 * i + g + 1)
                        dve.tensor_tensor(on[:, g, :], osb[:, g % 2, :], rden[:], ALU.mult).then_inc(s_on, 1)
                    for t in range(KD):
                        dve.wait_ge(s_wps, KD * i + t + 1)
                        dve.scalar_tensor_tensor(out=x_t[:, t, now], in0=psum[:, 1 + t, :], scalar=x_bo[:, t:t + 1],
                                                 in1=x_t[:, t, now], op0=ALU.add, op1=ALU.add).then_inc(s_x2, 1)

            def denominators(pe, i, g):
                pe.wait_ge(s_os, 4 * i + g + 1)
                pe.wait_ge(s_rd, 4 * i + g)
                pe.matmul(psum[:, 7, :], den_sel, osb[:, g % 2, :], start=True, stop=True).then_inc(s_dn, 1)

            @block.tensor
            def _(pe):
                pe.wait_ge(k_row, 16 * NPR)
                pe.wait_ge(ld_xw, 16 * 4)
                with pe.Fori(0, NB) as i:
                    now = bass.ds(i * BLK, BLK)
                    pe.wait_ge(s_x2, KD * i)
                    for k in range(KD):
                        mm = pe.matmul(psum[:, 0, :], mean_w, x_t[:, k, now], start=k == 0, stop=k == KD - 1)
                    mm.then_inc(s_mean, 1)
                    pe.wait_ge(s_sq, i + 1)
                    for k in range(KD):
                        mm = pe.matmul(psum[:, 0, :], mean_w, sq[:, k, :], start=k == 0, stop=k == KD - 1)
                    mm.then_inc(s_var, 1)
                    pe.wait_ge(s_xn, i + 1)
                    for t in range(KD):
                        for k in range(KD):
                            mm = pe.matmul(psum[:, 1 + t, :], x_wq[:, k, t * P:(t + 1) * P], xn[:, k, :], start=k == 0, stop=k == KD - 1)
                        mm.then_inc(s_qps, 1)
                    pe.wait_ge(s_qq, KD * i + KD)
                    regrouped = pe.to_reg(16 * NPR * (i + 1))
                    pe.wait_ge(ld_const, 16)
                    pe.wait_ge(s_qop, regrouped)
                    with pe.Fori(0, H // 2) as h2:
                        for w in range(2 * NC):
                            e, c = divmod(w, NC)
                            pe.wait_ge(s_mx, H * NC * i + 2 * NC * h2 + max(w - 1, 0))
                            h = bass.ds(2 * h2 + e, 1)
                            for b in range(4):
                                cols = min(BLK, KEYS - b * BLK)
                                mm = pe.matmul(psum[:, 4 * (w % 2) + b, 0:cols], q_op[0:SHIFT, h, c * CH:(c + 1) * CH].rearrange("p o n -> p (o n)"),
                                               k_op[0:SHIFT, h, b * BLK:b * BLK + cols].rearrange("p o n -> p (o n)"), start=True, stop=True)
                            mm.then_inc(s_ms, 1)
                    pe.wait_ge(s_mx, H * NC * (i + 1))
                    for c in range(NC):
                        mm = pe.transpose(psum[0:H, 7, c * CH:(c + 1) * CH], nmx[:, c, :], ident)
                    mm.then_inc(s_mt, 1)
                    pe.wait_ge(s_mrow, 16 * i + 16)

                    def weighted(n):
                        g, kt = divmod(n, KT)
                        rows = min(P, KEYS - kt * P)
                        pe.wait_ge(s_ex, 2 * GR * i + 2 * n + 2)
                        if kt == 0:
                            pe.wait_ge(s_os, 4 * i + g)
                        for j in range(4):
                            mm = pe.matmul(psum[32 * j:32 * j + 32, 6, :], v_pad[0:rows, kt, 4 * g + j, :], pr[0:rows, n % 3, j, :],
                                           start=kt == 0, stop=kt == KT - 1)
                        mm.then_inc(s_pv, 1)

                    for n in range(GR):
                        g, kt = divmod(n, KT)
                        rows = min(P, KEYS - kt * P)
                        for e in range(2):
                            p = 2 * n + e
                            pe.wait_ge(s_ex, 2 * GR * i + max(p - 2, 0))
                            for j in range(2):
                                h = 4 * g + 2 * e + j
                                mm = pe.matmul(psum[0:rows, 2 * (p % 3) + j, :], k_op[0:SHIFT + 1, h, kt * P:kt * P + rows],
                                               q_op[0:SHIFT + 1, h, :], start=True, stop=True)
                            mm.then_inc(s_sc, 1)
                        if n > 0:
                            weighted(n - 1)
                        if kt == 3 and g > 0:
                            denominators(pe, i, g - 1)
                    weighted(GR - 1)
                    denominators(pe, i, 3)
                    pe.wait_ge(s_on, 4 * i + 4)
                    for t in range(KD):
                        for g in range(4):
                            mm = pe.matmul(psum[:, 1 + t, :], x_wo[:, g, t * P:(t + 1) * P], on[:, g, :], start=g == 0, stop=g == 3)
                        mm.then_inc(s_wps, 1)

        slot_rows = nc.dram_tensor("slot_rows", (P * TILES, 2), F32, kind="Internal").ap()
        xn_rows = nc.dram_tensor("xn_rows", (N + P, D), F32, kind="Internal").ap()
        y_rows = nc.dram_tensor("y_rows", (N + P, D), F32, kind="Internal").ap()
        e_tile = sb("e_tile", [P, TILES])
        e_int = sb("e_int", [P, TILES], I32)
        with ExitStack() as st, nc.Block() as block:
            def sbr(name, shape, dt=F32):
                return st.enter_context(nc.sbuf_tensor(name, shape, dt))

            def semr(name):
                return sem("r_" + name)

            rconst = sbr("rconst", [P, TT * EXP + TILES + TT + 1])
            seg = rconst[:, 0:TT * EXP]
            tile_no = rconst[:, TT * EXP:TT * EXP + TILES]
            tok_no = rconst[:, TT * EXP + TILES:]
            keys = sbr("keys", [P, KD, EXP])
            rw = sbr("rw", [P, KD, EXP])
            rt = sbr("rt", [P, KD, EXP])
            ksq = sbr("ksq", [P, KD, EXP])
            rb = sbr("rb", [P, EXP])
            cst = sbr("cst", [P, EXP])
            neg = sbr("neg", [P, EXP])
            zero = sbr("zero", [P, D])
            pad = sbr("pad", [P, TILES, 2])
            x2b = sbr("x2b", [P, KD, BLK])
            xsq = sbr("xsq", [P, KD, BLK])
            xr = sbr("xr", [P, 2, NC, D])
            x2r = sbr("x2r", [P, 2, NC, D])
            lg = sbr("lg", [P, TT, EXP])
            top = sbr("top", [P, TT, 8])
            tix = sbr("tix", [P, TT, 8], U32)
            tif = sbr("tif", [P, TT, TOPK])
            wx = sbr("wx", [P, TT, TOPK])
            wsum = sbr("wsum", [P, TT])
            oh = sbr("oh", [P, TT, TOPK, EXP])
            pick = sbr("pick", [P, TT, TOPK, EXP])
            chosen = sbr("chosen", [P, EXP, TT])
            upto = sbr("upto", [P, EXP, TT])
            need_i = sbr("need_i", [P, EXP], I32)
            need = sbr("need", [P, EXP])
            ends = sbr("ends", [P, EXP])
            first = sbr("first", [P, EXP])
            pos = sbr("pos", [P, EXP, TT])
            cmp_e = sbr("cmp_e", [P, TILES, EXP])
            slot = sbr("slot", [P, TT, TOPK])
            slot_i = sbr("slot_i", [P, TT, TOPK], I32)
            slot_p = sbr("slot_p", [P, TT, TOPK], I32)
            slot_t = sbr("slot_t", [P, TT, TOPK])
            entry = sbr("entry", [P, TT, TOPK, 2])

            l_r = semr("ld"); s_set = semr("set"); s_pad = semr("pad"); s_pre = semr("pre")
            s_mean = semr("mean"); s_cent = semr("cent"); s_sq = semr("sq"); s_var = semr("var")
            s_lnv = semr("lnv"); s_rstd = semr("rstd"); s_xn = semr("xn"); s_xsq = semr("xsq")
            s_x2b = semr("x2b"); s_cps = semr("cps"); s_cst = semr("cst"); s_lps = semr("lps"); s_lg = semr("lg")
            s_xtp = semr("xtp"); s_xr = semr("xr"); s_x2p = semr("x2p"); s_x2r = semr("x2r")
            s_zout = semr("zout"); s_xout = (semr("xout_0"), semr("xout_1")); s_yout = (semr("yout_0"), semr("yout_1"))
            s_top = semr("top"); s_gap = semr("gap"); s_tif = semr("tif");
            s_chosen = semr("chosen"); s_exp = semr("exp"); s_wsum = semr("wsum"); s_entry = semr("entry")
            s_cnt = semr("cnt"); s_need = semr("need"); s_pos = semr("pos"); s_slot = semr("slot")
            s_etile = semr("etile"); s_scat = semr("scat")

            @block.sync
            def _(sp):
                sp.dma_start(keys[:], d["f_keys"]).then_inc(l_r, 16)
                sp.dma_start(rw[:], d["f_rw"]).then_inc(l_r, 16)
                sp.dma_start(rb[:], d["f_rb"].partition_broadcast(P)).then_inc(l_r, 16)
                sp.dma_start(rconst[:], d["rconst"]).then_inc(l_r, 16)
                sp.wait_ge(s_set, 4)
                sp.dma_start(slot_rows.rearrange("(p t) c -> p t c", p=P), pad[:]).then_inc(s_pad, 16)
                sp.dma_start(xn_rows[N:N + P], zero[:]).then_inc(s_zout, 16)
                sp.dma_start(y_rows[N:N + P], zero[:]).then_inc(s_zout, 16)
                with sp.Fori(0, NB // 2) as i:
                    for a in range(2):
                        b = 2 * i + a
                        sp.wait_ge(s_x2r, 2 * b + 2)
                        sp.dma_start(y_rows[bass.ds(b * BLK, BLK)].rearrange("(t p) c -> p t c", p=P), x2r[:, a]).then_inc(s_yout[a], 16)
                        sp.wait_ge(s_xr, 2 * b + 2)
                        sp.dma_start(xn_rows[bass.ds(b * BLK, BLK)].rearrange("(t p) c -> p t c", p=P), xr[:, a]).then_inc(s_xout[a], 16)
                sp.wait_ge(s_zout, 32)
                for a in range(2):
                    sp.wait_ge(s_xout[a], 16 * NB // 2)
                    sp.wait_ge(s_yout[a], 16 * NB // 2)

            @block.gpsimd
            def _(pool):
                pool.wait_ge(s_pad, 16)
                pool.wait_ge(s_entry, 2)
                pool.wait_ge(s_slot, 8)
                for tt in range(TT):
                    for j in range(TOPK):
                        pool.indirect_dma_start(out=slot_rows, out_offset=bass.IndirectOffsetOnAxis(ap=slot_i[:, tt, j:j + 1].bitcast(U32), axis=0),
                                                in_=entry[:, tt, j, :], in_offset=None).then_inc(s_scat, 16)
                pool.wait_ge(s_scat, 16 * TT * TOPK)

            @block.scalar
            def _(act):
                with act.Fori(0, NB // 2) as h:
                    for a in range(2):
                        i = 2 * h + a
                        act.wait_ge(s_x2p, 2 * i)
                        act.activation(x2b[:], x_t[:, :, bass.ds(i * BLK, BLK)], ACT.Copy).then_inc(s_x2b, 1)
                        act.wait_ge(s_cent, i + 1)
                        act.activation(sq[:], cent[:], ACT.Square).then_inc(s_sq, 1)
                        act.wait_ge(s_var, i + 1)
                        act.activation(lnv[:], psum[:, 0, :], ACT.Ln, bias=eps_ln[:, 0:1]).then_inc(s_lnv, 1)
                        act.wait_ge(s_lnv, i + 1)
                        act.activation(rstd[:], lnv[:], ACT.Exp, scale=-0.5).then_inc(s_rstd, 1)
                        act.wait_ge(s_xn, i + 1)
                        act.activation(xsq[:], xn[:], ACT.Square).then_inc(s_xsq, 1)
                        act.wait_ge(s_xout[a], 16 * h)
                        for u in range(2):
                            act.wait_ge(s_xtp, 2 * i + u + 1)
                            act.activation(xr[:, a, 2 * u:2 * u + 2], psum[:, 2 + u, :].rearrange("p (t n) -> p t n", t=2),
                                           ACT.Copy).then_inc(s_xr, 1)
                act.wait_ge(s_gap, 1)
                act.activation(wx[:], wx[:], ACT.Exp).then_inc(s_exp, 1)

            @block.vector
            def _(dve):
                dve.memset(zero[:], 0.0).then_inc(s_set, 1)
                dve.memset(pad[:, :, 1:2], 0.0).then_inc(s_set, 1)
                dve.memset(neg[:], -1.0).then_inc(s_set, 1)
                dve.wait_ge(l_r, 16 * 4)
                dve.tensor_copy(pad[:, :, 0:1].bitcast(U32), tok_no[:, TT:TT + 1].unsqueeze(1).to_broadcast([P, TILES, 1])).then_inc(s_set, 1)
                dve.tensor_copy(entry[:, :, :, 0:1].bitcast(U32),
                                tok_no[:, 0:TT].unsqueeze(2).unsqueeze(3).to_broadcast([P, TT, TOPK, 1])).then_inc(s_entry, 1)
                dve.tensor_tensor(ksq[:], keys[:], keys[:], ALU.mult).then_inc(s_pre, 1)
                dve.scalar_tensor_tensor(out=rt[:], in0=keys[:], scalar=2.0, in1=rw[:], op0=ALU.mult, op1=ALU.add).then_inc(s_pre, 1)
                dve.wait_ge(s_cps, 1)
                dve.tensor_tensor(cst[:], rb[:], psum[:, 1, 0:EXP], ALU.subtract).then_inc(s_cst, 1)
                dve.wait_ge(s_cst, 1)
                with dve.Fori(0, NB // 2) as h:
                    for a in range(2):
                        i = 2 * h + a
                        dve.wait_ge(s_mean, i + 1)
                        dve.tensor_tensor(cent[:], x_t[:, :, bass.ds(i * BLK, BLK)], psum[:, 0:1, :].to_broadcast([P, KD, BLK]),
                                          ALU.subtract).then_inc(s_cent, 1)
                        dve.wait_ge(s_rstd, i + 1)
                        dve.wait_ge(s_cent, i + 1)
                        dve.tensor_tensor(xn[:], cent[:], rstd[:].unsqueeze(1).to_broadcast([P, KD, BLK]), ALU.mult).then_inc(s_xn, 1)
                        dve.wait_ge(s_yout[a], 16 * h)
                        for u in range(2):
                            dve.wait_ge(s_x2p, 2 * i + u + 1)
                            dve.tensor_copy(x2r[:, a, 2 * u:2 * u + 2], psum[:, 4 + u, :].rearrange("p (t n) -> p t n", t=2)).then_inc(s_x2r, 1)
                        dve.wait_ge(s_lps, i + 1)
                        dve.tensor_tensor(lg[:, bass.ds(NC * i, NC)], psum[:, 1, 0:NC * EXP].rearrange("p (t e) -> p t e", t=NC),
                                          cst[:].unsqueeze(1).to_broadcast([P, NC, EXP]), ALU.add).then_inc(s_lg, 1)
                dve.wait_ge(s_lg, NB)
                for tt in range(TT):
                    dve.max(top[:, tt, :], lg[:, tt, :]).then_inc(s_top, 1)
                dve.wait_ge(s_top, TT)
                for tt in range(TT):
                    dve.max_index(tix[:, tt, :], top[:, tt, :], lg[:, tt, :]).then_inc(s_top, 1)
                dve.tensor_tensor(wx[:], top[:, :, 0:TOPK], top[:, :, 0:1].to_broadcast([P, TT, TOPK]), ALU.subtract).then_inc(s_gap, 1)
                dve.wait_ge(s_top, 2 * TT)
                dve.tensor_copy(tif[:], tix[:, :, 0:TOPK]).then_inc(s_tif, 1)
                dve.wait_ge(s_tif, 1)
                dve.tensor_tensor(oh[:].rearrange("p t j e -> p (t j) e"),
                                  tif[:].rearrange("p t j -> p (t j)").unsqueeze(2).to_broadcast([P, TT * TOPK, EXP]),
                                  expert_no.unsqueeze(1).to_broadcast([P, TT * TOPK, EXP]), ALU.is_equal).then_inc(s_tif, 1)
                dve.wait_ge(s_tif, 2)
                dve.tensor_reduce(chosen[:], oh[:].rearrange("p t j e -> p e t j"), AX_X, ALU.add).then_inc(s_chosen, 1)
                dve.wait_ge(s_exp, 1)
                dve.tensor_reduce(wsum[:], wx[:], AX_X, ALU.add).then_inc(s_wsum, 1)
                dve.wait_ge(s_wsum, 1)
                dve.reciprocal(wsum[:], wsum[:]).then_inc(s_wsum, 1)
                dve.wait_ge(s_wsum, 2)
                dve.tensor_tensor(entry[:, :, :, 1:2].rearrange("p t j o -> p t (j o)"), wx[:], wsum[:].unsqueeze(2).to_broadcast([P, TT, TOPK]),
                                  ALU.mult).then_inc(s_entry, 1)
                dve.wait_ge(s_cnt, 1)
                total = psum[:, 2, 0:EXP * TT].rearrange("p (e t) -> p e t", e=EXP)
                within = psum[:, 3, 0:EXP * TT].rearrange("p (e t) -> p e t", e=EXP)
                dve.tensor_tensor_scan(upto[:].rearrange("p e t -> p (e t)"), seg, psum[:, 2, 0:EXP * TT], 0.0, ALU.mult, ALU.add).then_inc(s_need, 1)
                dve.wait_ge(s_need, 1)
                dve.tensor_scalar(need[:], upto[:, :, TT - 1], float(P - 1), None, ALU.add).then_inc(s_need, 1)
                dve.wait_ge(s_need, 2)
                dve.tensor_copy(need_i[:], need[:]).then_inc(s_need, 1)
                dve.wait_ge(s_need, 3)
                dve.tensor_scalar(need_i[:], need_i[:], 7, None, ALU.arith_shift_right).then_inc(s_need, 1)
                dve.wait_ge(s_need, 4)
                dve.tensor_copy(need[:], need_i[:]).then_inc(s_need, 1)
                dve.wait_ge(s_need, 5)
                dve.tensor_tensor_scan(ends[:], ones[:, 0:EXP], need[:], 0.0, ALU.mult, ALU.add).then_inc(s_need, 1)
                dve.wait_ge(s_need, 6)
                dve.tensor_tensor(first[:], ends[:], need[:], ALU.subtract).then_inc(s_need, 1)
                dve.wait_ge(s_need, 7)
                dve.tensor_scalar(first[:], first[:], float(P), -1.0, ALU.mult, ALU.add).then_inc(s_need, 1)
                dve.tensor_tensor(pos[:], upto[:], total, ALU.subtract).then_inc(s_pos, 1)
                dve.wait_ge(s_pos, 1)
                dve.tensor_tensor(pos[:], pos[:], within, ALU.add).then_inc(s_pos, 1)
                dve.wait_ge(s_pos, 2)
                dve.wait_ge(s_need, 8)
                dve.tensor_tensor(pos[:], pos[:], first[:].unsqueeze(2).to_broadcast([P, EXP, TT]), ALU.add).then_inc(s_pos, 1)
                dve.wait_ge(s_pos, 3)
                for j in range(TOPK):
                    dve.tensor_tensor(pick[:, :, j, :], oh[:, :, j, :], pos[:].rearrange("p e t -> p t e"), ALU.mult).then_inc(s_pos, 1)
                dve.wait_ge(s_pos, 3 + TOPK)
                dve.tensor_reduce(slot[:], pick[:], AX_X, ALU.add).then_inc(s_slot, 1)
                dve.wait_ge(s_slot, 1)
                dve.tensor_copy(slot_i[:], slot[:]).then_inc(s_slot, 1)
                dve.wait_ge(s_slot, 2)
                dve.tensor_scalar(slot_p[:], slot_i[:], 7, None, ALU.arith_shift_right).then_inc(s_slot, 1)
                dve.wait_ge(s_slot, 3)
                dve.tensor_copy(slot_t[:], slot_p[:]).then_inc(s_slot, 1)
                dve.wait_ge(s_slot, 4)
                dve.tensor_scalar(slot_t[:], slot_t[:], float(1 - P * TILES), None, ALU.mult).then_inc(s_slot, 1)
                dve.wait_ge(s_slot, 5)
                dve.tensor_scalar(slot[:], slot[:], float(TILES), None, ALU.mult).then_inc(s_slot, 1)
                dve.wait_ge(s_slot, 6)
                dve.tensor_tensor(slot[:], slot[:], slot_t[:], ALU.add).then_inc(s_slot, 1)
                dve.wait_ge(s_slot, 7)
                dve.tensor_copy(slot_i[:], slot[:]).then_inc(s_slot, 1)
                dve.tensor_tensor(cmp_e[:], tile_no.unsqueeze(2).to_broadcast([P, TILES, EXP]),
                                  ends[:].unsqueeze(1).to_broadcast([P, TILES, EXP]), ALU.is_ge).then_inc(s_etile, 1)
                dve.wait_ge(s_etile, 1)
                dve.tensor_reduce(e_tile[:], cmp_e[:], AX_X, ALU.add).then_inc(s_etile, 1)
                dve.wait_ge(s_etile, 2)
                dve.tensor_scalar(e_tile[:], e_tile[:], float(EXP - 1), None, ALU.min).then_inc(s_etile, 1)
                dve.wait_ge(s_etile, 3)
                dve.tensor_copy(e_int[:], e_tile[:]).then_inc(s_etile, 1)
                dve.wait_ge(s_etile, 4)

            @block.tensor
            def _(pe):
                pe.wait_ge(s_pre, 2)
                pe.wait_ge(s_set, 4)
                for k in range(KD):
                    mm = pe.matmul(psum[:, 1, 0:EXP], ones[:, 0:P], ksq[:, k, :], start=k == 0, stop=k == KD - 1)
                mm.then_inc(s_cps, 1)
                pe.wait_ge(s_cst, 1)
                with pe.Fori(0, NB) as i:
                    for k in range(KD):
                        mm = pe.matmul(psum[:, 0, :], mean_w, x_t[:, k, bass.ds(i * BLK, BLK)], start=k == 0, stop=k == KD - 1)
                    mm.then_inc(s_mean, 1)
                    pe.wait_ge(s_x2b, i + 1)
                    pe.wait_ge(s_x2r, 2 * i)
                    for u in range(2):
                        for c in range(2):
                            for k in range(KD):
                                mm = pe.transpose(psum[:, 4 + u, c * D + k * P:c * D + (k + 1) * P],
                                                  x2b[:, k, (2 * u + c) * P:(2 * u + c + 1) * P], ident)
                        mm.then_inc(s_x2p, 1)
                    pe.wait_ge(s_sq, i + 1)
                    for k in range(KD):
                        mm = pe.matmul(psum[:, 0, :], mean_w, sq[:, k, :], start=k == 0, stop=k == KD - 1)
                    mm.then_inc(s_var, 1)
                    pe.wait_ge(s_xn, i + 1)
                    pe.wait_ge(s_xr, 2 * i)
                    for u in range(2):
                        for c in range(2):
                            for k in range(KD):
                                mm = pe.transpose(psum[:, 2 + u, c * D + k * P:c * D + (k + 1) * P],
                                                  xn[:, k, (2 * u + c) * P:(2 * u + c + 1) * P], ident)
                        mm.then_inc(s_xtp, 1)
                    pe.wait_ge(s_xsq, i + 1)
                    pe.wait_ge(s_lg, i)
                    for c in range(NC):
                        for k in range(KD):
                            pe.matmul(psum[:, 1, c * EXP:(c + 1) * EXP], xn[:, k, c * P:(c + 1) * P], rt[:, k, :], start=k == 0, stop=False)
                        for k in range(KD):
                            mm = pe.matmul(psum[:, 1, c * EXP:(c + 1) * EXP], xsq[:, k, c * P:(c + 1) * P], neg[:], start=False, stop=k == KD - 1)
                    mm.then_inc(s_lps, 1)
                pe.wait_ge(s_chosen, 1)
                pe.wait_ge(s_xr, 2 * NB)
                pe.matmul(psum[:, 2, 0:EXP * TT], ones[:, 0:P], chosen[:].rearrange("p e t -> p (e t)"), start=True, stop=True)
                pe.matmul(psum[:, 3, 0:EXP * TT], causal, chosen[:].rearrange("p e t -> p (e t)"), start=True, stop=True).then_inc(s_cnt, 1)

        with ExitStack() as st, nc.Block() as block:
            def sbe(name, shape, dt=F32):
                return st.enter_context(nc.sbuf_tensor(name, shape, dt))

            def seme(name):
                return sem("e_" + name)

            w1 = sbe("w1", [P, 2, KD * F + FF])
            w2 = sbe("w2", [P, 2, FF, D])
            b2 = sbe("b2", [P, EXP, D])
            slots = sbe("slots", [P, TILES * 2])
            idx = sbe("idx", [P, 4], U32)
            xg = sbe("xg", [P, 4, D])
            xgt = sbe("xgt", [P, 2, KD, P])
            hid = sbe("hid", [P, 2, FF, P])
            yb = sbe("yb", [P, D])
            yt = sbe("yt", [P, 2, D])
            l_slots = seme("slots"); l_b2 = seme("ld_b2")
            l_w1 = [seme("ld_w1_0"), seme("ld_w1_1")]
            l_w2 = [seme("ld_w2_0"), seme("ld_w2_1")]
            l_xg = [seme("ld_xg_%d" % n) for n in range(4)]
            s_idx = seme("idx"); s_xt = seme("xt"); s_xgt = seme("xgt"); s_hp = seme("hp"); s_hid = seme("hid"); s_yp = seme("yp")
            s_yb = seme("yb"); s_y = seme("y"); s_add = seme("add")
            G = 4

            @block.sync
            def _(sp):
                sp.dma_start(slots[:], slot_rows.rearrange("(p t) c -> p (t c)", p=P)).then_inc(l_slots, 16)

                def expert(t):
                    return sp.value_load(e_int[0:1, bass.ds(t, 1)], min_val=0, max_val=EXP - 1)

                def load_w1(e, a):
                    sp.dma_start(w1[:, a], d["f_w1"][bass.ds(e, 1)].rearrange("o p f -> p (o f)")).then_inc(l_w1[a], 16)

                def load_w2(e, a):
                    sp.dma_start(w2[:, a], d["f_w2"][bass.ds(e, 1)].rearrange("o p k f -> p (o k) f")).then_inc(l_w2[a], 16)

                for t in range(2):
                    e = expert(t)
                    load_w1(e, t)
                    load_w2(e, t)
                sp.dma_start(b2[:], d["f_b2"].partition_broadcast(P)).then_inc(l_b2, 16)
                with sp.Fori(0, TILES // 2 - 1) as i:
                    for a in range(2):
                        t = 2 * i + a
                        e = expert(t + 2)
                        sp.wait_ge(s_hid, FF * (t + 1))
                        load_w1(e, a)
                        sp.wait_ge(s_yp, t + 1)
                        load_w2(e, a)
                sp.wait_ge(s_add, 16 * TILES)
                sp.dma_start(d["out"].rearrange("o n c -> (o n) c"), y_rows[0:N]).then_inc(out_done, 16)
                sp.wait_ge(out_done, 16)

            @block.gpsimd
            def _(pool):
                def gather(t, a):
                    pool.tensor_copy(idx[:, a:a + 1], slots[:, bass.ds(2 * t, 1)].bitcast(U32)).then_inc(s_idx, 1)
                    count = pool.to_reg(t + 1)
                    pool.wait_ge(l_slots, 16)
                    pool.wait_ge(s_idx, count)
                    pool.indirect_dma_start(out=xg[:, a], out_offset=None, in_=xn_rows,
                                            in_offset=bass.IndirectOffsetOnAxis(ap=idx[:, a:a + 1], axis=0)).then_inc(l_xg[a], 16)

                def add(t, a):
                    count = pool.to_reg(t + 1)
                    pool.wait_ge(l_slots, 16)
                    pool.wait_ge(s_y, count)
                    pool.indirect_dma_start(out=y_rows, out_offset=bass.IndirectOffsetOnAxis(ap=idx[:, a:a + 1], axis=0),
                                            in_=yt[:, a % 2], in_offset=None, compute_op=ALU.add).then_inc(s_add, 16)

                pool.wait_ge(l_slots, 16)
                for a in range(G - 1):
                    gather(a, a)
                with pool.Fori(0, TILES // G - 1) as i:
                    for a in range(G):
                        t = G * i + a
                        pool.wait_ge(s_add, 16 * t)
                        pool.wait_ge(s_xt, t)
                        gather(t + G - 1, (a + G - 1) % G)
                        add(t, a)
                for t in range(TILES - G, TILES):
                    pool.wait_ge(s_add, 16 * t)
                    if t + G - 1 < TILES:
                        pool.wait_ge(s_xt, t)
                        gather(t + G - 1, (t + G - 1) % G)
                    add(t, t % G)

            @block.scalar
            def _(act):
                with act.Fori(0, TILES // 2) as i:
                    for a in range(2):
                        t = 2 * i + a
                        for b in range(2):
                            act.wait_ge(s_hp, 2 * t + b + 1)
                            for f in range(FF // 2 * b, FF // 2 * (b + 1)):
                                act.activation(hid[:, a, f, :], psum[:, 2 * a + b, (f % 4) * P:(f % 4 + 1) * P], ACT.Gelu,
                                               bias=w1[:, a, KD * F + f:KD * F + f + 1]).then_inc(s_hid, 1)
                        act.wait_ge(s_yp, t)

            @block.vector
            def _(dve):
                def turn(t, a):
                    dve.wait_ge(s_xt, t + 1)
                    dve.tensor_copy(xgt[:, a], psum[:, 6 + a, 0:D].rearrange("p (k t) -> p k t", k=KD)).then_inc(s_xgt, 1)

                def result(t, a):
                    e = dve.value_load(e_int[0:1, bass.ds(t, 1)], min_val=0, max_val=EXP - 1)
                    dve.wait_ge(s_yp, t + 1)
                    dve.wait_ge(s_y, t)
                    dve.tensor_tensor(yb[:], psum[:, 4 + a, 0:D], b2[:, bass.ds(e, 1), :].rearrange("p o n -> p (o n)"), ALU.add).then_inc(s_yb, 1)
                    dve.wait_ge(s_yb, t + 1)
                    dve.tensor_scalar(yt[:, a], yb[:], slots[:, bass.ds(2 * t + 1, 1)], None, ALU.mult).then_inc(s_y, 1)
                    dve.wait_ge(s_add, 16 * t)

                dve.wait_ge(l_slots, 16)
                dve.wait_ge(l_b2, 16)
                turn(0, 0)
                with dve.Fori(0, TILES // 2 - 1) as i:
                    for a in range(2):
                        t = 2 * i + a
                        dve.wait_ge(s_hp, 2 * t)
                        turn(t + 1, 1 - a)
                        result(t, a)
                dve.wait_ge(s_hp, 2 * (TILES - 2))
                turn(TILES - 1, 1)
                result(TILES - 2, 0)
                result(TILES - 1, 1)

            @block.tensor
            def _(pe):
                def hidden(t, a, rnd, s):
                    pe.wait_ge(l_xg[s], 16 * rnd)
                    for k in range(KD):
                        mm = pe.transpose(psum[:, 6 + a, k * P:(k + 1) * P], xg[:, s, k * P:(k + 1) * P], ident)
                    mm.then_inc(s_xt, 1)

                def first(t, a, rnd):
                    pe.wait_ge(s_xgt, t + 1)
                    pe.wait_ge(l_w1[a], 16 * rnd)
                    for b in range(2):
                        for f in range(FF // 2 * b, FF // 2 * (b + 1)):
                            for k in range(KD):
                                mm = pe.matmul(psum[:, 2 * a + b, (f % 4) * P:(f % 4 + 1) * P], w1[:, a, k * F + f * P:k * F + (f + 1) * P],
                                               xgt[:, a, k, :], start=k == 0, stop=k == KD - 1)
                        mm.then_inc(s_hp, 1)

                def second(t, a, rnd):
                    pe.wait_ge(l_w2[a], 16 * rnd)
                    pe.wait_ge(s_hid, FF * (t + 1))
                    for f in range(FF):
                        mm = pe.matmul(psum[:, 4 + a, 0:D], hid[:, a, f, :], w2[:, a, f, :], start=f == 0, stop=f == FF - 1)
                    mm.then_inc(s_yp, 1)
                    pe.wait_ge(s_y, t)

                hidden(0, 0, 1, 0)
                first(0, 0, 1)
                with pe.Fori(0, TILES // G - 1) as i:
                    for a in range(G):
                        t = G * i + a
                        pe.wait_ge(s_xgt, t)
                        hidden(t + 1, (a + 1) % 2, i + 1 + (a + 1) // G, (a + 1) % G)
                        pe.wait_ge(s_hid, FF * t)
                        first(t + 1, (a + 1) % 2, 2 * i + 1 + (a + 1) // 2)
                        second(t, a % 2, 2 * i + 1 + a // 2)
                for t in range(TILES - G, TILES):
                    if t + 1 < TILES:
                        pe.wait_ge(s_xgt, t)
                        hidden(t + 1, (t + 1) % 2, (t + 1) // G + 1, (t + 1) % G)
                        pe.wait_ge(s_hid, FF * t)
                        first(t + 1, (t + 1) % 2, (t + 1) // 2 + 1)
                    second(t, t % 2, t // 2 + 1)


def layouts(i):
    rope, const = constants()

    def rows(w):
        return np.ascontiguousarray(w.reshape(-1, P, w.shape[-1]).transpose(1, 0, 2))

    def doubled(w):
        w = w.reshape(D, H, 1, HD)
        return rows(np.concatenate([w, w], axis=2).reshape(D, 2 * D))

    def column(v):
        return np.ascontiguousarray(v.reshape(-1, P).T)

    def padded(w):
        w = w.reshape(H, HD, w.shape[-1])
        return rows(np.concatenate([w, np.zeros_like(w)], axis=1).reshape(2 * D, w.shape[-1]))

    return {
        "x_t": rows(i["x"][0].T), "const": const, "rope": rope,
        "a_wq": doubled(i["L0_attn_Wq"]), "a_wk": doubled(i["L0_attn_Wk"]), "a_wv": rows(i["L0_attn_Wv"]),
        "a_wo": rows(i["L0_attn_Wo"]), "a_wg1": rows(i["L0_attn_Wg1"]), "a_wg2": np.ascontiguousarray(i["L0_attn_Wg2"]),
        "a_nw": column(i["L0_attn_norm_w"]),
        "ctx_t": rows(np.pad(i["ctx_1024"][0].T, ((0, 0), (0, KEYP - KEYS)))),
        "x_wq": rows(i["L0_xattn_W_q"].T), "x_wk": rows(i["L0_xattn_W_k"].T), "x_wv": rows(i["L0_xattn_W_v"].T),
        "x_wo": padded(i["L0_xattn_W_o"].T), "x_bq": column(i["L0_xattn_b_q"]), "x_bk": column(i["L0_xattn_b_k"]),
        "x_bv": i["L0_xattn_b_v"].reshape(D), "x_bo": column(i["L0_xattn_b_o"]),
        "f_keys": rows(i["L0_ffn_keys"].T), "f_rw": rows(i["L0_ffn_rw"].T), "f_rb": i["L0_ffn_rb"].reshape(EXP),
        "f_b2": np.ascontiguousarray(i["L0_ffn_b2"]), "rconst": routing_constants(),
        "f_w1": np.concatenate([i["L0_ffn_w1"].transpose(0, 2, 1).reshape(EXP, KD, P, F).transpose(0, 2, 1, 3).reshape(EXP, P, KD * F),
                                i["L0_ffn_b1"].reshape(EXP, FF, P).transpose(0, 2, 1)], axis=2),
        "f_w2": np.ascontiguousarray(i["L0_ffn_w2"].transpose(0, 2, 1).reshape(EXP, FF, P, D).transpose(0, 2, 1, 3)),
    }


def kernel(**inputs):
    import numpy as _np
    import concourse.bacc as _bacc
    from concourse import mybir as _mybir
    from concourse.bass_utils import run_bass_kernel_spmd as _run

    laid_out = layouts({name: _np.asarray(a) for name, a in inputs.items()})
    nc = _bacc.Bacc("TRN2", target_bir_lowering=False, num_devices=1)
    arrays, d = {}, {}
    for name, a in laid_out.items():
        arrays[f"in_{name}_dram"] = _np.ascontiguousarray(a)
        d[name] = nc.dram_tensor(f"in_{name}_dram", a.shape, _mybir.dt.from_np(a.dtype), kind="ExternalInput").ap()
    d["out"] = nc.dram_tensor("out_0_dram", (1, N, D), F32, kind="ExternalOutput").ap()
    decoder_layer(nc, d)
    r = _run(nc, [arrays], core_ids=[0])
    return r.results[0]["out_0_dram"]
```

```python
from contextlib import ExitStack

import numpy as np

import concourse.bass as bass
from concourse import mybir

ALU = mybir.AluOpType
ACT = mybir.ActivationFunctionType
F32 = mybir.dt.float32
BF16 = mybir.dt.bfloat16
U32 = mybir.dt.uint32
I32 = mybir.dt.int32
AX_X = mybir.AxisListType.X

P = 128
N = 2048
D = 256
KD = D // P
H = 16
HD = D // H
BLK = 512
NB = N // BLK
CH = 128
NC = BLK // CH
FT = 2 * D // P
HPT = H // FT
KEYS = 1601
KT = -(-KEYS // P)
KEYP = KT * P
KPART = KEYP // 4
EXP = 16
TOPK = 4
F = 1024
FF = F // P
TT = N // P
TILES = N * TOPK // P + EXP
NEG_LN_EPS = 1e-05
RMS_EPS = 1e-06


def constants():
    j = np.arange(HD, dtype=np.float32)
    freq = np.power(np.float32(10000.0), (np.float32(-2.0) * j / np.float32(HD)).astype(np.float32)).astype(np.float32)
    theta = (np.arange(N, dtype=np.float32)[:, None] * freq[None]).astype(np.float32)
    both = np.concatenate([np.cos(theta), np.sin(theta)], axis=1).T
    rope = np.ascontiguousarray(np.tile(both, (HPT, 1)).astype(np.float32))
    p = np.arange(P)
    const = np.zeros((P, 6, P), np.float32)
    const[:, 0, :] = 1.0 / D
    const[:, 1, :] = p[:, None] == p[None, :]
    const[:, 2, :] = p[:, None] <= p[None, :]
    const[:, 3, 0:64] = (p[:, None] // 32) == (np.arange(64)[None, :] // HD)
    const[:, 3, 64:64 + EXP] = np.arange(EXP)[None, :]
    const[:, 3, 96:96 + HPT] = (p[:, None] // 32) == np.arange(HPT)[None, :]
    const[:, 4, :] = (p[:, None] % 32 == HD) & (p[:, None] // 32 == p[None, :] // 32)
    for k in range(KD):
        const[:, 5, k * H:(k + 1) * H] = (k * P + p[:, None]) // HD == np.arange(H)[None, :]
    return rope, const


def routing_constants():
    table = np.zeros((P, TT * EXP + TILES + TT + 1), np.float32)
    table[:, 0:TT * EXP] = np.tile(np.arange(TT) > 0, EXP)[None]
    table[:, TT * EXP:TT * EXP + TILES] = np.arange(TILES)[None]
    table[:, TT * EXP + TILES:] = np.arange(TT + 1)[None] * P + np.arange(P)[:, None]
    return table


def decoder_layer(nc, d):
    with ExitStack() as ctx:
        def sb(name, shape, dt=F32):
            return ctx.enter_context(nc.sbuf_tensor(name, shape, dt))

        def sem(name):
            return ctx.enter_context(nc.semaphore(name))

        psum = ctx.enter_context(nc.psum_tensor("psum", [P, 8, BLK], F32))

        x_t = sb("x_t", [P, KD, N])
        const = sb("const", [P, 6, P])
        rope = sb("rope", [P, N])
        mean_w, ident, causal = const[:, 0, :], const[:, 1, :], const[:, 2, :]
        own_state, expert_no, head_rows, den_sel = const[:, 3, 0:64], const[:, 3, 64:64 + EXP], const[:, 3, 96:96 + HPT], const[:, 4, :]

        eps_ln = sb("eps_ln", [P, 1])
        eps_rms = sb("eps_rms", [P, 1])
        ones = sb("ones", [P, BLK])

        a_wq = sb("a_wq", [P, KD, 2 * D])
        a_wk = sb("a_wk", [P, KD, 2 * D])
        a_wv = sb("a_wv", [P, KD, D])
        a_wo = sb("a_wo", [P, KD, D])
        a_wg1 = sb("a_wg1", [P, KD, H])
        a_wg2 = sb("a_wg2", [H, D])
        a_nw = sb("a_nw", [P, KD])
        cent = sb("cent", [P, KD, BLK])
        sq = sb("sq", [P, KD, BLK])
        lnv = sb("lnv", [P, BLK])
        rstd = sb("rstd", [P, BLK])
        xn = sb("xn", [P, KD, BLK])

        ld_x, ld_const, ld_rope, ld_aw, ld_xw, ld_ctx, out_done = (sem(s) for s in (
            "ld_x", "ld_const", "ld_rope", "ld_aw", "ld_xw", "ld_ctx", "out_done"))
        set_up = sem("set_up")

        a_sems = []
        with ExitStack() as st, nc.Block() as block:
            def sba(name, shape, dt=F32):
                return st.enter_context(nc.sbuf_tensor(name, shape, dt))

            def sema(name):
                a_sems.append(nc.alloc_semaphore(name="a_" + name))
                return a_sems[-1]

            ek = sba("ek", [P, FT, BLK])
            zz = sba("zz", [P, FT, BLK])
            kf = sba("kf", [P, FT, BLK])
            eq = sba("eq", [P, FT, BLK])
            qc = sba("qc", [P, FT, BLK])
            qx = sba("qx", [P, FT, NC, HPT, CH])
            v_pl = sba("v_pl", [P, NC, D + 64])
            v_hd = sba("v_hd", [P, NC, H, 32])
            g1 = sba("g1", [H, BLK])
            gs = sba("gs", [P, KD, BLK])
            kft = sba("kft", [P, 2, FT, P])
            am = sba("am", [P, 2, HPT, CH])
            st8 = sba("st8", [P, 2, FT, 64])
            st_d = sba("st_d", [P, FT, 64])
            og = sba("og", [P, KD, BLK])
            nbm = sba("nbm", [P, FT])
            ngm = sba("ngm", [P, FT])
            dmx = sba("dmx", [P, FT])
            alp = sba("alp", [P, FT])
            z0 = sba("z0", [P, FT])
            a_wos = sba("a_wos", [P, KD, D])

            s_wos = sema("wos")
            s_mean = sema("mean"); s_cent = sema("cent"); s_sq = sema("sq"); s_var = sema("var")
            s_lnv = sema("lnv"); s_rstd = sema("rstd"); s_xn = sema("xn")
            s_kps = sema("kps"); s_nbm = sema("nbm"); s_dmx = sema("dmx"); s_ngm = sema("ngm")
            s_ek = sema("ek"); s_alp = sema("alp"); s_z0 = sema("z0"); s_zz = sema("zz"); s_kf = sema("kf")
            s_qps = sema("qps"); s_eq = sema("eq"); s_qc = sema("qc"); s_rq = sema("rq"); s_rr = sema("rr")
            s_qf = sema("qf"); s_qx = sema("qx")
            s_vps = sema("vps"); s_vpl = sema("vpl"); s_vhd = sema("vhd")
            s_h1 = sema("h1"); s_g1 = sema("g1"); s_gps = sema("gps"); s_eg = sema("eg"); s_g2 = sema("g2"); s_gs = sema("gs")
            s_ktp = sema("ktp"); s_kft = sema("kft"); s_aps = sema("aps"); s_am = sema("am")
            s_avr = sema("avr"); s_out = sema("out"); s_std = sema("std"); s_st = sema("st"); s_og = sema("og")
            s_osq = sema("osq"); s_ss = sema("ss"); s_lno = sema("lno"); s_ro = sema("ro"); s_on = sema("on")
            s_wps = sema("wps"); s_x1 = sema("x1")

            @block.sync
            def _(sp):
                sp.dma_start(x_t[:, :, :], d["x_t"]).then_inc(ld_x, 16)
                sp.dma_start(const[:, :, :], d["const"]).then_inc(ld_const, 16)
                for dst, name in ((a_wk, "a_wk"), (a_wq, "a_wq"), (a_wv, "a_wv"), (a_wo, "a_wo"), (a_wg1, "a_wg1"),
                                  (a_wg2, "a_wg2"), (a_nw, "a_nw")):
                    sp.dma_start(dst[:], d[name]).then_inc(ld_aw, 16)
                sp.dma_start(rope[:, :], d["rope"]).then_inc(ld_rope, 16)

            @block.gpsimd
            def _(pool):
                pool.memset(v_hd[:], 0.0).then_inc(set_up, 1)
                pool.wait_ge(ld_const, 16)
                pool.wait_ge(ld_rope, 16)
                with pool.Fori(0, NB) as i:
                    for f in range(FT):
                        count = pool.to_reg(FT * i + f + 1)
                        pool.wait_ge(ld_rope, 16)
                        pool.wait_ge(s_ek, count)
                        if f == 0:
                            pool.wait_ge(s_avr, NC * FT * i)
                        pool.tensor_tensor(kf[:, f, :], ek[:, f, :], rope[:, bass.ds(i * BLK, BLK)], ALU.mult).then_inc(s_kf, 1)
                    for u in range(2):
                        count = pool.to_reg(2 * i + u + 1)
                        pool.wait_ge(ld_const, 16)
                        pool.wait_ge(s_vpl, count)
                        src = v_pl[:, 2 * u:2 * u + 2, 0:D].rearrange("p c (h e d) -> p c h e d", e=2, d=HD)
                        for e in range(2):
                            for c in range(2):
                                dst = v_hd[:, 2 * u + c].rearrange("p (h e) d -> p h e d", e=2)
                                pool.tensor_scalar(dst[:, :, e, HD * e:HD * e + HD], src[:, c, :, e, :], 1.0, 1.0,
                                                   ALU.mult, ALU.mult).then_inc(s_vhd, 1)
                    for f in range(FT):
                        count = pool.to_reg(FT * i + f + 1)
                        pool.wait_ge(ld_const, 16)
                        pool.wait_ge(s_qf, count)
                        for g in range(HPT):
                            pool.tensor_scalar(qx[:, f, :, g, :], qc[:, f, :].rearrange("p (c t) -> p c t", c=NC),
                                               head_rows[:, g:g + 1], 1.0, ALU.mult, ALU.mult).then_inc(s_qx, 1)

            @block.scalar
            def _(act):
                act.preload_act_table_set("natural_log_exp_and_others")
                act.wait_ge(set_up, 6)
                with act.Fori(0, NB) as i:
                    act.wait_ge(s_cent, i + 1)
                    act.activation(sq[:], cent[:], ACT.Square).then_inc(s_sq, 1)
                    act.wait_ge(s_var, i + 1)
                    act.activation(lnv[:], psum[:, 0, :], ACT.Ln, bias=eps_ln[:, 0:1]).then_inc(s_lnv, 1)
                    act.wait_ge(s_lnv, i + 1)
                    act.activation(rstd[:], lnv[:], ACT.Exp, scale=-0.5).then_inc(s_rstd, 1)
                    for f in range(FT):
                        act.wait_ge(s_ngm, FT * i + f + 1)
                        if f == 0:
                            act.wait_ge(s_zz, FT * i)
                            act.wait_ge(s_kf, FT * i)
                        act.activation(ek[:, f, :], psum[:, 1 + f % 2, :], ACT.Exp, bias=ngm[:, f:f + 1]).then_inc(s_ek, 1)
                    act.activation(alp[:], dmx[:], ACT.Exp).then_inc(s_alp, 1)
                    for f in range(FT):
                        act.wait_ge(s_qps, FT * i + f + 1)
                        act.activation(eq[:, f, :], psum[:, 1 + f % 2, :], ACT.Exp, scale=-1.0).then_inc(s_eq, 1)
                    for u in range(2):
                        act.wait_ge(s_vps, 2 * i + u + 1)
                        act.activation(v_pl[:, 2 * u:2 * u + 2, 0:D], psum[:, 1 + u, :].rearrange("p (c n) -> p c n", c=2),
                                       ACT.Copy).then_inc(s_vpl, 1)
                    act.wait_ge(s_h1, i + 1)
                    act.activation(g1[:], psum[0:H, 1, :], ACT.Copy).then_inc(s_g1, 1)
                    for t in range(KD):
                        act.wait_ge(s_gps, KD * i + t + 1)
                        if t == 0:
                            act.wait_ge(s_og, NC * i)
                        act.activation(gs[:, t, :], psum[:, 2 - t, :], ACT.Exp, scale=-1.0).then_inc(s_eg, 1)
                    for c in range(NC):
                        act.wait_ge(s_ktp, NC * i + c + 1)
                        if c < 2:
                            act.wait_ge(s_out, NC * i)
                        else:
                            act.wait_ge(s_out, NC * i + c - 1)
                        act.activation(kft[:, c % 2], psum[:, 7, :].rearrange("p (f t) -> p f t", f=FT),
                                       ACT.Copy).then_inc(s_kft, 1)
                    act.wait_ge(s_og, NC * i + NC)
                    act.activation(sq[:], og[:], ACT.Square).then_inc(s_osq, 1)
                    act.wait_ge(s_ss, i + 1)
                    act.activation(lnv[:], psum[:, 0, :], ACT.Ln, bias=eps_rms[:, 0:1]).then_inc(s_lno, 1)
                    act.wait_ge(s_lno, i + 1)
                    act.activation(rstd[:], lnv[:], ACT.Exp, scale=-0.5).then_inc(s_ro, 1)

            @block.vector
            def _(dve):
                dve.memset(eps_ln[:], NEG_LN_EPS).then_inc(set_up, 1)
                dve.memset(eps_rms[:], RMS_EPS).then_inc(set_up, 1)
                dve.memset(ones[:], 1.0).then_inc(set_up, 1)
                dve.memset(ngm[:], 0.0).then_inc(set_up, 1)
                dve.memset(zz[:, :, BLK - 1:BLK], 1.0).then_inc(set_up, 1)
                dve.wait_ge(set_up, 6)
                dve.memset(st8[:], 0.0).then_inc(s_wos, 1)
                dve.memset(v_pl[:, :, D:D + 64], 0.0).then_inc(s_wos, 1)
                dve.wait_ge(ld_aw, 16 * 7)
                for k in range(KD):
                    dve.tensor_scalar(a_wos[:, k, :], a_wo[:, k, :], a_nw[:, k:k + 1], None, ALU.mult).then_inc(s_wos, 1)
                dve.wait_ge(s_wos, 2 + KD)
                dve.wait_ge(ld_rope, 16)
                dve.wait_ge(ld_x, 16)
                dve.wait_ge(ld_const, 16)
                with dve.Fori(0, NB) as i:
                    now = bass.ds(i * BLK, BLK)
                    dve.wait_ge(s_mean, i + 1)
                    dve.tensor_tensor(cent[:], x_t[:, :, now], psum[:, 0:1, :].to_broadcast([P, KD, BLK]),
                                      ALU.subtract).then_inc(s_cent, 1)
                    dve.wait_ge(s_rstd, i + 1)
                    dve.wait_ge(s_cent, i + 1)
                    dve.tensor_tensor(xn[:], cent[:], rstd[:].unsqueeze(1).to_broadcast([P, KD, BLK]), ALU.mult).then_inc(s_xn, 1)
                    for f in range(FT):
                        n = FT * i + f + 1
                        dve.wait_ge(s_kps, n)
                        dve.tensor_reduce(nbm[:, f:f + 1], psum[:, 1 + f % 2, :], AX_X, ALU.max, negate=True).then_inc(s_nbm, 1)
                        dve.wait_ge(s_nbm, n)
                        dve.tensor_scalar(dmx[:, f:f + 1], nbm[:, f:f + 1], ngm[:, f:f + 1], 0.0, ALU.subtract,
                                          ALU.min).then_inc(s_dmx, 1)
                        dve.wait_ge(s_dmx, n)
                        dve.tensor_tensor(ngm[:, f:f + 1], nbm[:, f:f + 1], ngm[:, f:f + 1], ALU.min).then_inc(s_ngm, 1)
                    for f in range(FT):
                        dve.wait_ge(s_eq, FT * i + f + 1)
                        if f == 0:
                            dve.wait_ge(s_avr, NC * FT * i)
                            dve.wait_ge(s_qx, FT * HPT * i)
                        dve.tensor_tensor(qc[:, f, :], psum[:, 1 + f % 2, :], rope[:, now], ALU.mult).then_inc(s_qc, 1)
                    dve.wait_ge(s_alp, i + 1)
                    dve.wait_ge(s_zz, FT * i)
                    dve.tensor_tensor(z0[:], zz[:, :, BLK - 1], alp[:], ALU.mult).then_inc(s_z0, 1)
                    dve.wait_ge(s_z0, i + 1)
                    for f in range(FT):
                        dve.wait_ge(s_ek, FT * i + f + 1)
                        dve.tensor_tensor_scan(zz[:, f, :], ones[:], ek[:, f, :], z0[:, f:f + 1], ALU.mult, ALU.add).then_inc(s_zz, 1)
                    dve.tensor_tensor(st8[:, 0], st8[:, 0], alp[:].unsqueeze(2).to_broadcast([P, FT, 64]), ALU.mult).then_inc(s_st, 1)
                    for f in range(FT):
                        n = FT * i + f + 1
                        dve.wait_ge(s_eq, n)
                        dve.wait_ge(s_zz, n)
                        dve.scalar_tensor_tensor(out=eq[:, f, :], in0=eq[:, f, :], scalar=1.0, in1=zz[:, f, :],
                                                 op0=ALU.add, op1=ALU.mult).then_inc(s_rq, 1)
                        dve.wait_ge(s_rq, n)
                        dve.reciprocal(eq[:, f, :], eq[:, f, :]).then_inc(s_rr, 1)
                        dve.wait_ge(s_rr, n)
                        dve.wait_ge(s_qc, n)
                        dve.tensor_tensor(qc[:, f, :], qc[:, f, :], eq[:, f, :], ALU.mult).then_inc(s_qf, 1)
                    dve.wait_ge(s_eg, KD * i + KD)
                    dve.tensor_scalar(gs[:], gs[:], 1.0, None, ALU.add).then_inc(s_g2, 1)
                    dve.wait_ge(s_g2, i + 1)
                    dve.reciprocal(gs[:], gs[:]).then_inc(s_gs, 1)
                    for u in range(NC * FT):
                        c, f = divmod(u, FT)
                        dve.wait_ge(s_aps, NC * FT * i + u + 1)
                        dve.wait_ge(s_avr, NC * FT * i + max(u - 1, 0))
                        dve.tensor_tensor(am[:, u % 2], psum[:, 3 + u % 2, :].rearrange("p (g t) -> p g t", g=HPT),
                                          causal.unsqueeze(1).to_broadcast([P, HPT, CH]), ALU.mult).then_inc(s_am, 1)
                        if f == FT - 1:
                            n = NC * i + c + 1
                            dve.wait_ge(s_out, n)
                            dve.tensor_tensor(st_d[:], psum[:, 0, :].rearrange("p (f n) -> p f n", f=FT)[:, :, 0:64],
                                              own_state.unsqueeze(1).to_broadcast([P, FT, 64]), ALU.mult).then_inc(s_std, 1)
                            dve.wait_ge(s_std, n)
                            dve.wait_ge(s_st, (NC + 1) * i + c + 1)
                            dve.tensor_tensor(st8[:, (c + 1) % 2], st8[:, c % 2], st_d[:], ALU.add).then_inc(s_st, 1)
                            dve.wait_ge(s_avr, NC * FT * i + FT * (c + 1))
                            dve.wait_ge(s_gs, i + 1)
                            if c == 0:
                                dve.wait_ge(s_osq, i)
                            dve.tensor_tensor(og[:, :, c * CH:(c + 1) * CH],
                                              psum[:, 5 + c % 2, 0:KD * CH].rearrange("p (k t) -> p k t", k=KD),
                                              gs[:, :, c * CH:(c + 1) * CH], ALU.mult).then_inc(s_og, 1)
                    dve.wait_ge(s_ro, i + 1)
                    dve.wait_ge(s_og, NC * i + NC)
                    dve.tensor_tensor(og[:], og[:], rstd[:].unsqueeze(1).to_broadcast([P, KD, BLK]), ALU.mult).then_inc(s_on, 1)
                    for t in range(KD):
                        dve.wait_ge(s_wps, KD * i + t + 1)
                        dve.tensor_tensor(x_t[:, t, now], psum[:, 2 - t, :], x_t[:, t, now], ALU.add).then_inc(s_x1, 1)

            @block.tensor
            def _(pe):
                pe.wait_ge(ld_const, 16)
                pe.wait_ge(ld_x, 16)
                pe.wait_ge(s_wos, 2 + KD)
                pe.wait_ge(set_up, 6)
                with pe.Fori(0, NB) as i:
                    now = bass.ds(i * BLK, BLK)
                    pe.wait_ge(s_x1, KD * i)
                    for k in range(KD):
                        mm = pe.matmul(psum[:, 0, :], mean_w, x_t[:, k, now], start=k == 0, stop=k == KD - 1)
                    mm.then_inc(s_mean, 1)
                    pe.wait_ge(s_sq, i + 1)
                    for k in range(KD):
                        mm = pe.matmul(psum[:, 0, :], mean_w, sq[:, k, :], start=k == 0, stop=k == KD - 1)
                    mm.then_inc(s_var, 1)
                    pe.wait_ge(s_xn, i + 1)
                    for f in range(FT):
                        if f >= 2:
                            pe.wait_ge(s_ek, FT * i + f - 1)
                        for k in range(KD):
                            mm = pe.matmul(psum[:, 1 + f % 2, :], a_wk[:, k, f * P:(f + 1) * P], xn[:, k, :], start=k == 0, stop=k == KD - 1)
                        mm.then_inc(s_kps, 1)
                    for f in range(FT):
                        if f < 2:
                            pe.wait_ge(s_ek, FT * i + f + 3)
                        else:
                            pe.wait_ge(s_eq, FT * i + f - 1)
                            pe.wait_ge(s_qc, FT * i + f - 1)
                        for k in range(KD):
                            mm = pe.matmul(psum[:, 1 + f % 2, :], a_wq[:, k, f * P:(f + 1) * P], xn[:, k, :], start=k == 0, stop=k == KD - 1)
                        mm.then_inc(s_qps, 1)
                    for u in range(2):
                        pe.wait_ge(s_eq, FT * i + 3 + u)
                        pe.wait_ge(s_qc, FT * i + 3 + u)
                        for c in range(2):
                            for k in range(KD):
                                mm = pe.matmul(psum[:, 1 + u, c * D:(c + 1) * D], xn[:, k, (2 * u + c) * CH:(2 * u + c + 1) * CH],
                                               a_wv[:, k, :], start=k == 0, stop=k == KD - 1)
                        mm.then_inc(s_vps, 1)
                    pe.wait_ge(s_vpl, 2 * i + 1)
                    for k in range(KD):
                        mm = pe.matmul(psum[0:H, 1, :], a_wg1[:, k, :], xn[:, k, :], start=k == 0, stop=k == KD - 1)
                    mm.then_inc(s_h1, 1)
                    pe.wait_ge(s_vpl, 2 * i + 2)
                    pe.wait_ge(s_g1, i + 1)
                    for t in range(KD):
                        pe.matmul(psum[:, 2 - t, :], a_wg2[:, t * P:(t + 1) * P], g1[:], start=True, stop=True).then_inc(s_gps, 1)

                    def values(u):
                        c, f = divmod(u, FT)
                        o = 5 + c % 2
                        if f == 0:
                            pe.wait_ge(s_st, (NC + 1) * i + c + 1)
                            if c >= 2:
                                pe.wait_ge(s_og, NC * i + c - 1)
                            else:
                                pe.wait_ge(s_og, NC * i)
                            pe.wait_ge(s_qf, FT * i + FT)
                            for ff in range(FT):
                                at = 64 * (ff % 2)
                                pe.matmul(psum[at:at + 64, o, (ff // 2) * CH:(ff // 2 + 1) * CH], st8[:, c % 2, ff, :],
                                          qc[:, ff, c * CH:(c + 1) * CH], start=ff < 2, stop=False, skip_group_check=True)
                            pe.wait_ge(s_vhd, 8 * i + 4 * (c // 2) + 4)
                        pe.wait_ge(s_am, NC * FT * i + u + 1)
                        for g in range(HPT):
                            h = HPT * f + g
                            at = 32 * (h // 2 % 4)
                            mm = pe.matmul(psum[at:at + 32, o, (h // 8) * CH:(h // 8 + 1) * CH], v_hd[:, c, h, :], am[:, u % 2, g, :],
                                           start=False, stop=f == FT - 1, skip_group_check=True)
                        mm.then_inc(s_avr, 1)

                    for u in range(NC * FT):
                        c, f = divmod(u, FT)
                        if f == 0:
                            pe.wait_ge(s_kf, FT * i + FT)
                            pe.wait_ge(s_kft, NC * i + c)
                            for ff in range(FT):
                                mm = pe.transpose(psum[:, 7, ff * P:(ff + 1) * P], kf[:, ff, c * CH:(c + 1) * CH], ident)
                            mm.then_inc(s_ktp, 1)
                        if c == 0:
                            pe.wait_ge(s_qx, FT * HPT * i + HPT * (f + 1))
                        pe.wait_ge(s_am, NC * FT * i + max(u - 1, 0))
                        pe.matmul(psum[:, 3 + u % 2, :], kf[:, f, c * CH:(c + 1) * CH],
                                  qx[:, f, c].rearrange("p g t -> p (g t)"), start=True, stop=True).then_inc(s_aps, 1)
                        if u > 0:
                            values(u - 1)
                        if f == 2:
                            pe.wait_ge(s_kft, NC * i + c + 1)
                            pe.wait_ge(s_st, (NC + 1) * i + c + 1)
                            for ff in range(FT):
                                mm = pe.matmul(psum[:, 0, ff * P:(ff + 1) * P], kft[:, c % 2, ff, :], v_pl[:, c, 64 * ff:64 * ff + P],
                                               start=True, stop=True)
                            mm.then_inc(s_out, 1)
                    values(NC * FT - 1)
                    pe.wait_ge(s_osq, i + 1)
                    for k in range(KD):
                        mm = pe.matmul(psum[:, 0, :], mean_w, sq[:, k, :], start=k == 0, stop=k == KD - 1)
                    mm.then_inc(s_ss, 1)
                    pe.wait_ge(s_on, i + 1)
                    for t in range(KD):
                        for k in range(KD):
                            mm = pe.matmul(psum[:, 2 - t, :], a_wos[:, k, t * P:(t + 1) * P], og[:, k, :], start=k == 0, stop=k == KD - 1)
                        mm.then_inc(s_wps, 1)


        k_op = sb("k_op", [P, H, KEYS], BF16)
        v_pad = sb("v_pad", [P, KT, H, 32])
        x_wo = sb("x_wo", [P, H // 4, D])
        x_wq = sb("x_wq", [P, KD, D])
        x_bq = sb("x_bq", [P, KD])
        x_bo = sb("x_bo", [P, KD])
        head_of = const[:, 5, 0:KD * H].rearrange("p (k h) -> p k h", k=KD)
        k_len = sb("k_len", [H, 1])
        k_dram = nc.dram_tensor("k_parts", (3, D, KEYP), BF16, kind="Internal").ap()
        q_dram = nc.dram_tensor("q_parts", (3, D, N), BF16, kind="Internal").ap()
        m_dram = nc.dram_tensor("shifts", (NB, H, BLK), BF16, kind="Internal").ap()
        Q_PART, K_PART = (0, 0, 1, 1, 0, 2), (0, 1, 0, 1, 2, 0)
        NPR = len(Q_PART)
        SHIFT = NPR * HD
        assert SHIFT == 96

        with ExitStack() as st, nc.Block() as block:
            ctx_t = st.enter_context(nc.sbuf_tensor("ctx_t", [P, KD, KEYP], F32))
            x_wk = st.enter_context(nc.sbuf_tensor("x_wk", [P, KD, D], F32))
            x_wv = st.enter_context(nc.sbuf_tensor("x_wv", [P, KD, D], F32))
            x_bk = st.enter_context(nc.sbuf_tensor("x_bk", [P, KD], F32))
            x_bv = st.enter_context(nc.sbuf_tensor("x_bv", [P, D], F32))
            kk = st.enter_context(nc.sbuf_tensor("kk", [P, KD, KPART], F32))
            k_sq = st.enter_context(nc.sbuf_tensor("k_sq", [P, KD, KPART], F32))
            k_len4 = st.enter_context(nc.sbuf_tensor("k_len4", [H, 4], F32))
            kp = st.enter_context(nc.sbuf_tensor("kp", [P, 3, KD, KPART], BF16))
            kps, kk_in, kp0, kr0, kp1, kp2, k_out, k_row, vps, v_in, v_set, k_sqd, k_lps, k_lmax = (sem("k_" + n) for n in (
                "kps", "kk_in", "kp0", "kr0", "kp1", "kp2", "out", "row", "vps", "v_in", "v_set", "sqd", "lps", "lmax"))

            @block.sync
            def _(sp):
                for dst, name in ((ctx_t, "ctx_t"), (x_wk, "x_wk"), (x_bk, "x_bk"), (x_wv, "x_wv")):
                    sp.dma_start(dst[:], d[name]).then_inc(ld_ctx, 16)
                sp.dma_start(x_bv[:], d["x_bv"].partition_broadcast(P)).then_inc(ld_ctx, 16)
                for dst, name in ((x_wo, "x_wo"), (x_wq, "x_wq"), (x_bq, "x_bq"), (x_bo, "x_bo")):
                    sp.dma_start(dst[:], d[name]).then_inc(ld_xw, 16)
                with sp.Fori(0, 4) as i:
                    sp.wait_ge(kp2, i + 1)
                    sp.wait_ge(kp1, i + 1)
                    for n in range(3):
                        sp.dma_start(k_dram[n].rearrange("(t p) n -> p t n", p=P)[:, :, bass.ds(i * KPART, KPART)],
                                     kp[:, n]).then_inc(k_out, 16)
                sp.wait_ge(k_out, 16 * 12)
                for r, n in enumerate(K_PART):
                    sp.dma_start(k_op[r * HD:(r + 1) * HD], k_dram[n].rearrange("(h j) n -> j h n", j=HD)[:, :, 0:KEYS]).then_inc(k_row, 16)

            @block.gpsimd
            def _(pool):
                pool.memset(k_op[SHIFT:SHIFT + 1], -1.0).then_inc(v_set, 1)
                pool.wait_ge(v_set, 1)
                pool.memset(v_pad[:], 0.0).then_inc(v_set, 1)
                pool.wait_ge(v_set, 2)
                pool.memset(v_pad[:, :, :, HD:HD + 1], 1.0).then_inc(v_set, 1)

            @block.scalar
            def _(act):
                act.wait_ge(ld_ctx, 16 * 5)
                with act.Fori(0, 4) as i:
                    for t in range(KD):
                        act.wait_ge(kps, KD * i + t + 1)
                        if t == 0:
                            act.wait_ge(kp2, i)
                        act.activation(kk[:, t, :], psum[:, t, 0:KPART], ACT.Identity, bias=x_bk[:, t:t + 1]).then_inc(kk_in, 1)
                    act.wait_ge(k_lps, i)
                    act.activation(k_sq[:, 0, :], psum[:, 0, 0:KPART], ACT.Square, bias=x_bk[:, 0:1]).then_inc(k_sqd, 1)
                    act.activation(k_sq[:, 1, :], psum[:, 1, 0:KPART], ACT.Square, bias=x_bk[:, 1:2]).then_inc(k_sqd, 1)

            @block.vector
            def _(dve):
                dve.wait_ge(ld_ctx, 16 * 5)
                dve.wait_ge(v_set, 3)
                for kt in range(KT):
                    rows = min(P, KEYS - kt * P)
                    dve.wait_ge(vps, kt + 1)
                    dve.tensor_tensor(v_pad[0:rows, kt, :, 0:HD], psum[0:rows, 4 + kt % 2, 0:D].rearrange("p (h d) -> p h d", h=H),
                                      x_bv[0:rows].rearrange("p (h d) -> p h d", h=H), ALU.add).then_inc(v_in, 1)
                with dve.Fori(0, 4) as i:
                    dve.wait_ge(kk_in, KD * i + KD)
                    dve.wait_ge(k_out, 48 * i)
                    dve.tensor_copy(kp[:, 0], kk[:]).then_inc(kp0, 1)
                    dve.wait_ge(kp0, i + 1)
                    dve.tensor_tensor(kk[:], kk[:], kp[:, 0], ALU.subtract).then_inc(kr0, 1)
                    dve.wait_ge(kr0, i + 1)
                    dve.tensor_copy(kp[:, 1], kk[:]).then_inc(kp1, 1)
                    dve.wait_ge(kp1, i + 1)
                    dve.tensor_tensor(kp[:, 2], kk[:], kp[:, 1], ALU.subtract).then_inc(kp2, 1)
                    dve.wait_ge(k_lps, i + 1)
                    dve.tensor_reduce(k_len4[:, bass.ds(i, 1)], psum[0:H, 2, 0:KPART], AX_X, ALU.max).then_inc(k_lmax, 1)
                dve.wait_ge(k_lmax, 4)
                dve.tensor_reduce(k_len[:], k_len4[:], AX_X, ALU.max).then_inc(k_lmax, 1)

            @block.tensor
            def _(pe):
                pe.wait_ge(ld_ctx, 16 * 5)
                for kt in range(KT):
                    rows = min(P, KEYS - kt * P)
                    if kt >= 2:
                        pe.wait_ge(v_in, kt - 1)
                    for k in range(KD):
                        mm = pe.matmul(psum[0:rows, 4 + kt % 2, 0:D], ctx_t[:, k, kt * P:kt * P + rows], x_wv[:, k, :],
                                       start=k == 0, stop=k == KD - 1)
                    mm.then_inc(vps, 1)
                with pe.Fori(0, 4) as i:
                    for t in range(KD):
                        pe.wait_ge(k_sqd, 2 * i)
                        for k in range(KD):
                            mm = pe.matmul(psum[:, t, 0:KPART], x_wk[:, k, t * P:(t + 1) * P], ctx_t[:, k, bass.ds(i * KPART, KPART)],
                                           start=k == 0, stop=k == KD - 1)
                        mm.then_inc(kps, 1)
                    pe.wait_ge(k_sqd, 2 * i + 2)
                    pe.wait_ge(k_lmax, i)
                    for k in range(KD):
                        mm = pe.matmul(psum[0:H, 2, 0:KPART], head_of[:, k, :], k_sq[:, k, :], start=k == 0, stop=k == KD - 1)
                    mm.then_inc(k_lps, 1)

        MAX_BOUND = 40.0
        exact = sb("exact", [1, 1], I32)
        with ExitStack() as st, nc.Block() as block:
            def sbq(name, shape, dt=F32):
                return st.enter_context(nc.sbuf_tensor(name, shape, dt))

            qq = sbq("qq", [P, KD, BLK])
            q_sq = sbq("q_sq", [P, KD, BLK])
            qp = sbq("qp", [P, 2, 3, KD, BLK], BF16)
            bound2 = sbq("bound2", [H, BLK])
            lnb = sbq("lnb", [H, BLK])
            shift = sbq("shift", [H, 2, BLK], BF16)
            b_max = sbq("b_max", [H, NB])
            b_all = sbq("b_all", [H, 1])
            b_low = sbq("b_low", [H, 1])
            s_mean, s_cent, s_sq, s_var, s_lnv, s_rstd, s_xn = (sem("q_" + n) for n in ("mean", "cent", "sq", "var", "lnv", "rstd", "xn"))
            s_qps, s_qq, s_qp0, s_qr0, s_qp1, s_qp2 = (sem("q_" + n) for n in ("qps", "qq", "qp0", "qr0", "qp1", "qp2"))
            s_qsq, s_len, s_b2, s_lnb, s_shift, s_bmax, s_few, s_flag = (sem("q_" + n) for n in ("qsq", "len", "b2", "lnb", "shift", "bmax", "few", "flag"))
            s_qout = (sem("q_qout_0"), sem("q_qout_1"))

            @block.sync
            def _(sp):
                with sp.Fori(0, NB // 2) as h:
                    for a in range(2):
                        i = 2 * h + a
                        now = bass.ds(i * BLK, BLK)
                        sp.wait_ge(s_shift, i + 1)
                        sp.dma_start(m_dram[bass.ds(i, 1)].rearrange("o h n -> (o h) n"), shift[:, a]).then_inc(s_qout[a], 16)
                        sp.wait_ge(s_qp1, i + 1)
                        sp.wait_ge(s_qp2, i + 1)
                        for n in range(3):
                            sp.dma_start(q_dram[n].rearrange("(t p) n -> p t n", p=P)[:, :, now], qp[:, a, n]).then_inc(s_qout[a], 16)
                for a in range(2):
                    sp.wait_ge(s_qout[a], 64 * NB // 2)

            @block.scalar
            def _(act):
                with act.Fori(0, NB // 2) as h:
                    for a in range(2):
                        i = 2 * h + a
                        act.wait_ge(s_cent, i + 1)
                        act.activation(sq[:], cent[:], ACT.Square).then_inc(s_sq, 1)
                        act.wait_ge(s_var, i + 1)
                        act.activation(lnv[:], psum[:, 0, :], ACT.Ln, bias=eps_ln[:, 0:1]).then_inc(s_lnv, 1)
                        act.wait_ge(s_lnv, i + 1)
                        act.activation(rstd[:], lnv[:], ACT.Exp, scale=-0.5).then_inc(s_rstd, 1)
                        act.wait_ge(s_qq, KD * i + KD)
                        act.activation(q_sq[:], qq[:], ACT.Square).then_inc(s_qsq, 1)
                        act.wait_ge(s_b2, i + 1)
                        act.activation(lnb[:], bound2[:], ACT.Ln).then_inc(s_lnb, 1)
                        act.wait_ge(s_lnb, i + 1)
                        act.wait_ge(s_qout[a], 64 * h)
                        act.activation(shift[:, a], lnb[:], ACT.Exp, scale=0.5).then_inc(s_shift, 1)

            @block.vector
            def _(dve):
                dve.wait_ge(ld_xw, 16 * 4)
                with dve.Fori(0, NB // 2) as h2:
                    for a in range(2):
                        i = 2 * h2 + a
                        dve.wait_ge(s_mean, i + 1)
                        dve.tensor_tensor(cent[:], x_t[:, :, bass.ds(i * BLK, BLK)], psum[:, 0:1, :].to_broadcast([P, KD, BLK]),
                                          ALU.subtract).then_inc(s_cent, 1)
                        dve.wait_ge(s_rstd, i + 1)
                        dve.wait_ge(s_cent, i + 1)
                        dve.tensor_tensor(xn[:], cent[:], rstd[:].unsqueeze(1).to_broadcast([P, KD, BLK]), ALU.mult).then_inc(s_xn, 1)
                        for t in range(KD):
                            dve.wait_ge(s_qps, KD * i + t + 1)
                            dve.tensor_scalar(qq[:, t, :], psum[:, 1 + t, :], x_bq[:, t:t + 1], float(HD) ** -0.5, ALU.add,
                                              ALU.mult).then_inc(s_qq, 1)
                        dve.wait_ge(s_qq, KD * i + KD)
                        dve.wait_ge(s_qout[a], 64 * h2)
                        dve.tensor_copy(qp[:, a, 0], qq[:]).then_inc(s_qp0, 1)
                        dve.wait_ge(s_len, i + 1)
                        dve.tensor_scalar(bound2[:], psum[0:H, 3, :], k_len[:, 0:1], 1e-12, ALU.mult, ALU.add).then_inc(s_b2, 1)
                        dve.wait_ge(s_qp0, i + 1)
                        dve.wait_ge(s_qsq, i + 1)
                        dve.tensor_tensor(qq[:], qq[:], qp[:, a, 0], ALU.subtract).then_inc(s_qr0, 1)
                        dve.wait_ge(s_b2, i + 1)
                        dve.tensor_reduce(b_max[:, bass.ds(i, 1)], bound2[:], AX_X, ALU.max).then_inc(s_bmax, 1)
                        dve.wait_ge(s_qr0, i + 1)
                        dve.tensor_copy(qp[:, a, 1], qq[:]).then_inc(s_qp1, 1)
                        dve.wait_ge(s_qp1, i + 1)
                        dve.tensor_tensor(qp[:, a, 2], qq[:], qp[:, a, 1], ALU.subtract).then_inc(s_qp2, 1)
                        dve.wait_ge(s_lnb, i + 1)
                dve.wait_ge(s_bmax, NB)
                dve.tensor_reduce(b_all[:], b_max[:], AX_X, ALU.max).then_inc(s_bmax, 1)
                dve.wait_ge(s_bmax, NB + 1)
                dve.tensor_scalar(b_low[:], b_all[:], MAX_BOUND ** 2, None, ALU.is_le).then_inc(s_bmax, 1)
                dve.wait_ge(s_few, 1)
                dve.tensor_scalar(exact[:], psum[0:1, 0, 0:1], float(H) - 0.5, None, ALU.is_lt).then_inc(s_flag, 1)
                dve.wait_ge(s_flag, 1)

            @block.tensor
            def _(pe):
                pe.wait_ge(ld_xw, 16 * 4)
                with pe.Fori(0, NB) as i:
                    for k in range(KD):
                        mm = pe.matmul(psum[:, 0, :], mean_w, x_t[:, k, bass.ds(i * BLK, BLK)], start=k == 0, stop=k == KD - 1)
                    mm.then_inc(s_mean, 1)
                    pe.wait_ge(s_sq, i + 1)
                    for k in range(KD):
                        mm = pe.matmul(psum[:, 0, :], mean_w, sq[:, k, :], start=k == 0, stop=k == KD - 1)
                    mm.then_inc(s_var, 1)
                    pe.wait_ge(s_xn, i + 1)
                    pe.wait_ge(s_qq, KD * i)
                    for t in range(KD):
                        for k in range(KD):
                            mm = pe.matmul(psum[:, 1 + t, :], x_wq[:, k, t * P:(t + 1) * P], xn[:, k, :], start=k == 0, stop=k == KD - 1)
                        mm.then_inc(s_qps, 1)
                    pe.wait_ge(s_qsq, i + 1)
                    pe.wait_ge(s_b2, i)
                    for k in range(KD):
                        mm = pe.matmul(psum[0:H, 3, :], head_of[:, k, :], q_sq[:, k, :], start=k == 0, stop=k == KD - 1)
                    mm.then_inc(s_len, 1)
                pe.wait_ge(s_bmax, NB + 2)
                pe.matmul(psum[0:1, 0, 0:1], b_low[:], ones[0:H, 0:1], start=True, stop=True).then_inc(s_few, 1)

        with ExitStack() as st, nc.Block() as block:
            q_all = st.enter_context(nc.sbuf_tensor("q_all", [P, H, BLK], BF16))
            mx = st.enter_context(nc.sbuf_tensor("mx", [P, NC, H], F32))
            mx_t = st.enter_context(nc.sbuf_tensor("mx_t", [H, BLK], BF16))
            x_q, x_ms, x_mx, x_mt, x_mn, x_out = (sem("x_" + n) for n in ("q", "ms", "mx", "mt", "mn", "out"))

            @block.sync
            def _(sp):
                with sp.If(sp.value_load(exact[0:1, 0:1], min_val=0, max_val=1)):
                    with sp.Fori(0, NB) as i:
                        sp.wait_ge(x_ms, H * NC * i)
                        for r, n in enumerate(Q_PART):
                            sp.dma_start(q_all[r * HD:(r + 1) * HD], q_dram[n].rearrange("(h j) n -> j h n", j=HD)[:, :, bass.ds(i * BLK, BLK)]).then_inc(x_q, 16)
                        sp.wait_ge(x_mn, i + 1)
                        sp.dma_start(m_dram[bass.ds(i, 1)].rearrange("o h n -> (o h) n"), mx_t[:]).then_inc(x_out, 16)
                    sp.wait_ge(x_out, 16 * NB)

            @block.scalar
            def _(act):
                with act.If(act.value_load(exact[0:1, 0:1], min_val=0, max_val=1)):
                    with act.Fori(0, NB) as i:
                        act.wait_ge(x_mt, i + 1)
                        act.wait_ge(x_out, 16 * i)
                        act.activation(mx_t[:], psum[0:H, 7, :], ACT.Copy).then_inc(x_mn, 1)

            @block.vector
            def _(dve):
                with dve.If(dve.value_load(exact[0:1, 0:1], min_val=0, max_val=1)):
                    with dve.Fori(0, NB) as i:
                        turned = dve.to_reg(i)
                        dve.wait_ge(ld_const, 16)
                        dve.wait_ge(x_mt, turned)
                        with dve.Fori(0, H // 2) as h2:
                            for w in range(2 * NC):
                                e, c = divmod(w, NC)
                                dve.wait_ge(x_ms, H * NC * i + 2 * NC * h2 + w + 1)
                                dve.tensor_reduce(mx[:, c, bass.ds(2 * h2 + e, 1)],
                                                  psum[:, 4 * (w % 2):4 * (w % 2) + 4, :].rearrange("p b n -> p (b n)")[:, 0:KEYS],
                                                  AX_X, ALU.max).then_inc(x_mx, 1)

            @block.tensor
            def _(pe):
                with pe.If(pe.value_load(exact[0:1, 0:1], min_val=0, max_val=1)):
                    with pe.Fori(0, NB) as i:
                        copied = pe.to_reg(i)
                        loaded = pe.to_reg(16 * NPR * (i + 1))
                        pe.wait_ge(ld_const, 16)
                        pe.wait_ge(x_mn, copied)
                        pe.wait_ge(x_q, loaded)
                        with pe.Fori(0, H // 2) as h2:
                            for w in range(2 * NC):
                                e, c = divmod(w, NC)
                                pe.wait_ge(x_mx, H * NC * i + 2 * NC * h2 + max(w - 1, 0))
                                h = bass.ds(2 * h2 + e, 1)
                                for b in range(4):
                                    cols = min(BLK, KEYS - b * BLK)
                                    mm = pe.matmul(psum[:, 4 * (w % 2) + b, 0:cols], q_all[0:SHIFT, h, c * CH:(c + 1) * CH].rearrange("p o n -> p (o n)"),
                                                   k_op[0:SHIFT, h, b * BLK:b * BLK + cols].rearrange("p o n -> p (o n)"), start=True, stop=True)
                                mm.then_inc(x_ms, 1)
                        pe.wait_ge(x_mx, H * NC * (i + 1))
                        for c in range(NC):
                            mm = pe.transpose(psum[0:H, 7, c * CH:(c + 1) * CH], mx[:, c, :], ident)
                        mm.then_inc(x_mt, 1)

        with ExitStack() as st:
            def sbb(name, shape, dt=F32):
                return st.enter_context(nc.sbuf_tensor(name, shape, dt))

            q_op = sbb("q_op", [P, H, BLK], BF16)
            pr = sbb("pr", [P, 3, 4, BLK])
            osb = sbb("osb", [P, 2, BLK])
            rden = sbb("rden", [P, BLK])
            on = sbb("on", [P, 4, BLK])
            GR = KT * 4
            s_sc, s_ex, s_pv, s_os, s_dn, s_rd, s_on, s_wps, s_x2 = (sem("b_" + n) for n in ("sc", "ex", "pv", "os", "dn", "rd", "on", "wps", "x2"))
            s_qop = [sem("b_qop_%d" % g) for g in range(4)]

            nc.clear_and_free_semaphores(a_sems)
            block = st.enter_context(nc.Block())

            @block.sync
            def _(sp):
                def load_queries(i, g):
                    heads = slice(4 * g, 4 * g + 4)
                    for r, n in enumerate(Q_PART):
                        sp.dma_start(q_op[r * HD:(r + 1) * HD, heads],
                                     q_dram[n].rearrange("(h j) n -> j h n", j=HD)[:, heads, bass.ds(i * BLK, BLK)]).then_inc(s_qop[g], 16)
                    sp.dma_start(q_op[SHIFT:SHIFT + 1, heads], m_dram[bass.ds(i, 1), heads]).then_inc(s_qop[g], 16)

                for g in range(4):
                    load_queries(0, g)
                with sp.Fori(0, NB - 1) as i:
                    for g in range(4):
                        sp.wait_ge(s_sc, 2 * GR * i + 2 * KT * (g + 1))
                        load_queries(i + 1, g)

            @block.scalar
            def _(act):
                with act.Fori(0, NB) as i:
                    for n in range(GR):
                        for e in range(2):
                            p = 2 * n + e
                            act.wait_ge(s_sc, 2 * GR * i + p + 1)
                            if n >= 3:
                                act.wait_ge(s_pv, GR * i + n - 2)
                            else:
                                act.wait_ge(s_pv, GR * i)
                            rows = min(P, KEYS - (n % KT) * P)
                            b = 2 * (p % 3)
                            act.activation(pr[0:rows, n % 3, 2 * e:2 * e + 2, :], psum[0:rows, b:b + 2, :], ACT.Exp).then_inc(s_ex, 1)

            @block.vector
            def _(dve):
                with dve.Fori(0, NB) as i:
                    now = bass.ds(i * BLK, BLK)
                    for g in range(4):
                        dve.wait_ge(s_pv, GR * i + KT * (g + 1))
                        dve.tensor_copy(osb[:, g % 2, :], psum[:, 6, :]).then_inc(s_os, 1)
                        dve.wait_ge(s_dn, 4 * i + g + 1)
                        dve.reciprocal(rden[:], psum[:, 7, :]).then_inc(s_rd, 1)
                        dve.wait_ge(s_rd, 4 * i + g + 1)
                        dve.wait_ge(s_os, 4 * i + g + 1)
                        dve.tensor_tensor(on[:, g, :], osb[:, g % 2, :], rden[:], ALU.mult).then_inc(s_on, 1)
                    for t in range(KD):
                        dve.wait_ge(s_wps, KD * i + t + 1)
                        dve.scalar_tensor_tensor(out=x_t[:, t, now], in0=psum[:, 7, :], scalar=x_bo[:, t:t + 1],
                                                 in1=x_t[:, t, now], op0=ALU.add, op1=ALU.add).then_inc(s_x2, 1)

            @block.tensor
            def _(pe):
                def scores(i, n):
                    g, kt = divmod(n, KT)
                    rows = min(P, KEYS - kt * P)
                    if kt == 0:
                        pe.wait_ge(s_qop[g], 16 * (NPR + 1) * (i + 1))
                    for e in range(2):
                        p = 2 * n + e
                        pe.wait_ge(s_ex, 2 * GR * i + max(p - 2, 0))
                        for j in range(2):
                            h = 4 * g + 2 * e + j
                            mm = pe.matmul(psum[0:rows, 2 * (p % 3) + j, :], k_op[0:SHIFT + 1, h, kt * P:kt * P + rows],
                                           q_op[0:SHIFT + 1, h, :], start=True, stop=True)
                        mm.then_inc(s_sc, 1)

                def weighted(i, n):
                    g, kt = divmod(n, KT)
                    rows = min(P, KEYS - kt * P)
                    pe.wait_ge(s_ex, 2 * GR * i + 2 * n + 2)
                    if kt == 0:
                        pe.wait_ge(s_os, 4 * i + g)
                    for j in range(4):
                        mm = pe.matmul(psum[32 * j:32 * j + 32, 6, :], v_pad[0:rows, kt, 4 * g + j, :], pr[0:rows, n % 3, j, :],
                                       start=kt == 0, stop=kt == KT - 1)
                    mm.then_inc(s_pv, 1)

                def denominators(i, g):
                    pe.wait_ge(s_os, 4 * i + g + 1)
                    pe.wait_ge(s_rd, 4 * i + g)
                    if g == 0:
                        pe.wait_ge(s_x2, KD * i)
                    pe.matmul(psum[:, 7, :], den_sel, osb[:, g % 2, :], start=True, stop=True).then_inc(s_dn, 1)

                def output(i, t):
                    pe.wait_ge(s_on, 4 * i + 4)
                    pe.wait_ge(s_x2, KD * i + t)
                    for g in range(4):
                        mm = pe.matmul(psum[:, 7, :], x_wo[:, g, t * P:(t + 1) * P], on[:, g, :], start=g == 0, stop=g == 3)
                    mm.then_inc(s_wps, 1)

                def steps(i, first):
                    for n in range(GR):
                        g, kt = divmod(n, KT)
                        scores(i, n)
                        if n > 0:
                            weighted(i, n - 1)
                        elif not first:
                            weighted(i - 1, GR - 1)
                        if kt == 3 and g > 0:
                            denominators(i, g - 1)
                        elif kt == 3 and not first:
                            denominators(i - 1, 3)
                        if n in (7, 10) and not first:
                            output(i - 1, 0 if n == 7 else 1)

                pe.wait_ge(k_row, 16 * NPR)
                steps(0, True)
                with pe.Fori(1, NB) as i:
                    steps(i, False)
                weighted(NB - 1, GR - 1)
                denominators(NB - 1, 3)
                output(NB - 1, 0)
                output(NB - 1, 1)

        slot_rows = nc.dram_tensor("slot_rows", (P * TILES, 2), F32, kind="Internal").ap()
        xn_rows = nc.dram_tensor("xn_rows", (N + P, D), F32, kind="Internal").ap()
        y_rows = nc.dram_tensor("y_rows", (N + P, D), F32, kind="Internal").ap()
        e_tile = sb("e_tile", [P, TILES])
        e_int = sb("e_int", [P, TILES], I32)
        with ExitStack() as st, nc.Block() as block:
            def sbr(name, shape, dt=F32):
                return st.enter_context(nc.sbuf_tensor(name, shape, dt))

            def semr(name):
                return sem("r_" + name)

            rconst = sbr("rconst", [P, TT * EXP + TILES + TT + 1])
            seg = rconst[:, 0:TT * EXP]
            tile_no = rconst[:, TT * EXP:TT * EXP + TILES]
            tok_no = rconst[:, TT * EXP + TILES:]
            keys = sbr("keys", [P, KD, EXP])
            rw = sbr("rw", [P, KD, EXP])
            rt = sbr("rt", [P, KD, EXP])
            ksq = sbr("ksq", [P, KD, EXP])
            rb = sbr("rb", [P, EXP])
            cst = sbr("cst", [P, EXP])
            neg = sbr("neg", [P, EXP])
            zero = sbr("zero", [P, D])
            pad = sbr("pad", [P, TILES, 2])
            x2b = sbr("x2b", [P, KD, BLK])
            xsq = sbr("xsq", [P, KD, BLK])
            xr = sbr("xr", [P, 2, NC, D])
            x2r = sbr("x2r", [P, 2, NC, D])
            lg = sbr("lg", [P, TT, EXP])
            top = sbr("top", [P, TT, 8])
            tix = sbr("tix", [P, TT, 8], U32)
            tif = sbr("tif", [P, TT, TOPK])
            wx = sbr("wx", [P, TT, TOPK])
            wsum = sbr("wsum", [P, TT])
            oh = sbr("oh", [P, TT, TOPK, EXP])
            pick = sbr("pick", [P, TT, TOPK, EXP])
            chosen = sbr("chosen", [P, EXP, TT])
            upto = sbr("upto", [P, EXP, TT])
            need_i = sbr("need_i", [P, EXP], I32)
            need = sbr("need", [P, EXP])
            ends = sbr("ends", [P, EXP])
            first = sbr("first", [P, EXP])
            pos = sbr("pos", [P, EXP, TT])
            cmp_e = sbr("cmp_e", [P, TILES, EXP])
            slot = sbr("slot", [P, TT, TOPK])
            slot_i = sbr("slot_i", [P, TT, TOPK], I32)
            slot_p = sbr("slot_p", [P, TT, TOPK], I32)
            slot_t = sbr("slot_t", [P, TT, TOPK])
            entry = sbr("entry", [P, TT, TOPK, 2])

            l_r = semr("ld"); s_set = semr("set"); s_pad = semr("pad"); s_pre = semr("pre")
            s_mean = semr("mean"); s_cent = semr("cent"); s_sq = semr("sq"); s_var = semr("var")
            s_lnv = semr("lnv"); s_rstd = semr("rstd"); s_xn = semr("xn"); s_xsq = semr("xsq")
            s_x2b = semr("x2b"); s_cps = semr("cps"); s_cst = semr("cst"); s_lps = semr("lps"); s_lg = semr("lg")
            s_xtp = semr("xtp"); s_xr = semr("xr"); s_x2p = semr("x2p"); s_x2r = semr("x2r")
            s_zout = semr("zout"); s_xout = (semr("xout_0"), semr("xout_1")); s_yout = (semr("yout_0"), semr("yout_1"))
            s_top = semr("top"); s_gap = semr("gap"); s_tif = semr("tif");
            s_chosen = semr("chosen"); s_exp = semr("exp"); s_wsum = semr("wsum"); s_entry = semr("entry")
            s_cnt = semr("cnt"); s_need = semr("need"); s_pos = semr("pos"); s_slot = semr("slot")
            s_etile = semr("etile"); s_scat = semr("scat")

            @block.sync
            def _(sp):
                sp.dma_start(keys[:], d["f_keys"]).then_inc(l_r, 16)
                sp.dma_start(rw[:], d["f_rw"]).then_inc(l_r, 16)
                sp.dma_start(rb[:], d["f_rb"].partition_broadcast(P)).then_inc(l_r, 16)
                sp.dma_start(rconst[:], d["rconst"]).then_inc(l_r, 16)
                sp.wait_ge(s_set, 4)
                sp.dma_start(slot_rows.rearrange("(p t) c -> p t c", p=P), pad[:]).then_inc(s_pad, 16)
                sp.dma_start(xn_rows[N:N + P], zero[:]).then_inc(s_zout, 16)
                sp.dma_start(y_rows[N:N + P], zero[:]).then_inc(s_zout, 16)
                with sp.Fori(0, NB // 2) as i:
                    for a in range(2):
                        b = 2 * i + a
                        sp.wait_ge(s_x2r, 2 * b + 2)
                        sp.dma_start(y_rows[bass.ds(b * BLK, BLK)].rearrange("(t p) c -> p t c", p=P), x2r[:, a]).then_inc(s_yout[a], 16)
                        sp.wait_ge(s_xr, 2 * b + 2)
                        sp.dma_start(xn_rows[bass.ds(b * BLK, BLK)].rearrange("(t p) c -> p t c", p=P), xr[:, a]).then_inc(s_xout[a], 16)
                sp.wait_ge(s_zout, 32)
                for a in range(2):
                    sp.wait_ge(s_xout[a], 16 * NB // 2)
                    sp.wait_ge(s_yout[a], 16 * NB // 2)

            @block.gpsimd
            def _(pool):
                pool.wait_ge(s_pad, 16)
                pool.wait_ge(s_entry, 2)
                pool.wait_ge(s_slot, 8)
                for tt in range(TT):
                    for j in range(TOPK):
                        pool.indirect_dma_start(out=slot_rows, out_offset=bass.IndirectOffsetOnAxis(ap=slot_i[:, tt, j:j + 1].bitcast(U32), axis=0),
                                                in_=entry[:, tt, j, :], in_offset=None).then_inc(s_scat, 16)
                pool.wait_ge(s_scat, 16 * TT * TOPK)

            @block.scalar
            def _(act):
                with act.Fori(0, NB // 2) as h:
                    for a in range(2):
                        i = 2 * h + a
                        act.wait_ge(s_x2p, 2 * i)
                        act.activation(x2b[:], x_t[:, :, bass.ds(i * BLK, BLK)], ACT.Copy).then_inc(s_x2b, 1)
                        act.wait_ge(s_cent, i + 1)
                        act.activation(sq[:], cent[:], ACT.Square).then_inc(s_sq, 1)
                        act.wait_ge(s_var, i + 1)
                        act.activation(lnv[:], psum[:, 0, :], ACT.Ln, bias=eps_ln[:, 0:1]).then_inc(s_lnv, 1)
                        act.wait_ge(s_lnv, i + 1)
                        act.activation(rstd[:], lnv[:], ACT.Exp, scale=-0.5).then_inc(s_rstd, 1)
                        act.wait_ge(s_xn, i + 1)
                        act.activation(xsq[:], xn[:], ACT.Square).then_inc(s_xsq, 1)
                        act.wait_ge(s_xout[a], 16 * h)
                        for u in range(2):
                            act.wait_ge(s_xtp, 2 * i + u + 1)
                            act.activation(xr[:, a, 2 * u:2 * u + 2], psum[:, 2 + u, :].rearrange("p (t n) -> p t n", t=2),
                                           ACT.Copy).then_inc(s_xr, 1)
                act.wait_ge(s_gap, 1)
                act.activation(wx[:], wx[:], ACT.Exp).then_inc(s_exp, 1)

            @block.vector
            def _(dve):
                dve.memset(zero[:], 0.0).then_inc(s_set, 1)
                dve.memset(pad[:, :, 1:2], 0.0).then_inc(s_set, 1)
                dve.memset(neg[:], -1.0).then_inc(s_set, 1)
                dve.wait_ge(l_r, 16 * 4)
                dve.tensor_copy(pad[:, :, 0:1].bitcast(U32), tok_no[:, TT:TT + 1].unsqueeze(1).to_broadcast([P, TILES, 1])).then_inc(s_set, 1)
                dve.tensor_copy(entry[:, :, :, 0:1].bitcast(U32),
                                tok_no[:, 0:TT].unsqueeze(2).unsqueeze(3).to_broadcast([P, TT, TOPK, 1])).then_inc(s_entry, 1)
                dve.tensor_tensor(ksq[:], keys[:], keys[:], ALU.mult).then_inc(s_pre, 1)
                dve.scalar_tensor_tensor(out=rt[:], in0=keys[:], scalar=2.0, in1=rw[:], op0=ALU.mult, op1=ALU.add).then_inc(s_pre, 1)
                dve.wait_ge(s_cps, 1)
                dve.tensor_tensor(cst[:], rb[:], psum[:, 1, 0:EXP], ALU.subtract).then_inc(s_cst, 1)
                dve.wait_ge(s_cst, 1)
                with dve.Fori(0, NB // 2) as h:
                    for a in range(2):
                        i = 2 * h + a
                        dve.wait_ge(s_mean, i + 1)
                        dve.tensor_tensor(cent[:], x_t[:, :, bass.ds(i * BLK, BLK)], psum[:, 0:1, :].to_broadcast([P, KD, BLK]),
                                          ALU.subtract).then_inc(s_cent, 1)
                        dve.wait_ge(s_rstd, i + 1)
                        dve.wait_ge(s_cent, i + 1)
                        dve.tensor_tensor(xn[:], cent[:], rstd[:].unsqueeze(1).to_broadcast([P, KD, BLK]), ALU.mult).then_inc(s_xn, 1)
                        dve.wait_ge(s_yout[a], 16 * h)
                        for u in range(2):
                            dve.wait_ge(s_x2p, 2 * i + u + 1)
                            dve.tensor_copy(x2r[:, a, 2 * u:2 * u + 2], psum[:, 4 + u, :].rearrange("p (t n) -> p t n", t=2)).then_inc(s_x2r, 1)
                        dve.wait_ge(s_lps, i + 1)
                        dve.tensor_tensor(lg[:, bass.ds(NC * i, NC)], psum[:, 1, 0:NC * EXP].rearrange("p (t e) -> p t e", t=NC),
                                          cst[:].unsqueeze(1).to_broadcast([P, NC, EXP]), ALU.add).then_inc(s_lg, 1)
                dve.wait_ge(s_lg, NB)
                for tt in range(TT):
                    dve.max(top[:, tt, :], lg[:, tt, :]).then_inc(s_top, 1)
                dve.wait_ge(s_top, TT)
                for tt in range(TT):
                    dve.max_index(tix[:, tt, :], top[:, tt, :], lg[:, tt, :]).then_inc(s_top, 1)
                dve.tensor_tensor(wx[:], top[:, :, 0:TOPK], top[:, :, 0:1].to_broadcast([P, TT, TOPK]), ALU.subtract).then_inc(s_gap, 1)
                dve.wait_ge(s_top, 2 * TT)
                dve.tensor_copy(tif[:], tix[:, :, 0:TOPK]).then_inc(s_tif, 1)
                dve.wait_ge(s_tif, 1)
                dve.tensor_tensor(oh[:].rearrange("p t j e -> p (t j) e"),
                                  tif[:].rearrange("p t j -> p (t j)").unsqueeze(2).to_broadcast([P, TT * TOPK, EXP]),
                                  expert_no.unsqueeze(1).to_broadcast([P, TT * TOPK, EXP]), ALU.is_equal).then_inc(s_tif, 1)
                dve.wait_ge(s_tif, 2)
                dve.tensor_reduce(chosen[:], oh[:].rearrange("p t j e -> p e t j"), AX_X, ALU.add).then_inc(s_chosen, 1)
                dve.wait_ge(s_exp, 1)
                dve.tensor_reduce(wsum[:], wx[:], AX_X, ALU.add).then_inc(s_wsum, 1)
                dve.wait_ge(s_wsum, 1)
                dve.reciprocal(wsum[:], wsum[:]).then_inc(s_wsum, 1)
                dve.wait_ge(s_wsum, 2)
                dve.tensor_tensor(entry[:, :, :, 1:2].rearrange("p t j o -> p t (j o)"), wx[:], wsum[:].unsqueeze(2).to_broadcast([P, TT, TOPK]),
                                  ALU.mult).then_inc(s_entry, 1)
                dve.wait_ge(s_cnt, 1)
                total = psum[:, 2, 0:EXP * TT].rearrange("p (e t) -> p e t", e=EXP)
                within = psum[:, 3, 0:EXP * TT].rearrange("p (e t) -> p e t", e=EXP)
                dve.tensor_tensor_scan(upto[:].rearrange("p e t -> p (e t)"), seg, psum[:, 2, 0:EXP * TT], 0.0, ALU.mult, ALU.add).then_inc(s_need, 1)
                dve.wait_ge(s_need, 1)
                dve.tensor_scalar(need[:], upto[:, :, TT - 1], float(P - 1), None, ALU.add).then_inc(s_need, 1)
                dve.wait_ge(s_need, 2)
                dve.tensor_copy(need_i[:], need[:]).then_inc(s_need, 1)
                dve.wait_ge(s_need, 3)
                dve.tensor_scalar(need_i[:], need_i[:], 7, None, ALU.arith_shift_right).then_inc(s_need, 1)
                dve.wait_ge(s_need, 4)
                dve.tensor_copy(need[:], need_i[:]).then_inc(s_need, 1)
                dve.wait_ge(s_need, 5)
                dve.tensor_tensor_scan(ends[:], ones[:, 0:EXP], need[:], 0.0, ALU.mult, ALU.add).then_inc(s_need, 1)
                dve.wait_ge(s_need, 6)
                dve.tensor_tensor(first[:], ends[:], need[:], ALU.subtract).then_inc(s_need, 1)
                dve.wait_ge(s_need, 7)
                dve.tensor_scalar(first[:], first[:], float(P), -1.0, ALU.mult, ALU.add).then_inc(s_need, 1)
                dve.tensor_tensor(pos[:], upto[:], total, ALU.subtract).then_inc(s_pos, 1)
                dve.wait_ge(s_pos, 1)
                dve.tensor_tensor(pos[:], pos[:], within, ALU.add).then_inc(s_pos, 1)
                dve.wait_ge(s_pos, 2)
                dve.wait_ge(s_need, 8)
                dve.tensor_tensor(pos[:], pos[:], first[:].unsqueeze(2).to_broadcast([P, EXP, TT]), ALU.add).then_inc(s_pos, 1)
                dve.wait_ge(s_pos, 3)
                for j in range(TOPK):
                    dve.tensor_tensor(pick[:, :, j, :], oh[:, :, j, :], pos[:].rearrange("p e t -> p t e"), ALU.mult).then_inc(s_pos, 1)
                dve.wait_ge(s_pos, 3 + TOPK)
                dve.tensor_reduce(slot[:], pick[:], AX_X, ALU.add).then_inc(s_slot, 1)
                dve.wait_ge(s_slot, 1)
                dve.tensor_copy(slot_i[:], slot[:]).then_inc(s_slot, 1)
                dve.wait_ge(s_slot, 2)
                dve.tensor_scalar(slot_p[:], slot_i[:], 7, None, ALU.arith_shift_right).then_inc(s_slot, 1)
                dve.wait_ge(s_slot, 3)
                dve.tensor_copy(slot_t[:], slot_p[:]).then_inc(s_slot, 1)
                dve.wait_ge(s_slot, 4)
                dve.tensor_scalar(slot_t[:], slot_t[:], float(1 - P * TILES), None, ALU.mult).then_inc(s_slot, 1)
                dve.wait_ge(s_slot, 5)
                dve.tensor_scalar(slot[:], slot[:], float(TILES), None, ALU.mult).then_inc(s_slot, 1)
                dve.wait_ge(s_slot, 6)
                dve.tensor_tensor(slot[:], slot[:], slot_t[:], ALU.add).then_inc(s_slot, 1)
                dve.wait_ge(s_slot, 7)
                dve.tensor_copy(slot_i[:], slot[:]).then_inc(s_slot, 1)
                dve.tensor_tensor(cmp_e[:], tile_no.unsqueeze(2).to_broadcast([P, TILES, EXP]),
                                  ends[:].unsqueeze(1).to_broadcast([P, TILES, EXP]), ALU.is_ge).then_inc(s_etile, 1)
                dve.wait_ge(s_etile, 1)
                dve.tensor_reduce(e_tile[:], cmp_e[:], AX_X, ALU.add).then_inc(s_etile, 1)
                dve.wait_ge(s_etile, 2)
                dve.tensor_scalar(e_tile[:], e_tile[:], float(EXP - 1), None, ALU.min).then_inc(s_etile, 1)
                dve.wait_ge(s_etile, 3)
                dve.tensor_copy(e_int[:], e_tile[:]).then_inc(s_etile, 1)
                dve.wait_ge(s_etile, 4)

            @block.tensor
            def _(pe):
                pe.wait_ge(s_pre, 2)
                pe.wait_ge(s_set, 4)
                for k in range(KD):
                    mm = pe.matmul(psum[:, 1, 0:EXP], ones[:, 0:P], ksq[:, k, :], start=k == 0, stop=k == KD - 1)
                mm.then_inc(s_cps, 1)
                pe.wait_ge(s_cst, 1)
                with pe.Fori(0, NB) as i:
                    for k in range(KD):
                        mm = pe.matmul(psum[:, 0, :], mean_w, x_t[:, k, bass.ds(i * BLK, BLK)], start=k == 0, stop=k == KD - 1)
                    mm.then_inc(s_mean, 1)
                    pe.wait_ge(s_x2b, i + 1)
                    pe.wait_ge(s_x2r, 2 * i)
                    for u in range(2):
                        for c in range(2):
                            for k in range(KD):
                                mm = pe.transpose(psum[:, 4 + u, c * D + k * P:c * D + (k + 1) * P],
                                                  x2b[:, k, (2 * u + c) * P:(2 * u + c + 1) * P], ident)
                        mm.then_inc(s_x2p, 1)
                    pe.wait_ge(s_sq, i + 1)
                    for k in range(KD):
                        mm = pe.matmul(psum[:, 0, :], mean_w, sq[:, k, :], start=k == 0, stop=k == KD - 1)
                    mm.then_inc(s_var, 1)
                    pe.wait_ge(s_xn, i + 1)
                    pe.wait_ge(s_xr, 2 * i)
                    for u in range(2):
                        for c in range(2):
                            for k in range(KD):
                                mm = pe.transpose(psum[:, 2 + u, c * D + k * P:c * D + (k + 1) * P],
                                                  xn[:, k, (2 * u + c) * P:(2 * u + c + 1) * P], ident)
                        mm.then_inc(s_xtp, 1)
                    pe.wait_ge(s_xsq, i + 1)
                    pe.wait_ge(s_lg, i)
                    for c in range(NC):
                        for k in range(KD):
                            pe.matmul(psum[:, 1, c * EXP:(c + 1) * EXP], xn[:, k, c * P:(c + 1) * P], rt[:, k, :], start=k == 0, stop=False)
                        for k in range(KD):
                            mm = pe.matmul(psum[:, 1, c * EXP:(c + 1) * EXP], xsq[:, k, c * P:(c + 1) * P], neg[:], start=False, stop=k == KD - 1)
                    mm.then_inc(s_lps, 1)
                pe.wait_ge(s_chosen, 1)
                pe.wait_ge(s_xr, 2 * NB)
                pe.matmul(psum[:, 2, 0:EXP * TT], ones[:, 0:P], chosen[:].rearrange("p e t -> p (e t)"), start=True, stop=True)
                pe.matmul(psum[:, 3, 0:EXP * TT], causal, chosen[:].rearrange("p e t -> p (e t)"), start=True, stop=True).then_inc(s_cnt, 1)

        with ExitStack() as st, nc.Block() as block:
            def sbe(name, shape, dt=F32):
                return st.enter_context(nc.sbuf_tensor(name, shape, dt))

            def seme(name):
                return sem("e_" + name)

            w1 = sbe("w1", [P, 2, KD * F + FF])
            w2 = sbe("w2", [P, 2, FF, D])
            b2 = sbe("b2", [P, EXP, D])
            slots = sbe("slots", [P, TILES * 2])
            idx = sbe("idx", [P, 4], U32)
            xg = sbe("xg", [P, 4, D])
            xgt = sbe("xgt", [P, 2, KD, P])
            hid = sbe("hid", [P, 2, FF, P])
            yb = sbe("yb", [P, D])
            yt = sbe("yt", [P, 2, D])
            l_slots = seme("slots"); l_b2 = seme("ld_b2")
            l_w1 = [seme("ld_w1_0"), seme("ld_w1_1")]
            l_w2 = [seme("ld_w2_0"), seme("ld_w2_1")]
            l_xg = [seme("ld_xg_%d" % n) for n in range(4)]
            s_idx = seme("idx"); s_xt = seme("xt"); s_xgt = seme("xgt"); s_hp = seme("hp"); s_hid = seme("hid"); s_yp = seme("yp")
            s_yb = seme("yb"); s_y = seme("y"); s_add = seme("add")
            G = 4

            @block.sync
            def _(sp):
                sp.dma_start(slots[:], slot_rows.rearrange("(p t) c -> p (t c)", p=P)).then_inc(l_slots, 16)

                def expert(t):
                    return sp.value_load(e_int[0:1, bass.ds(t, 1)], min_val=0, max_val=EXP - 1)

                def load_w1(e, a):
                    sp.dma_start(w1[:, a], d["f_w1"][bass.ds(e, 1)].rearrange("o p f -> p (o f)")).then_inc(l_w1[a], 16)

                def load_w2(e, a):
                    sp.dma_start(w2[:, a], d["f_w2"][bass.ds(e, 1)].rearrange("o p k f -> p (o k) f")).then_inc(l_w2[a], 16)

                for t in range(2):
                    e = expert(t)
                    load_w1(e, t)
                    load_w2(e, t)
                sp.dma_start(b2[:], d["f_b2"].partition_broadcast(P)).then_inc(l_b2, 16)
                with sp.Fori(0, TILES // 2 - 1) as i:
                    for a in range(2):
                        t = 2 * i + a
                        e = expert(t + 2)
                        sp.wait_ge(s_hid, FF * (t + 1))
                        load_w1(e, a)
                        sp.wait_ge(s_yp, t + 1)
                        load_w2(e, a)
                sp.wait_ge(s_add, 16 * TILES)
                sp.dma_start(d["out"].rearrange("o n c -> (o n) c"), y_rows[0:N]).then_inc(out_done, 16)
                sp.wait_ge(out_done, 16)

            @block.gpsimd
            def _(pool):
                def gather(t, a):
                    pool.tensor_copy(idx[:, a:a + 1], slots[:, bass.ds(2 * t, 1)].bitcast(U32)).then_inc(s_idx, 1)
                    count = pool.to_reg(t + 1)
                    pool.wait_ge(l_slots, 16)
                    pool.wait_ge(s_idx, count)
                    pool.indirect_dma_start(out=xg[:, a], out_offset=None, in_=xn_rows,
                                            in_offset=bass.IndirectOffsetOnAxis(ap=idx[:, a:a + 1], axis=0)).then_inc(l_xg[a], 16)

                def add(t, a):
                    count = pool.to_reg(t + 1)
                    pool.wait_ge(l_slots, 16)
                    pool.wait_ge(s_y, count)
                    pool.indirect_dma_start(out=y_rows, out_offset=bass.IndirectOffsetOnAxis(ap=idx[:, a:a + 1], axis=0),
                                            in_=yt[:, a % 2], in_offset=None, compute_op=ALU.add).then_inc(s_add, 16)

                pool.wait_ge(l_slots, 16)
                for a in range(G - 1):
                    gather(a, a)
                with pool.Fori(0, TILES // G - 1) as i:
                    for a in range(G):
                        t = G * i + a
                        pool.wait_ge(s_add, 16 * t)
                        pool.wait_ge(s_xt, t)
                        gather(t + G - 1, (a + G - 1) % G)
                        add(t, a)
                for t in range(TILES - G, TILES):
                    pool.wait_ge(s_add, 16 * t)
                    if t + G - 1 < TILES:
                        pool.wait_ge(s_xt, t)
                        gather(t + G - 1, (t + G - 1) % G)
                    add(t, t % G)

            @block.scalar
            def _(act):
                with act.Fori(0, TILES // 2) as i:
                    for a in range(2):
                        t = 2 * i + a
                        for b in range(2):
                            act.wait_ge(s_hp, 2 * t + b + 1)
                            for f in range(FF // 2 * b, FF // 2 * (b + 1)):
                                act.activation(hid[:, a, f, :], psum[:, 2 * a + b, (f % 4) * P:(f % 4 + 1) * P], ACT.Gelu,
                                               bias=w1[:, a, KD * F + f:KD * F + f + 1]).then_inc(s_hid, 1)
                        act.wait_ge(s_yp, t)

            @block.vector
            def _(dve):
                def turn(t, a):
                    dve.wait_ge(s_xt, t + 1)
                    dve.tensor_copy(xgt[:, a], psum[:, 6 + a, 0:D].rearrange("p (k t) -> p k t", k=KD)).then_inc(s_xgt, 1)

                def result(t, a):
                    e = dve.value_load(e_int[0:1, bass.ds(t, 1)], min_val=0, max_val=EXP - 1)
                    dve.wait_ge(s_yp, t + 1)
                    dve.wait_ge(s_y, t)
                    dve.tensor_tensor(yb[:], psum[:, 4 + a, 0:D], b2[:, bass.ds(e, 1), :].rearrange("p o n -> p (o n)"), ALU.add).then_inc(s_yb, 1)
                    dve.wait_ge(s_yb, t + 1)
                    dve.tensor_scalar(yt[:, a], yb[:], slots[:, bass.ds(2 * t + 1, 1)], None, ALU.mult).then_inc(s_y, 1)
                    dve.wait_ge(s_add, 16 * t)

                dve.wait_ge(l_slots, 16)
                dve.wait_ge(l_b2, 16)
                turn(0, 0)
                with dve.Fori(0, TILES // 2 - 1) as i:
                    for a in range(2):
                        t = 2 * i + a
                        dve.wait_ge(s_hp, 2 * t)
                        turn(t + 1, 1 - a)
                        result(t, a)
                dve.wait_ge(s_hp, 2 * (TILES - 2))
                turn(TILES - 1, 1)
                result(TILES - 2, 0)
                result(TILES - 1, 1)

            @block.tensor
            def _(pe):
                def hidden(t, a, rnd, s):
                    pe.wait_ge(l_xg[s], 16 * rnd)
                    for k in range(KD):
                        mm = pe.transpose(psum[:, 6 + a, k * P:(k + 1) * P], xg[:, s, k * P:(k + 1) * P], ident)
                    mm.then_inc(s_xt, 1)

                def first(t, a, rnd):
                    pe.wait_ge(s_xgt, t + 1)
                    pe.wait_ge(l_w1[a], 16 * rnd)
                    for b in range(2):
                        for f in range(FF // 2 * b, FF // 2 * (b + 1)):
                            for k in range(KD):
                                mm = pe.matmul(psum[:, 2 * a + b, (f % 4) * P:(f % 4 + 1) * P], w1[:, a, k * F + f * P:k * F + (f + 1) * P],
                                               xgt[:, a, k, :], start=k == 0, stop=k == KD - 1)
                        mm.then_inc(s_hp, 1)

                def second(t, a, rnd):
                    pe.wait_ge(l_w2[a], 16 * rnd)
                    pe.wait_ge(s_hid, FF * (t + 1))
                    for f in range(FF):
                        mm = pe.matmul(psum[:, 4 + a, 0:D], hid[:, a, f, :], w2[:, a, f, :], start=f == 0, stop=f == FF - 1)
                    mm.then_inc(s_yp, 1)
                    pe.wait_ge(s_y, t)

                hidden(0, 0, 1, 0)
                first(0, 0, 1)
                with pe.Fori(0, TILES // G - 1) as i:
                    for a in range(G):
                        t = G * i + a
                        pe.wait_ge(s_xgt, t)
                        hidden(t + 1, (a + 1) % 2, i + 1 + (a + 1) // G, (a + 1) % G)
                        pe.wait_ge(s_hid, FF * t)
                        first(t + 1, (a + 1) % 2, 2 * i + 1 + (a + 1) // 2)
                        second(t, a % 2, 2 * i + 1 + a // 2)
                for t in range(TILES - G, TILES):
                    if t + 1 < TILES:
                        pe.wait_ge(s_xgt, t)
                        hidden(t + 1, (t + 1) % 2, (t + 1) // G + 1, (t + 1) % G)
                        pe.wait_ge(s_hid, FF * t)
                        first(t + 1, (t + 1) % 2, (t + 1) // 2 + 1)
                    second(t, t % 2, t // 2 + 1)


def layouts(i):
    rope, const = constants()

    def rows(w):
        return np.ascontiguousarray(w.reshape(-1, P, w.shape[-1]).transpose(1, 0, 2))

    def doubled(w):
        w = w.reshape(D, H, 1, HD)
        return rows(np.concatenate([w, w], axis=2).reshape(D, 2 * D))

    def column(v):
        return np.ascontiguousarray(v.reshape(-1, P).T)

    def padded(w):
        w = w.reshape(H, HD, w.shape[-1])
        return rows(np.concatenate([w, np.zeros_like(w)], axis=1).reshape(2 * D, w.shape[-1]))

    return {
        "x_t": rows(i["x"][0].T), "const": const, "rope": rope,
        "a_wq": doubled(i["L0_attn_Wq"]), "a_wk": doubled(i["L0_attn_Wk"]), "a_wv": rows(i["L0_attn_Wv"]),
        "a_wo": rows(i["L0_attn_Wo"]), "a_wg1": rows(i["L0_attn_Wg1"]), "a_wg2": np.ascontiguousarray(i["L0_attn_Wg2"]),
        "a_nw": column(i["L0_attn_norm_w"]),
        "ctx_t": rows(np.pad(i["ctx_1024"][0].T, ((0, 0), (0, KEYP - KEYS)))),
        "x_wq": rows(i["L0_xattn_W_q"].T), "x_wk": rows(i["L0_xattn_W_k"].T), "x_wv": rows(i["L0_xattn_W_v"].T),
        "x_wo": padded(i["L0_xattn_W_o"].T), "x_bq": column(i["L0_xattn_b_q"]), "x_bk": column(i["L0_xattn_b_k"]),
        "x_bv": i["L0_xattn_b_v"].reshape(D), "x_bo": column(i["L0_xattn_b_o"]),
        "f_keys": rows(i["L0_ffn_keys"].T), "f_rw": rows(i["L0_ffn_rw"].T), "f_rb": i["L0_ffn_rb"].reshape(EXP),
        "f_b2": np.ascontiguousarray(i["L0_ffn_b2"]), "rconst": routing_constants(),
        "f_w1": np.concatenate([i["L0_ffn_w1"].transpose(0, 2, 1).reshape(EXP, KD, P, F).transpose(0, 2, 1, 3).reshape(EXP, P, KD * F),
                                i["L0_ffn_b1"].reshape(EXP, FF, P).transpose(0, 2, 1)], axis=2),
        "f_w2": np.ascontiguousarray(i["L0_ffn_w2"].transpose(0, 2, 1).reshape(EXP, FF, P, D).transpose(0, 2, 1, 3)),
    }


def kernel(**inputs):
    import numpy as _np
    import concourse.bacc as _bacc
    from concourse import mybir as _mybir
    from concourse.bass_utils import run_bass_kernel_spmd as _run

    laid_out = layouts({name: _np.asarray(a) for name, a in inputs.items()})
    nc = _bacc.Bacc("TRN2", target_bir_lowering=False, num_devices=1)
    arrays, d = {}, {}
    for name, a in laid_out.items():
        arrays[f"in_{name}_dram"] = _np.ascontiguousarray(a)
        d[name] = nc.dram_tensor(f"in_{name}_dram", a.shape, _mybir.dt.from_np(a.dtype), kind="ExternalInput").ap()
    d["out"] = nc.dram_tensor("out_0_dram", (1, N, D), F32, kind="ExternalOutput").ap()
    decoder_layer(nc, d)
    r = _run(nc, [arrays], core_ids=[0])
    return r.results[0]["out_0_dram"]
```

```python
from contextlib import ExitStack

import numpy as np

import concourse.bass as bass
from concourse import mybir

ALU = mybir.AluOpType
ACT = mybir.ActivationFunctionType
F32 = mybir.dt.float32
BF16 = mybir.dt.bfloat16
U32 = mybir.dt.uint32
I32 = mybir.dt.int32
AX_X = mybir.AxisListType.X

P = 128
N = 2048
D = 256
KD = D // P
H = 16
HD = D // H
BLK = 512
NB = N // BLK
CH = 128
NC = BLK // CH
FT = 2 * D // P
HPT = H // FT
KEYS = 1601
KT = -(-KEYS // P)
KEYP = KT * P
KPART = KEYP // 4
EXP = 16
TOPK = 4
F = 1024
FF = F // P
TT = N // P
TILES = N * TOPK // P + EXP
SPAN = EXP * TT + 1
LN_EPS = 1e-05
RMS_EPS = 1e-06


def constants():
    j = np.arange(HD, dtype=np.float32)
    freq = np.power(np.float32(10000.0), (np.float32(-2.0) * j / np.float32(HD)).astype(np.float32)).astype(np.float32)
    theta = (np.arange(N, dtype=np.float32)[:, None] * freq[None]).astype(np.float32)
    both = np.concatenate([np.cos(theta), np.sin(theta)], axis=1).T
    rope = np.ascontiguousarray(np.tile(both, (HPT, 1)).astype(np.float32))
    p = np.arange(P)
    const = np.zeros((P, 6, P), np.float32)
    const[:, 0, :] = 1.0 / D
    const[:, 1, :] = p[:, None] == p[None, :]
    const[:, 2, :] = p[:, None] <= p[None, :]
    const[:, 3, 0:64] = (p[:, None] // 32) == (np.arange(64)[None, :] // HD)
    const[:, 3, 64:64 + EXP] = np.arange(EXP)[None, :]
    const[:, 3, 96:96 + HPT] = (p[:, None] // 32) == np.arange(HPT)[None, :]
    const[:, 4, :] = (p[:, None] % 32 == HD) & (p[:, None] // 32 == p[None, :] // 32)
    for k in range(KD):
        const[:, 5, k * H:(k + 1) * H] = (k * P + p[:, None]) // HD == np.arange(H)[None, :]
    return rope, const


def routing_constants():
    table = np.zeros((P, NC * EXP + EXP + TILES + TT + 1), np.float32)
    table[:, 0:NC * EXP] = np.tile(np.arange(NC) > 0, EXP)[None]
    table[:, NC * EXP:NC * EXP + EXP] = np.arange(EXP)[None] * N - 1
    table[:, NC * EXP + EXP:NC * EXP + EXP + TILES] = np.arange(TILES)[None]
    table[:, NC * EXP + EXP + TILES:] = np.arange(TT + 1)[None] * P + np.arange(P)[:, None]
    return table



def decoder_layer(nc, d):
    with ExitStack() as ctx:
        def sb(name, shape, dt=F32):
            return ctx.enter_context(nc.sbuf_tensor(name, shape, dt))

        def sem(name):
            return ctx.enter_context(nc.semaphore(name))

        psum = ctx.enter_context(nc.psum_tensor("psum", [P, 8, BLK], F32))

        x_t = sb("x_t", [P, KD, N])
        const = sb("const", [P, 6, P])
        mean_w, ident, causal = const[:, 0, :], const[:, 1, :], const[:, 2, :]
        own_state, expert_no, head_rows, den_sel = const[:, 3, 0:64], const[:, 3, 64:64 + EXP], const[:, 3, 96:96 + HPT], const[:, 4, :]

        eps_ln = sb("eps_ln", [P, 1])
        eps_rms = sb("eps_rms", [P, 1])
        ones = sb("ones", [P, BLK])

        cent = sb("cent", [P, KD, BLK])
        sq = sb("sq", [P, KD, BLK])
        lnv = sb("lnv", [P, BLK])
        rstd = sb("rstd", [P, BLK])
        xn = sb("xn", [P, KD, BLK])

        ld_x0, ld_x, ld_const, ld_rope, ld_aw, ld_xw, ld_ctx, out_done = (sem(s) for s in (
            "ld_x0", "ld_x", "ld_const", "ld_rope", "ld_aw", "ld_xw", "ld_ctx", "out_done"))
        set_up = sem("set_up")

        x_wo = sb("x_wo", [P, H // 4, D])
        x_wq = sb("x_wq", [P, KD, D])
        x_bq = sb("x_bq", [P, KD])
        x_bo = sb("x_bo", [P, KD])
        ctx_t = sb("ctx_t", [P, KD, KEYP])
        x_wk = sb("x_wk", [P, KD, D])
        x_wv = sb("x_wv", [P, KD, D])
        x_bk = sb("x_bk", [P, KD])

        a_sems = []
        with ExitStack() as st, nc.Block() as block:
            def sba(name, shape, dt=F32):
                return st.enter_context(nc.sbuf_tensor(name, shape, dt))

            def sema(name):
                a_sems.append(nc.alloc_semaphore(name="a_" + name))
                return a_sems[-1]

            rope = sba("rope", [P, N])
            a_wq = sba("a_wq", [P, KD, 2 * D])
            a_wk = sba("a_wk", [P, KD, 2 * D])
            a_wv = sba("a_wv", [P, KD, D])
            a_wo = sba("a_wo", [P, KD, D])
            a_wg1 = sba("a_wg1", [P, KD, H])
            a_wg2 = sba("a_wg2", [H, D])
            a_nw = sba("a_nw", [P, KD])
            ek = sba("ek", [P, FT, BLK])
            zz = sba("zz", [P, FT, BLK])
            kf = sba("kf", [P, FT, BLK])
            eq = sba("eq", [P, FT, BLK])
            qc = sba("qc", [P, FT, BLK])
            qx = sba("qx", [P, FT, NC, HPT, CH])
            v_pl = sba("v_pl", [P, NC, D + 64])
            v_hd = sba("v_hd", [P, NC, H, 32])
            g1 = sba("g1", [H, BLK])
            gs = sba("gs", [P, KD, BLK])
            kft = sba("kft", [P, 2, FT, P])
            am = sba("am", [P, 2, HPT, CH])
            st8 = sba("st8", [P, 2, FT, 64])
            st_d = sba("st_d", [P, FT, 64])
            og = sba("og", [P, KD, BLK])
            nbm = sba("nbm", [P, FT])
            ngm = sba("ngm", [P, FT])
            dmx = sba("dmx", [P, FT])
            alp = sba("alp", [P, FT])
            z0 = sba("z0", [P, FT])
            a_wos = sba("a_wos", [P, KD, D])

            s_wos = sema("wos")
            s_mean = sema("mean"); s_cent = sema("cent"); s_sq = sema("sq"); s_var = sema("var")
            s_lnv = sema("lnv"); s_rstd = sema("rstd"); s_xn = sema("xn")
            s_kps = sema("kps"); s_nbm = sema("nbm"); s_dmx = sema("dmx"); s_ngm = sema("ngm")
            s_ek = sema("ek"); s_alp = sema("alp"); s_z0 = sema("z0"); s_zz = sema("zz"); s_kf = sema("kf")
            s_qps = sema("qps"); s_eq = sema("eq"); s_qc = sema("qc"); s_rq = sema("rq"); s_lq = sema("lq"); s_rr = sema("rr")
            s_qf = sema("qf"); s_qx = sema("qx"); s_qxl = sema("qxl")
            s_vps = sema("vps"); s_vpl = sema("vpl"); s_vhd = sema("vhd")
            s_h1 = sema("h1"); s_g1 = sema("g1"); s_gps = sema("gps"); s_eg = sema("eg"); s_g2 = sema("g2"); s_gs = sema("gs")
            s_ktp = sema("ktp"); s_kft = sema("kft"); s_aps = sema("aps"); s_am = sema("am")
            s_avr = sema("avr"); s_out = sema("out"); s_std = sema("std"); s_st = sema("st"); s_og = sema("og")
            s_osq = sema("osq"); s_ss = sema("ss"); s_lno = sema("lno"); s_ro = sema("ro"); s_on = sema("on")
            s_wps = sema("wps"); s_x1 = sema("x1")

            @block.sync
            def _(sp):
                sp.dma_start(const[:, :, :], d["const"]).then_inc(ld_const, 16)
                sp.dma_start(x_t[:, :, 0:BLK], d["x_t"][:, :, 0:BLK]).then_inc(ld_x0, 16)
                for dst, name in ((a_wk, "a_wk"), (a_wq, "a_wq"), (a_wv, "a_wv"), (a_wo, "a_wo"), (a_wg1, "a_wg1"),
                                  (a_wg2, "a_wg2"), (a_nw, "a_nw")):
                    sp.dma_start(dst[:], d[name]).then_inc(ld_aw, 16)
                sp.dma_start(rope[:, :], d["rope"]).then_inc(ld_rope, 16)
                sp.dma_start(x_t[:, :, BLK:N], d["x_t"][:, :, BLK:N]).then_inc(ld_x, 16)
                for dst, name in ((ctx_t, "ctx_t"), (x_wk, "x_wk"), (x_bk, "x_bk"), (x_wv, "x_wv")):
                    sp.dma_start(dst[:], d[name]).then_inc(ld_ctx, 16)
                for dst, name in ((x_wo, "x_wo"), (x_wq, "x_wq"), (x_bq, "x_bq"), (x_bo, "x_bo")):
                    sp.dma_start(dst[:], d[name]).then_inc(ld_xw, 16)

            @block.gpsimd
            def _(pool):
                pool.memset(v_hd[:], 0.0).then_inc(set_up, 1)
                pool.wait_ge(ld_const, 16)
                pool.wait_ge(ld_rope, 16)
                with pool.Fori(0, NB) as i:
                    for f in range(FT):
                        count = pool.to_reg(FT * i + f + 1)
                        pool.wait_ge(ld_rope, 16)
                        pool.wait_ge(s_ek, count)
                        if f == 0:
                            pool.wait_ge(s_avr, NC * FT * i)
                        pool.tensor_tensor(kf[:, f, :], ek[:, f, :], rope[:, bass.ds(i * BLK, BLK)], ALU.mult).then_inc(s_kf, 1)
                    for u in range(2):
                        count = pool.to_reg(2 * i + u + 1)
                        pool.wait_ge(ld_const, 16)
                        pool.wait_ge(s_vpl, count)
                        src = v_pl[:, 2 * u:2 * u + 2, 0:D].rearrange("p c (h e d) -> p c h e d", e=2, d=HD)
                        for e in range(2):
                            for c in range(2):
                                dst = v_hd[:, 2 * u + c].rearrange("p (h e) d -> p h e d", e=2)
                                pool.tensor_scalar(dst[:, :, e, HD * e:HD * e + HD], src[:, c, :, e, :], 1.0, 1.0,
                                                   ALU.mult, ALU.mult).then_inc(s_vhd, 1)
                    for f in range(FT - 1):
                        count = pool.to_reg(FT * i + f + 1)
                        pool.wait_ge(ld_const, 16)
                        pool.wait_ge(s_qf, count)
                        for g in range(HPT):
                            pool.tensor_scalar(qx[:, f, :, g, :], qc[:, f, :].rearrange("p (c t) -> p c t", c=NC),
                                               head_rows[:, g:g + 1], 1.0, ALU.mult, ALU.mult).then_inc(s_qx, 1)

            @block.scalar
            def _(act):
                act.preload_act_table_set("natural_log_exp_and_others")
                act.wait_ge(set_up, 6)

                def squares(b):
                    act.wait_ge(s_cent, b + 1)
                    act.activation(sq[:], cent[:], ACT.Square).then_inc(s_sq, 1)

                def deviations(b):
                    act.wait_ge(s_var, b + 1)
                    act.activation(lnv[:], psum[:, 1, :], ACT.Ln, bias=eps_ln[:, 0:1]).then_inc(s_lnv, 1)
                    act.wait_ge(s_lnv, b + 1)
                    act.activation(rstd[:], lnv[:], ACT.Exp, scale=-0.5).then_inc(s_rstd, 1)

                squares(0)
                deviations(0)
                with act.Fori(0, NB) as i:
                    for f in range(FT):
                        act.wait_ge(s_ngm, FT * i + f + 1)
                        if f == 0:
                            act.wait_ge(s_zz, FT * i)
                            act.wait_ge(s_kf, FT * i)
                        act.activation(ek[:, f, :], psum[:, 1 + f % 2, :], ACT.Exp, bias=ngm[:, f:f + 1]).then_inc(s_ek, 1)
                    act.activation(alp[:], dmx[:], ACT.Exp).then_inc(s_alp, 1)
                    for f in range(FT):
                        act.wait_ge(s_qps, FT * i + f + 1)
                        act.activation(eq[:, f, :], psum[:, 1 + f % 2, :], ACT.Exp, scale=-1.0).then_inc(s_eq, 1)
                    for u in range(2):
                        act.wait_ge(s_vps, 2 * i + u + 1)
                        act.activation(v_pl[:, 2 * u:2 * u + 2, 0:D], psum[:, 1 + u, :].rearrange("p (c n) -> p c n", c=2),
                                       ACT.Copy).then_inc(s_vpl, 1)
                    act.wait_ge(s_h1, i + 1)
                    act.activation(g1[:], psum[0:H, 1, :], ACT.Copy).then_inc(s_g1, 1)
                    for t in range(KD):
                        act.wait_ge(s_gps, KD * i + t + 1)
                        if t == 0:
                            act.wait_ge(s_og, NC * i)
                        act.activation(gs[:, t, :], psum[:, 2 - t, :], ACT.Exp, scale=-1.0).then_inc(s_eg, 1)
                    for f in range(FT):
                        n = FT * i + f + 1
                        act.wait_ge(s_rq, n)
                        act.activation(eq[:, f, :], eq[:, f, :], ACT.Ln).then_inc(s_lq, 1)
                        act.wait_ge(s_lq, n)
                        act.activation(eq[:, f, :], eq[:, f, :], ACT.Exp, scale=-1.0).then_inc(s_rr, 1)
                    act.wait_ge(s_eg, KD * i + KD)
                    act.activation(gs[:], gs[:], ACT.Ln, bias=ones[:, 0:1]).then_inc(s_g2, 1)
                    act.wait_ge(s_g2, i + 1)
                    act.activation(gs[:], gs[:], ACT.Exp, scale=-1.0).then_inc(s_gs, 1)
                    squares(i + 1)
                    for c in range(NC):
                        if c == 1:
                            deviations(i + 1)
                        act.wait_ge(s_ktp, NC * i + c + 1)
                        if c < 2:
                            act.wait_ge(s_out, NC * i)
                        else:
                            act.wait_ge(s_out, NC * i + c - 1)
                        act.activation(kft[:, c % 2], psum[:, 7, :].rearrange("p (f t) -> p f t", f=FT),
                                       ACT.Copy).then_inc(s_kft, 1)
                        if c == 0:
                            act.wait_ge(s_qf, FT * i + FT)
                            for g in range(HPT):
                                act.activation(qx[:, FT - 1, :, g, :], qc[:, FT - 1, :].rearrange("p (c t) -> p c t", c=NC),
                                               ACT.Copy, scale=head_rows[:, g:g + 1]).then_inc(s_qxl, 1)
                    act.wait_ge(s_og, NC * i + NC)
                    act.activation(sq[:], og[:], ACT.Square).then_inc(s_osq, 1)
                    act.wait_ge(s_ss, i + 1)
                    act.activation(lnv[:], psum[:, 0, :], ACT.Ln, bias=eps_rms[:, 0:1]).then_inc(s_lno, 1)
                    act.wait_ge(s_lno, i + 1)
                    act.wait_ge(s_xn, i + 2)
                    act.activation(rstd[:], lnv[:], ACT.Exp, scale=-0.5).then_inc(s_ro, 1)

            @block.vector
            def _(dve):
                def centred(b, at):
                    dve.wait_ge(s_mean, b + 1)
                    dve.tensor_tensor(cent[:], x_t[:, :, bass.ds(at * BLK, BLK)], psum[:, 1:2, :].to_broadcast([P, KD, BLK]),
                                      ALU.subtract).then_inc(s_cent, 1)

                def normalised(b):
                    dve.wait_ge(s_rstd, b + 1)
                    dve.wait_ge(s_cent, b + 1)
                    dve.tensor_tensor(xn[:], cent[:], rstd[:].unsqueeze(1).to_broadcast([P, KD, BLK]), ALU.mult).then_inc(s_xn, 1)

                dve.memset(eps_ln[:], LN_EPS).then_inc(set_up, 1)
                dve.memset(eps_rms[:], RMS_EPS).then_inc(set_up, 1)
                dve.memset(ones[:], 1.0).then_inc(set_up, 1)
                dve.memset(ngm[:], 0.0).then_inc(set_up, 1)
                dve.memset(zz[:, :, BLK - 1:BLK], 1.0).then_inc(set_up, 1)
                dve.wait_ge(set_up, 6)
                dve.memset(st8[:], 0.0).then_inc(s_wos, 1)
                dve.memset(v_pl[:, :, D:D + 64], 0.0).then_inc(s_wos, 1)
                dve.wait_ge(ld_const, 16)
                dve.wait_ge(ld_x0, 16)
                centred(0, 0)
                normalised(0)
                dve.wait_ge(ld_aw, 16 * 7)
                for k in range(KD):
                    dve.tensor_scalar(a_wos[:, k, :], a_wo[:, k, :], a_nw[:, k:k + 1], None, ALU.mult).then_inc(s_wos, 1)
                dve.wait_ge(s_wos, 2 + KD)
                dve.wait_ge(ld_rope, 16)
                dve.wait_ge(ld_x, 16)
                dve.wait_ge(ld_const, 16)

                with dve.Fori(0, NB) as i:
                    now = bass.ds(i * BLK, BLK)
                    for f in range(FT):
                        n = FT * i + f + 1
                        dve.wait_ge(s_kps, n)
                        dve.tensor_reduce(nbm[:, f:f + 1], psum[:, 1 + f % 2, :], AX_X, ALU.max, negate=True).then_inc(s_nbm, 1)
                        dve.wait_ge(s_nbm, n)
                        dve.tensor_scalar(dmx[:, f:f + 1], nbm[:, f:f + 1], ngm[:, f:f + 1], 0.0, ALU.subtract,
                                          ALU.min).then_inc(s_dmx, 1)
                        dve.wait_ge(s_dmx, n)
                        dve.tensor_tensor(ngm[:, f:f + 1], nbm[:, f:f + 1], ngm[:, f:f + 1], ALU.min).then_inc(s_ngm, 1)
                    for f in range(FT):
                        dve.wait_ge(s_eq, FT * i + f + 1)
                        if f == 0:
                            dve.wait_ge(s_avr, NC * FT * i)
                            dve.wait_ge(s_qx, (FT - 1) * HPT * i)
                            dve.wait_ge(s_qxl, HPT * i)
                        dve.tensor_tensor(qc[:, f, :], psum[:, 1 + f % 2, :], rope[:, now], ALU.mult).then_inc(s_qc, 1)
                    dve.wait_ge(s_alp, i + 1)
                    dve.wait_ge(s_zz, FT * i)
                    dve.tensor_tensor(z0[:], zz[:, :, BLK - 1], alp[:], ALU.mult).then_inc(s_z0, 1)
                    dve.wait_ge(s_z0, i + 1)
                    for f in range(FT):
                        dve.wait_ge(s_ek, FT * i + f + 1)
                        dve.tensor_tensor_scan(zz[:, f, :], ones[:], ek[:, f, :], z0[:, f:f + 1], ALU.mult, ALU.add).then_inc(s_zz, 1)
                    dve.tensor_tensor(st8[:, 0], st8[:, 0], alp[:].unsqueeze(2).to_broadcast([P, FT, 64]), ALU.mult).then_inc(s_st, 1)
                    for f in range(FT):
                        n = FT * i + f + 1
                        dve.wait_ge(s_eq, n)
                        dve.wait_ge(s_zz, n)
                        dve.scalar_tensor_tensor(out=eq[:, f, :], in0=eq[:, f, :], scalar=1.0, in1=zz[:, f, :],
                                                 op0=ALU.add, op1=ALU.mult).then_inc(s_rq, 1)
                    for f in range(FT):
                        n = FT * i + f + 1
                        dve.wait_ge(s_rr, n)
                        dve.wait_ge(s_qc, n)
                        dve.tensor_tensor(qc[:, f, :], qc[:, f, :], eq[:, f, :], ALU.mult).then_inc(s_qf, 1)
                    centred(i + 1, (i + 1) % NB)
                    for u in range(NC * FT):
                        c, f = divmod(u, FT)
                        if u == FT:
                            dve.wait_ge(s_h1, i + 1)
                            normalised(i + 1)
                        dve.wait_ge(s_aps, NC * FT * i + u + 1)
                        dve.wait_ge(s_avr, NC * FT * i + max(u - 1, 0))
                        dve.tensor_tensor(am[:, u % 2], psum[:, 3 + u % 2, :].rearrange("p (g t) -> p g t", g=HPT),
                                          causal.unsqueeze(1).to_broadcast([P, HPT, CH]), ALU.mult).then_inc(s_am, 1)
                        if f == FT - 1:
                            n = NC * i + c + 1
                            dve.wait_ge(s_out, n)
                            dve.tensor_tensor(st_d[:], psum[:, 0, :].rearrange("p (f n) -> p f n", f=FT)[:, :, 0:64],
                                              own_state.unsqueeze(1).to_broadcast([P, FT, 64]), ALU.mult).then_inc(s_std, 1)
                            dve.wait_ge(s_std, n)
                            dve.wait_ge(s_st, (NC + 1) * i + c + 1)
                            dve.tensor_tensor(st8[:, (c + 1) % 2], st8[:, c % 2], st_d[:], ALU.add).then_inc(s_st, 1)
                            dve.wait_ge(s_avr, NC * FT * i + FT * (c + 1))
                            dve.wait_ge(s_gs, i + 1)
                            if c == 0:
                                dve.wait_ge(s_osq, i)
                            dve.tensor_tensor(og[:, :, c * CH:(c + 1) * CH],
                                              psum[:, 5 + c % 2, 0:KD * CH].rearrange("p (k t) -> p k t", k=KD),
                                              gs[:, :, c * CH:(c + 1) * CH], ALU.mult).then_inc(s_og, 1)
                    dve.wait_ge(s_ro, i + 1)
                    dve.wait_ge(s_og, NC * i + NC)
                    dve.tensor_tensor(og[:], og[:], rstd[:].unsqueeze(1).to_broadcast([P, KD, BLK]), ALU.mult).then_inc(s_on, 1)
                    for t in range(KD):
                        dve.wait_ge(s_wps, KD * i + t + 1)
                        dve.tensor_tensor(x_t[:, t, now], psum[:, 2 - t, :], x_t[:, t, now], ALU.add).then_inc(s_x1, 1)

            @block.tensor
            def _(pe):
                pe.wait_ge(ld_const, 16)
                pe.wait_ge(ld_x0, 16)

                def mean(at):
                    for k in range(KD):
                        mm = pe.matmul(psum[:, 1, :], mean_w, x_t[:, k, bass.ds(at * BLK, BLK)], start=k == 0, stop=k == KD - 1)
                    mm.then_inc(s_mean, 1)

                def variance(b):
                    pe.wait_ge(s_sq, b + 1)
                    for k in range(KD):
                        mm = pe.matmul(psum[:, 1, :], mean_w, sq[:, k, :], start=k == 0, stop=k == KD - 1)
                    mm.then_inc(s_var, 1)

                mean(0)
                variance(0)
                pe.wait_ge(ld_x, 16)
                pe.wait_ge(ld_aw, 16 * 7)
                pe.wait_ge(s_wos, 2 + KD)
                pe.wait_ge(set_up, 6)
                with pe.Fori(0, NB) as i:
                    pe.wait_ge(s_x1, KD * i)
                    pe.wait_ge(s_xn, i + 1)
                    for f in range(FT):
                        if f >= 2:
                            pe.wait_ge(s_ek, FT * i + f - 1)
                        for k in range(KD):
                            mm = pe.matmul(psum[:, 1 + f % 2, :], a_wk[:, k, f * P:(f + 1) * P], xn[:, k, :], start=k == 0, stop=k == KD - 1)
                        mm.then_inc(s_kps, 1)
                    for f in range(FT):
                        if f < 2:
                            pe.wait_ge(s_ek, FT * i + f + 3)
                        else:
                            pe.wait_ge(s_eq, FT * i + f - 1)
                            pe.wait_ge(s_qc, FT * i + f - 1)
                        for k in range(KD):
                            mm = pe.matmul(psum[:, 1 + f % 2, :], a_wq[:, k, f * P:(f + 1) * P], xn[:, k, :], start=k == 0, stop=k == KD - 1)
                        mm.then_inc(s_qps, 1)
                    for u in range(2):
                        pe.wait_ge(s_eq, FT * i + 3 + u)
                        pe.wait_ge(s_qc, FT * i + 3 + u)
                        for c in range(2):
                            for k in range(KD):
                                mm = pe.matmul(psum[:, 1 + u, c * D:(c + 1) * D], xn[:, k, (2 * u + c) * CH:(2 * u + c + 1) * CH],
                                               a_wv[:, k, :], start=k == 0, stop=k == KD - 1)
                        mm.then_inc(s_vps, 1)
                    pe.wait_ge(s_vpl, 2 * i + 1)
                    for k in range(KD):
                        mm = pe.matmul(psum[0:H, 1, :], a_wg1[:, k, :], xn[:, k, :], start=k == 0, stop=k == KD - 1)
                    mm.then_inc(s_h1, 1)
                    pe.wait_ge(s_vpl, 2 * i + 2)
                    pe.wait_ge(s_g1, i + 1)
                    for t in range(KD):
                        pe.matmul(psum[:, 2 - t, :], a_wg2[:, t * P:(t + 1) * P], g1[:], start=True, stop=True).then_inc(s_gps, 1)

                    pe.wait_ge(s_eg, KD * i + KD)
                    mean((i + 1) % NB)

                    def values(u):
                        c, f = divmod(u, FT)
                        o = 5 + c % 2
                        if f == 0:
                            pe.wait_ge(s_st, (NC + 1) * i + c + 1)
                            if c >= 2:
                                pe.wait_ge(s_og, NC * i + c - 1)
                            else:
                                pe.wait_ge(s_og, NC * i)
                            pe.wait_ge(s_qf, FT * i + FT)
                            for ff in range(FT):
                                at = 64 * (ff % 2)
                                pe.matmul(psum[at:at + 64, o, (ff // 2) * CH:(ff // 2 + 1) * CH], st8[:, c % 2, ff, :],
                                          qc[:, ff, c * CH:(c + 1) * CH], start=ff < 2, stop=False, skip_group_check=True)
                            pe.wait_ge(s_vhd, 8 * i + 4 * (c // 2) + 4)
                        pe.wait_ge(s_am, NC * FT * i + u + 1)
                        for g in range(HPT):
                            h = HPT * f + g
                            at = 32 * (h // 2 % 4)
                            mm = pe.matmul(psum[at:at + 32, o, (h // 8) * CH:(h // 8 + 1) * CH], v_hd[:, c, h, :], am[:, u % 2, g, :],
                                           start=False, stop=f == FT - 1, skip_group_check=True)
                        mm.then_inc(s_avr, 1)

                    for u in range(NC * FT):
                        c, f = divmod(u, FT)
                        if f == 0:
                            pe.wait_ge(s_kf, FT * i + FT)
                            pe.wait_ge(s_kft, NC * i + c)
                            for ff in range(FT):
                                mm = pe.transpose(psum[:, 7, ff * P:(ff + 1) * P], kf[:, ff, c * CH:(c + 1) * CH], ident)
                            mm.then_inc(s_ktp, 1)
                        if c == 0:
                            if f < FT - 1:
                                pe.wait_ge(s_qx, (FT - 1) * HPT * i + HPT * (f + 1))
                            else:
                                pe.wait_ge(s_qxl, HPT * (i + 1))
                        pe.wait_ge(s_am, NC * FT * i + max(u - 1, 0))
                        pe.matmul(psum[:, 3 + u % 2, :], kf[:, f, c * CH:(c + 1) * CH],
                                  qx[:, f, c].rearrange("p g t -> p (g t)"), start=True, stop=True).then_inc(s_aps, 1)
                        if u > 0:
                            values(u - 1)
                        if u == 1:
                            variance(i + 1)
                        if f == 2:
                            pe.wait_ge(s_kft, NC * i + c + 1)
                            pe.wait_ge(s_st, (NC + 1) * i + c + 1)
                            for ff in range(FT):
                                mm = pe.matmul(psum[:, 0, ff * P:(ff + 1) * P], kft[:, c % 2, ff, :], v_pl[:, c, 64 * ff:64 * ff + P],
                                               start=True, stop=True)
                            mm.then_inc(s_out, 1)
                    values(NC * FT - 1)
                    pe.wait_ge(s_osq, i + 1)
                    for k in range(KD):
                        mm = pe.matmul(psum[:, 0, :], mean_w, sq[:, k, :], start=k == 0, stop=k == KD - 1)
                    mm.then_inc(s_ss, 1)
                    pe.wait_ge(s_on, i + 1)
                    for t in range(KD):
                        for k in range(KD):
                            mm = pe.matmul(psum[:, 2 - t, :], a_wos[:, k, t * P:(t + 1) * P], og[:, k, :], start=k == 0, stop=k == KD - 1)
                        mm.then_inc(s_wps, 1)


        k_op = sb("k_op", [P, H, KEYS], BF16)
        v_pad = sb("v_pad", [P, KT, H, 32])
        head_of = const[:, 5, 0:KD * H].rearrange("p (k h) -> p k h", k=KD)
        k_len = sb("k_len", [H, 1])
        k_dram = nc.dram_tensor("k_parts", (3, D, KEYP), BF16, kind="Internal").ap()
        q_dram = nc.dram_tensor("q_parts", (3, D, N), BF16, kind="Internal").ap()
        m_dram = nc.dram_tensor("shifts", (NB, H, BLK), BF16, kind="Internal").ap()
        Q_PART, K_PART = (0, 0, 1, 1, 0, 2), (0, 1, 0, 1, 2, 0)
        NPR = len(Q_PART)
        SHIFT = NPR * HD
        assert SHIFT == 96

        MAX_BOUND = 40.0
        exact = sb("exact", [1, 1], I32)
        with ExitStack() as st, nc.Block() as block:
            def sbk(name, shape, dt=F32):
                return st.enter_context(nc.sbuf_tensor(name, shape, dt))

            x_bv = sbk("x_bv", [P, D])
            kk = sbk("kk", [P, KD, KPART])
            k_sq = sbk("k_sq", [P, KD, KPART])
            k_len4 = sbk("k_len4", [H, 4])
            kp = sbk("kp", [P, 3, KD, KPART], BF16)
            qq = sbk("qq", [P, KD, BLK])
            q_sq = sbk("q_sq", [P, KD, BLK])
            qp = sbk("qp", [P, 3, KD, BLK], BF16)
            q_len = sbk("q_len", [H, NB, BLK])
            shift = sbk("shift", [H, NB, BLK], BF16)
            b_all = sbk("b_all", [H, 1])
            b_low = sbk("b_low", [H, 1])
            kps, kk_in, kp0, kr0, kp1, kp2, k_out, k_row, vps, v_in, v_set, k_sqd, k_lps, k_lmax = (sem("k_" + n) for n in (
                "kps", "kk_in", "kp0", "kr0", "kp1", "kp2", "out", "row", "vps", "v_in", "v_set", "sqd", "lps", "lmax"))
            s_mean, s_cent, s_sq, s_var, s_lnv, s_rstd, s_xn = (sem("q_" + n) for n in ("mean", "cent", "sq", "var", "lnv", "rstd", "xn"))
            s_qps, s_qq, s_qp0, s_qr0, s_qp1, s_qp2 = (sem("q_" + n) for n in ("qps", "qq", "qp0", "qr0", "qp1", "qp2"))
            s_qsq, s_qlp, s_qlen, s_b2, s_lnb, s_shift, s_bmax, s_few, s_flag, s_qout, s_mout = (sem("q_" + n) for n in (
                "qsq", "qlp", "qlen", "b2", "lnb", "shift", "bmax", "few", "flag", "qout", "mout"))

            @block.sync
            def _(sp):
                sp.dma_start(x_bv[:], d["x_bv"].partition_broadcast(P)).then_inc(ld_ctx, 16)
                with sp.Fori(0, NB) as i:
                    sp.wait_ge(kp2, i + 1)
                    sp.wait_ge(kp1, i + 1)
                    for n in range(3):
                        sp.dma_start(k_dram[n].rearrange("(t p) n -> p t n", p=P)[:, :, bass.ds(i * KPART, KPART)],
                                     kp[:, n]).then_inc(k_out, 16)
                    sp.wait_ge(s_qp1, i + 1)
                    sp.wait_ge(s_qp2, i + 1)
                    for n in range(3):
                        sp.dma_start(q_dram[n].rearrange("(t p) n -> p t n", p=P)[:, :, bass.ds(i * BLK, BLK)], qp[:, n]).then_inc(s_qout, 16)
                sp.wait_ge(k_out, 16 * 12)
                for r, n in enumerate(K_PART):
                    sp.dma_start(k_op[r * HD:(r + 1) * HD], k_dram[n].rearrange("(h j) n -> j h n", j=HD)[:, :, 0:KEYS]).then_inc(k_row, 16)
                sp.wait_ge(s_shift, 1)
                sp.dma_start(m_dram.rearrange("b h n -> h b n"), shift[:]).then_inc(s_mout, 16)
                sp.wait_ge(s_mout, 16)
                sp.wait_ge(s_qout, 16 * 3 * NB)

            @block.gpsimd
            def _(pool):
                pool.memset(k_op[SHIFT:SHIFT + 1], -1.0).then_inc(v_set, 1)
                pool.wait_ge(v_set, 1)
                pool.memset(v_pad[:], 0.0).then_inc(v_set, 1)
                pool.wait_ge(v_set, 2)
                pool.memset(v_pad[:, :, :, HD:HD + 1], 1.0).then_inc(v_set, 1)

            @block.scalar
            def _(act):
                act.wait_ge(ld_ctx, 16 * 5)
                with act.Fori(0, NB) as i:
                    act.wait_ge(s_cent, i + 1)
                    act.activation(sq[:], cent[:], ACT.Square).then_inc(s_sq, 1)
                    for t in range(KD):
                        act.wait_ge(kps, KD * i + t + 1)
                        if t == 0:
                            act.wait_ge(kp2, i)
                            act.wait_ge(k_lps, i)
                        act.activation(kk[:, t, :], psum[:, 4 + t, 0:KPART], ACT.Identity, bias=x_bk[:, t:t + 1]).then_inc(kk_in, 1)
                        act.activation(k_sq[:, t, :], psum[:, 4 + t, 0:KPART], ACT.Square, bias=x_bk[:, t:t + 1]).then_inc(k_sqd, 1)
                    act.wait_ge(s_var, i + 1)
                    act.activation(lnv[:], psum[:, 0, :], ACT.Ln, bias=eps_ln[:, 0:1]).then_inc(s_lnv, 1)
                    act.wait_ge(s_lnv, i + 1)
                    act.activation(rstd[:], lnv[:], ACT.Exp, scale=-0.5).then_inc(s_rstd, 1)
                    act.wait_ge(s_qq, KD * i + KD)
                    act.activation(q_sq[:], qq[:], ACT.Square).then_inc(s_qsq, 1)
                act.wait_ge(s_b2, 1)
                act.activation(q_len[:], q_len[:], ACT.Ln).then_inc(s_lnb, 1)
                act.wait_ge(s_lnb, 1)
                act.activation(shift[:], q_len[:], ACT.Exp, scale=0.5).then_inc(s_shift, 1)

            @block.vector
            def _(dve):
                dve.wait_ge(ld_ctx, 16 * 5)
                dve.wait_ge(ld_xw, 16 * 4)
                with dve.Fori(0, NB) as i:
                    dve.wait_ge(s_mean, i + 1)
                    dve.tensor_tensor(cent[:], x_t[:, :, bass.ds(i * BLK, BLK)], psum[:, 0:1, :].to_broadcast([P, KD, BLK]),
                                      ALU.subtract).then_inc(s_cent, 1)
                    dve.wait_ge(kk_in, KD * i + KD)
                    dve.wait_ge(k_out, 48 * i)
                    dve.tensor_copy(kp[:, 0], kk[:]).then_inc(kp0, 1)
                    dve.wait_ge(kp0, i + 1)
                    dve.tensor_tensor(kk[:], kk[:], kp[:, 0], ALU.subtract).then_inc(kr0, 1)
                    dve.wait_ge(s_rstd, i + 1)
                    dve.wait_ge(s_cent, i + 1)
                    dve.tensor_tensor(xn[:], cent[:], rstd[:].unsqueeze(1).to_broadcast([P, KD, BLK]), ALU.mult).then_inc(s_xn, 1)
                    dve.wait_ge(kr0, i + 1)
                    dve.tensor_copy(kp[:, 1], kk[:]).then_inc(kp1, 1)
                    dve.wait_ge(kp1, i + 1)
                    dve.tensor_tensor(kp[:, 2], kk[:], kp[:, 1], ALU.subtract).then_inc(kp2, 1)
                    dve.wait_ge(k_lps, i + 1)
                    dve.tensor_reduce(k_len4[:, bass.ds(i, 1)], psum[0:H, 6, 0:KPART], AX_X, ALU.max).then_inc(k_lmax, 1)
                    for t in range(KD):
                        dve.wait_ge(s_qps, KD * i + t + 1)
                        dve.tensor_scalar(qq[:, t, :], psum[:, 1 + t, :], x_bq[:, t:t + 1], float(HD) ** -0.5, ALU.add,
                                          ALU.mult).then_inc(s_qq, 1)
                    dve.wait_ge(s_qq, KD * i + KD)
                    dve.wait_ge(s_qout, 48 * i)
                    dve.tensor_copy(qp[:, 0], qq[:]).then_inc(s_qp0, 1)
                    dve.wait_ge(s_qp0, i + 1)
                    dve.wait_ge(s_qsq, i + 1)
                    dve.tensor_tensor(qq[:], qq[:], qp[:, 0], ALU.subtract).then_inc(s_qr0, 1)
                    dve.wait_ge(s_qr0, i + 1)
                    dve.tensor_copy(qp[:, 1], qq[:]).then_inc(s_qp1, 1)
                    dve.wait_ge(s_qp1, i + 1)
                    dve.tensor_tensor(qp[:, 2], qq[:], qp[:, 1], ALU.subtract).then_inc(s_qp2, 1)
                    dve.wait_ge(s_qlp, i + 1)
                    dve.tensor_copy(q_len[:, bass.ds(i, 1), :].rearrange("h o n -> h (o n)"), psum[0:H, 3, :]).then_inc(s_qlen, 1)
                dve.wait_ge(k_lmax, 4)
                dve.tensor_reduce(k_len[:], k_len4[:], AX_X, ALU.max).then_inc(k_lmax, 1)
                dve.wait_ge(k_lmax, 5)
                dve.wait_ge(s_qlen, NB)
                dve.tensor_scalar(q_len[:], q_len[:], k_len[:, 0:1], 1e-12, ALU.mult, ALU.add).then_inc(s_bmax, 1)
                dve.wait_ge(s_bmax, 1)
                dve.tensor_reduce(b_all[:], q_len[:].rearrange("h b n -> h (b n)"), AX_X, ALU.max).then_inc(s_b2, 1)
                dve.wait_ge(s_b2, 1)
                dve.tensor_scalar(b_low[:], b_all[:], MAX_BOUND ** 2, None, ALU.is_le).then_inc(s_bmax, 1)
                dve.wait_ge(v_set, 3)
                for kt in range(KT):
                    rows = min(P, KEYS - kt * P)
                    dve.wait_ge(vps, kt + 1)
                    dve.tensor_tensor(v_pad[0:rows, kt, :, 0:HD], psum[0:rows, 4 + kt % 2, 0:D].rearrange("p (h d) -> p h d", h=H),
                                      x_bv[0:rows].rearrange("p (h d) -> p h d", h=H), ALU.add).then_inc(v_in, 1)
                dve.wait_ge(s_few, 1)
                dve.tensor_scalar(exact[:], psum[0:1, 0, 0:1], float(H) - 0.5, None, ALU.is_lt).then_inc(s_flag, 1)
                dve.wait_ge(s_flag, 1)

            @block.tensor
            def _(pe):
                pe.wait_ge(ld_ctx, 16 * 5)
                pe.wait_ge(ld_xw, 16 * 4)
                with pe.Fori(0, NB) as i:
                    for k in range(KD):
                        mm = pe.matmul(psum[:, 0, :], mean_w, x_t[:, k, bass.ds(i * BLK, BLK)], start=k == 0, stop=k == KD - 1)
                    mm.then_inc(s_mean, 1)
                    for t in range(KD):
                        pe.wait_ge(k_sqd, KD * i)
                        for k in range(KD):
                            mm = pe.matmul(psum[:, 4 + t, 0:KPART], x_wk[:, k, t * P:(t + 1) * P], ctx_t[:, k, bass.ds(i * KPART, KPART)],
                                           start=k == 0, stop=k == KD - 1)
                        mm.then_inc(kps, 1)
                    pe.wait_ge(s_sq, i + 1)
                    for k in range(KD):
                        mm = pe.matmul(psum[:, 0, :], mean_w, sq[:, k, :], start=k == 0, stop=k == KD - 1)
                    mm.then_inc(s_var, 1)
                    pe.wait_ge(k_sqd, KD * i + KD)
                    pe.wait_ge(k_lmax, i)
                    for k in range(KD):
                        mm = pe.matmul(psum[0:H, 6, 0:KPART], head_of[:, k, :], k_sq[:, k, :], start=k == 0, stop=k == KD - 1)
                    mm.then_inc(k_lps, 1)
                    pe.wait_ge(s_xn, i + 1)
                    pe.wait_ge(s_qq, KD * i)
                    for t in range(KD):
                        for k in range(KD):
                            mm = pe.matmul(psum[:, 1 + t, :], x_wq[:, k, t * P:(t + 1) * P], xn[:, k, :], start=k == 0, stop=k == KD - 1)
                        mm.then_inc(s_qps, 1)
                    pe.wait_ge(s_qsq, i + 1)
                    pe.wait_ge(s_qlen, i)
                    for k in range(KD):
                        mm = pe.matmul(psum[0:H, 3, :], head_of[:, k, :], q_sq[:, k, :], start=k == 0, stop=k == KD - 1)
                    mm.then_inc(s_qlp, 1)
                pe.wait_ge(k_sqd, KD * NB)
                for kt in range(KT):
                    rows = min(P, KEYS - kt * P)
                    if kt >= 2:
                        pe.wait_ge(v_in, kt - 1)
                    for k in range(KD):
                        mm = pe.matmul(psum[0:rows, 4 + kt % 2, 0:D], ctx_t[:, k, kt * P:kt * P + rows], x_wv[:, k, :],
                                       start=k == 0, stop=k == KD - 1)
                    mm.then_inc(vps, 1)
                pe.wait_ge(s_bmax, 2)
                pe.matmul(psum[0:1, 0, 0:1], b_low[:], ones[0:H, 0:1], start=True, stop=True).then_inc(s_few, 1)

        with ExitStack() as st, nc.Block() as block:
            q_all = st.enter_context(nc.sbuf_tensor("q_all", [P, H, BLK], BF16))
            mx = st.enter_context(nc.sbuf_tensor("mx", [P, NC, H], F32))
            mx_t = st.enter_context(nc.sbuf_tensor("mx_t", [H, BLK], BF16))
            x_q, x_ms, x_mx, x_mt, x_mn, x_out = (sem("x_" + n) for n in ("q", "ms", "mx", "mt", "mn", "out"))

            @block.sync
            def _(sp):
                with sp.If(sp.value_load(exact[0:1, 0:1], min_val=0, max_val=1)):
                    with sp.Fori(0, NB) as i:
                        sp.wait_ge(x_ms, H * NC * i)
                        for r, n in enumerate(Q_PART):
                            sp.dma_start(q_all[r * HD:(r + 1) * HD], q_dram[n].rearrange("(h j) n -> j h n", j=HD)[:, :, bass.ds(i * BLK, BLK)]).then_inc(x_q, 16)
                        sp.wait_ge(x_mn, i + 1)
                        sp.dma_start(m_dram[bass.ds(i, 1)].rearrange("o h n -> (o h) n"), mx_t[:]).then_inc(x_out, 16)
                    sp.wait_ge(x_out, 16 * NB)

            @block.scalar
            def _(act):
                with act.If(act.value_load(exact[0:1, 0:1], min_val=0, max_val=1)):
                    with act.Fori(0, NB) as i:
                        act.wait_ge(x_mt, i + 1)
                        act.wait_ge(x_out, 16 * i)
                        act.activation(mx_t[:], psum[0:H, 7, :], ACT.Copy).then_inc(x_mn, 1)

            @block.vector
            def _(dve):
                with dve.If(dve.value_load(exact[0:1, 0:1], min_val=0, max_val=1)):
                    with dve.Fori(0, NB) as i:
                        turned = dve.to_reg(i)
                        dve.wait_ge(ld_const, 16)
                        dve.wait_ge(x_mt, turned)
                        with dve.Fori(0, H // 2) as h2:
                            for w in range(2 * NC):
                                e, c = divmod(w, NC)
                                dve.wait_ge(x_ms, H * NC * i + 2 * NC * h2 + w + 1)
                                dve.tensor_reduce(mx[:, c, bass.ds(2 * h2 + e, 1)],
                                                  psum[:, 4 * (w % 2):4 * (w % 2) + 4, :].rearrange("p b n -> p (b n)")[:, 0:KEYS],
                                                  AX_X, ALU.max).then_inc(x_mx, 1)

            @block.tensor
            def _(pe):
                with pe.If(pe.value_load(exact[0:1, 0:1], min_val=0, max_val=1)):
                    with pe.Fori(0, NB) as i:
                        copied = pe.to_reg(i)
                        loaded = pe.to_reg(16 * NPR * (i + 1))
                        pe.wait_ge(ld_const, 16)
                        pe.wait_ge(x_mn, copied)
                        pe.wait_ge(x_q, loaded)
                        with pe.Fori(0, H // 2) as h2:
                            for w in range(2 * NC):
                                e, c = divmod(w, NC)
                                pe.wait_ge(x_mx, H * NC * i + 2 * NC * h2 + max(w - 1, 0))
                                h = bass.ds(2 * h2 + e, 1)
                                for b in range(4):
                                    cols = min(BLK, KEYS - b * BLK)
                                    mm = pe.matmul(psum[:, 4 * (w % 2) + b, 0:cols], q_all[0:SHIFT, h, c * CH:(c + 1) * CH].rearrange("p o n -> p (o n)"),
                                                   k_op[0:SHIFT, h, b * BLK:b * BLK + cols].rearrange("p o n -> p (o n)"), start=True, stop=True)
                                mm.then_inc(x_ms, 1)
                        pe.wait_ge(x_mx, H * NC * (i + 1))
                        for c in range(NC):
                            mm = pe.transpose(psum[0:H, 7, c * CH:(c + 1) * CH], mx[:, c, :], ident)
                        mm.then_inc(x_mt, 1)

        slot_rows = nc.dram_tensor("slot_rows", (P * SPAN, 2), F32, kind="Internal").ap()
        xn_rows = nc.dram_tensor("xn_rows", (N + P, D), F32, kind="Internal").ap()
        y_rows = nc.dram_tensor("y_rows", (N + P, D), F32, kind="Internal").ap()
        e_tile = sb("e_tile", [P, TILES])
        e_int = sb("e_int", [P, TILES], I32)
        fresh = sb("fresh", [P, TILES], I32)
        place = sb("place", [P, TILES], I32)
        with ExitStack() as st:
            def sbb(name, shape, dt=F32):
                return st.enter_context(nc.sbuf_tensor(name, shape, dt))

            q_op = sbb("q_op", [P, H, BLK], BF16)
            pr = sbb("pr", [P, 3, 4, BLK])
            osb = sbb("osb", [P, 2, BLK])
            rden = sbb("rden", [P, BLK])
            on = sbb("on", [P, 4, BLK])
            GR = KT * 4
            s_sc, s_ex, s_pv, s_os, s_dn, s_rd, s_on, s_wps, s_x2 = (sem("b_" + n) for n in ("sc", "ex", "pv", "os", "dn", "rd", "on", "wps", "x2"))
            s_qop = [sem("b_qop_%d" % g) for g in range(4)]

            rconst = sbb("rconst", [P, NC * EXP + EXP + TILES + TT + 1])
            seg = rconst[:, 0:NC * EXP]
            region = rconst[:, NC * EXP:NC * EXP + EXP]
            tile_no = rconst[:, NC * EXP + EXP:NC * EXP + EXP + TILES]
            tok_no = rconst[:, NC * EXP + EXP + TILES:]
            keys = sbb("keys", [P, KD, EXP])
            rw = sbb("rw", [P, KD, EXP])
            rt = sbb("rt", [P, KD, EXP])
            ksq = sbb("ksq", [P, KD, EXP])
            rb = sbb("rb", [P, EXP])
            cst = sbb("cst", [P, EXP])
            neg = sbb("neg", [P, EXP])
            room = ctx_t[:].rearrange("p k n -> p (k n)")
            x2b = room[:, 0:KD * BLK].rearrange("p (k n) -> p k n", k=KD)
            x2r = room[:, KD * BLK:KD * BLK + NC * D].rearrange("p (t n) -> p t n", t=NC)
            xr = room[:, KD * BLK + NC * D:KD * BLK + 2 * NC * D].rearrange("p (t n) -> p t n", t=NC)
            pad = room[:, KD * BLK + NC * D:KD * BLK + NC * D + 2 * SPAN].rearrange("p (t c) -> p t c", c=2)
            lg = sbb("lg", [P, NC, EXP])
            top = sbb("top", [P, NC, 8])
            tix = sbb("tix", [P, NC, 8], U32)
            tif = sbb("tif", [P, NC, TOPK])
            wx = sbb("wx", [P, NC, TOPK])
            wsum = sbb("wsum", [P, NC])
            oh = sbb("oh", [P, NC, TOPK, EXP])
            pick = sbb("pick", [P, NC, TOPK, EXP])
            chosen = sbb("chosen", [P, EXP, NC])
            upto = sbb("upto", [P, EXP, NC])
            base = sbb("base", [P, EXP])
            pos = sbb("pos", [P, EXP, NC])
            slot = sbb("slot", [P, NC, TOPK])
            slot_i = sbb("slot_i", [P, NC, TOPK], I32)
            slot_t = sbb("slot_t", [P, NC, TOPK])
            entry = sbb("entry", [P, NC, TOPK, 2])
            need_i = sbb("need_i", [P, EXP], I32)
            need = sbb("need", [P, EXP])
            ends = sbb("ends", [P, EXP])
            jump = sbb("jump", [P, TILES])
            cmp_e = pr[:, 0].rearrange("p j n -> p (j n)")[:, 0:TILES * EXP].rearrange("p (t e) -> p t e", e=EXP)
            l_r, s_set, s_pad, s_zout, s_cps, s_pre = (sem("r_" + n) for n in ("ld", "set", "pad", "zout", "cps", "pre"))
            s_mean, s_cent, s_sq, s_var, s_lnv, s_rstd, s_xn, s_xsq, s_lps, s_lg = (sem("r_" + n) for n in (
                "mean", "cent", "sq", "var", "lnv", "rstd", "xn", "xsq", "lps", "lg"))
            s_x2b, s_x2p, s_x2r, s_yout, s_xtp, s_xr, s_xout = (sem("r_" + n) for n in ("x2b", "x2p", "x2r", "yout", "xtp", "xr", "xout"))
            s_top, s_gap, s_exp, s_oh, s_wsum, s_entry, s_cnt, s_within, s_slot, s_scat, s_etile, s_pair = (sem("r_" + n) for n in (
                "top", "gap", "exp", "oh", "wsum", "entry", "cnt", "within", "slot", "scat", "etile", "pair"))
            nc.clear_and_free_semaphores(a_sems)
            block = st.enter_context(nc.Block())

            @block.sync
            def _(sp):
                def load_queries(i, g):
                    heads = slice(4 * g, 4 * g + 4)
                    for r, n in enumerate(Q_PART):
                        sp.dma_start(q_op[r * HD:(r + 1) * HD, heads],
                                     q_dram[n].rearrange("(h j) n -> j h n", j=HD)[:, heads, bass.ds(i * BLK, BLK)]).then_inc(s_qop[g], 16)
                    sp.dma_start(q_op[SHIFT:SHIFT + 1, heads], m_dram[bass.ds(i, 1), heads]).then_inc(s_qop[g], 16)

                load_queries(0, 0)
                sp.dma_start(keys[:], d["f_keys"]).then_inc(l_r, 16)
                sp.dma_start(rw[:], d["f_rw"]).then_inc(l_r, 16)
                sp.dma_start(rb[:], d["f_rb"].partition_broadcast(P)).then_inc(l_r, 16)
                sp.dma_start(rconst[:], d["rconst"]).then_inc(l_r, 16)
                for g in range(1, 4):
                    load_queries(0, g)
                sp.wait_ge(s_set, 4)
                sp.dma_start(slot_rows.rearrange("(p t) c -> p t c", p=P), pad).then_inc(s_pad, 16)
                sp.dma_start(xn_rows[N:N + P], x2r[:, 0]).then_inc(s_zout, 16)
                sp.dma_start(y_rows[N:N + P], x2r[:, 1]).then_inc(s_zout, 16)
                with sp.Fori(0, NB - 1) as i:
                    for g in range(4):
                        sp.wait_ge(s_sc, 2 * GR * i + 2 * KT * (g + 1))
                        load_queries(i + 1, g)

            @block.gpsimd
            def _(pool):
                pool.wait_ge(s_pad, 16)
                with pool.Fori(0, NB) as j:
                    rows = bass.ds(j * BLK, BLK)
                    pool.wait_ge(s_x2, KD * j + KD)
                    pool.tensor_copy(x2b, x_t[:, :, rows]).then_inc(s_x2b, 1)
                    pool.wait_ge(s_cent, j + 1)
                    pool.tensor_tensor(sq[:], cent[:], cent[:], ALU.mult).then_inc(s_pair, 1)
                    pool.wait_ge(s_pair, 2 * j + 1)
                    pool.tensor_tensor(sq[:, 0, :], sq[:, 0, :], sq[:, 1, :], ALU.add).then_inc(s_sq, 1)
                    pool.wait_ge(s_x2r, 2 * j + 2)
                    pool.dma_start(y_rows[rows].rearrange("(t p) c -> p t c", p=P), x2r).then_inc(s_yout, 16)
                    pool.wait_ge(s_xn, j + 1)
                    pool.tensor_tensor(sq[:], xn[:], xn[:], ALU.mult).then_inc(s_pair, 1)
                    pool.wait_ge(s_pair, 2 * j + 2)
                    pool.tensor_tensor(sq[:, 0, :], sq[:, 0, :], sq[:, 1, :], ALU.add).then_inc(s_xsq, 1)
                    turned = pool.to_reg(2 * j + 2)
                    pool.wait_ge(s_pad, 16)
                    pool.wait_ge(s_xr, turned)
                    pool.dma_start(xn_rows[rows].rearrange("(t p) c -> p t c", p=P), xr).then_inc(s_xout, 16)
                    placed = pool.to_reg(7 * j + 7)
                    pool.wait_ge(s_pad, 16)
                    pool.wait_ge(s_slot, placed)
                    for c in range(NC):
                        for k in range(TOPK):
                            pool.indirect_dma_start(out=slot_rows, out_offset=bass.IndirectOffsetOnAxis(ap=slot_i[:, c, k:k + 1].bitcast(U32), axis=0),
                                                    in_=entry[:, c, k, :], in_offset=None).then_inc(s_scat, 16)
                pool.wait_ge(s_scat, 16 * TT * TOPK)
                pool.wait_ge(s_zout, 32)
                pool.wait_ge(s_yout, 16 * NB)
                pool.wait_ge(s_xout, 16 * NB)

            @block.scalar
            def _(act):
                def deviations(j):
                    act.wait_ge(s_var, j + 1)
                    act.activation(lnv[:], psum[:, 7, :], ACT.Ln, bias=eps_ln[:, 0:1]).then_inc(s_lnv, 1)
                    act.wait_ge(s_lnv, j + 1)
                    act.activation(rstd[:], lnv[:], ACT.Exp, scale=-0.5).then_inc(s_rstd, 1)

                def weights(j):
                    act.wait_ge(s_gap, j + 1)
                    act.activation(wx[:], wx[:], ACT.Exp).then_inc(s_exp, 1)

                def steps(i, first):
                    for n in range(GR):
                        for e in range(2):
                            p = 2 * n + e
                            act.wait_ge(s_sc, 2 * GR * i + p + 1)
                            if n >= 3:
                                act.wait_ge(s_pv, GR * i + n - 2)
                            else:
                                act.wait_ge(s_pv, GR * i)
                            rows = min(P, KEYS - (n % KT) * P)
                            b = 2 * (p % 3)
                            act.activation(pr[0:rows, n % 3, 2 * e:2 * e + 2, :], psum[0:rows, b:b + 2, :], ACT.Exp).then_inc(s_ex, 1)
                        if n == 21 and not first:
                            deviations(i - 1)
                        if n == 43 and not first:
                            weights(i - 1)

                steps(0, True)
                with act.Fori(1, NB) as i:
                    steps(i, False)
                deviations(NB - 1)
                weights(NB - 1)

            @block.vector
            def _(dve):
                def sums(i, g):
                    dve.wait_ge(s_pv, GR * i + KT * (g + 1))
                    dve.tensor_copy(osb[:, g % 2, :], psum[:, 6, :]).then_inc(s_os, 1)

                def heads(i, g):
                    dve.wait_ge(s_dn, 4 * i + g + 1)
                    dve.reciprocal(rden[:], psum[:, 7, :]).then_inc(s_rd, 1)
                    dve.wait_ge(s_rd, 4 * i + g + 1)
                    dve.wait_ge(s_os, 4 * i + g + 1)
                    dve.tensor_tensor(on[:, g, :], osb[:, g % 2, :], rden[:], ALU.mult).then_inc(s_on, 1)

                def residual(i):
                    for t in range(KD):
                        dve.wait_ge(s_wps, KD * i + t + 1)
                        dve.scalar_tensor_tensor(out=x_t[:, t, bass.ds(i * BLK, BLK)], in0=psum[:, 7, :], scalar=x_bo[:, t:t + 1],
                                                 in1=x_t[:, t, bass.ds(i * BLK, BLK)], op0=ALU.add, op1=ALU.add).then_inc(s_x2, 1)

                def centred(j):
                    dve.wait_ge(s_mean, j + 1)
                    dve.wait_ge(s_x2, KD * j + KD)
                    dve.tensor_tensor(cent[:], x_t[:, :, bass.ds(j * BLK, BLK)], psum[:, 7:8, :].to_broadcast([P, KD, BLK]),
                                      ALU.subtract).then_inc(s_cent, 1)

                def residual_rows(j):
                    dve.wait_ge(s_zout, 32)
                    dve.wait_ge(s_yout, 16 * j)
                    for u in range(2):
                        dve.wait_ge(s_x2p, 2 * j + u + 1)
                        dve.tensor_copy(x2r[:, 2 * u:2 * u + 2], psum[:, 7, :].rearrange("p (t n) -> p t n", t=2)).then_inc(s_x2r, 1)

                def normalised(j):
                    dve.wait_ge(s_rstd, j + 1)
                    dve.wait_ge(s_lps, j)
                    dve.tensor_tensor(xn[:], cent[:], rstd[:].unsqueeze(1).to_broadcast([P, KD, BLK]), ALU.mult).then_inc(s_xn, 1)

                def normalised_rows(j):
                    dve.wait_ge(s_pad, 16)
                    dve.wait_ge(s_xout, 16 * j)
                    for u in range(2):
                        dve.wait_ge(s_xtp, 2 * j + u + 1)
                        dve.tensor_copy(xr[:, 2 * u:2 * u + 2], psum[:, 7, :].rearrange("p (t n) -> p t n", t=2)).then_inc(s_xr, 1)

                def best(j):
                    dve.wait_ge(s_lps, j + 1)
                    dve.tensor_tensor(lg[:], psum[:, 7, 0:NC * EXP].rearrange("p (t e) -> p t e", t=NC),
                                      cst[:].unsqueeze(1).to_broadcast([P, NC, EXP]), ALU.add).then_inc(s_lg, 1)
                    summed = dve.to_reg(j + 1)
                    dve.wait_ge(ld_const, 16)
                    dve.wait_ge(s_lg, summed)
                    for c in range(NC):
                        dve.max(top[:, c, :], lg[:, c, :]).then_inc(s_top, 1)
                    ordered = dve.to_reg(2 * NC * j + NC)
                    dve.wait_ge(ld_const, 16)
                    dve.wait_ge(s_top, ordered)
                    for c in range(NC):
                        dve.max_index(tix[:, c, :], top[:, c, :], lg[:, c, :]).then_inc(s_top, 1)

                def choice(j):
                    dve.tensor_tensor(wx[:], top[:, :, 0:TOPK], top[:, :, 0:1].to_broadcast([P, NC, TOPK]), ALU.subtract).then_inc(s_gap, 1)
                    dve.wait_ge(s_top, 2 * NC * j + 2 * NC)
                    dve.tensor_copy(tif[:], tix[:, :, 0:TOPK]).then_inc(s_oh, 1)
                    dve.wait_ge(s_oh, 3 * j + 1)
                    dve.tensor_tensor(oh[:].rearrange("p t j e -> p (t j) e"),
                                      tif[:].rearrange("p t j -> p (t j)").unsqueeze(2).to_broadcast([P, NC * TOPK, EXP]),
                                      expert_no.unsqueeze(1).to_broadcast([P, NC * TOPK, EXP]), ALU.is_equal).then_inc(s_oh, 1)
                    dve.wait_ge(s_oh, 3 * j + 2)
                    dve.tensor_reduce(chosen[:], oh[:].rearrange("p t j e -> p e t j"), AX_X, ALU.add).then_inc(s_oh, 1)

                def entries(j):
                    dve.wait_ge(s_scat, 16 * NC * TOPK * j)
                    dve.tensor_copy(entry[:, :, :, 0:1].bitcast(U32),
                                    tok_no[:, bass.ds(j * NC, NC)].unsqueeze(2).unsqueeze(3).to_broadcast([P, NC, TOPK, 1])).then_inc(s_entry, 1)
                    dve.wait_ge(s_exp, j + 1)
                    dve.tensor_reduce(wsum[:], wx[:], AX_X, ALU.add).then_inc(s_wsum, 1)
                    dve.wait_ge(s_wsum, 2 * j + 1)
                    dve.reciprocal(wsum[:], wsum[:]).then_inc(s_wsum, 1)
                    dve.wait_ge(s_wsum, 2 * j + 2)
                    dve.tensor_tensor(entry[:, :, :, 1:2].rearrange("p t j o -> p t (j o)"), wx[:], wsum[:].unsqueeze(2).to_broadcast([P, NC, TOPK]),
                                      ALU.mult).then_inc(s_entry, 1)
                    dve.wait_ge(s_cnt, j + 1)
                    total = psum[:, 7, 0:EXP * NC].rearrange("p (e t) -> p e t", e=EXP)
                    within = psum[:, 7, EXP * NC:2 * EXP * NC].rearrange("p (e t) -> p e t", e=EXP)
                    dve.tensor_tensor_scan(upto[:].rearrange("p e t -> p (e t)"), seg, psum[:, 7, 0:EXP * NC], 0.0, ALU.mult, ALU.add).then_inc(s_within, 1)
                    dve.wait_ge(s_within, 5 * j + 1)
                    dve.tensor_tensor(pos[:], upto[:], total, ALU.subtract).then_inc(s_within, 1)
                    dve.wait_ge(s_within, 5 * j + 2)
                    dve.tensor_tensor(pos[:], pos[:], within, ALU.add).then_inc(s_within, 1)
                    dve.wait_ge(s_within, 5 * j + 3)
                    dve.tensor_tensor(pos[:], pos[:], base[:].unsqueeze(2).to_broadcast([P, EXP, NC]), ALU.add).then_inc(s_within, 1)
                    dve.wait_ge(s_within, 5 * j + 4)
                    dve.tensor_tensor(base[:], base[:], upto[:, :, NC - 1], ALU.add).then_inc(s_within, 1)
                    dve.tensor_tensor(pick[:], oh[:], pos[:].rearrange("p e t -> p t e").unsqueeze(2).to_broadcast([P, NC, TOPK, EXP]),
                                      ALU.mult).then_inc(s_slot, 1)
                    dve.wait_ge(s_slot, 7 * j + 1)
                    dve.tensor_reduce(slot[:], pick[:], AX_X, ALU.add).then_inc(s_slot, 1)
                    dve.wait_ge(s_slot, 7 * j + 2)
                    dve.tensor_copy(slot_i[:], slot[:]).then_inc(s_slot, 1)
                    dve.wait_ge(s_slot, 7 * j + 3)
                    dve.tensor_scalar(slot_i[:], slot_i[:], 7, None, ALU.arith_shift_right).then_inc(s_slot, 1)
                    dve.wait_ge(s_slot, 7 * j + 4)
                    dve.tensor_scalar(slot_t[:], slot_i[:], float(1 - P * SPAN), None, ALU.mult).then_inc(s_slot, 1)
                    dve.wait_ge(s_slot, 7 * j + 5)
                    dve.scalar_tensor_tensor(out=slot_t[:], in0=slot[:], scalar=float(SPAN), in1=slot_t[:], op0=ALU.mult, op1=ALU.add).then_inc(s_slot, 1)
                    dve.wait_ge(s_slot, 7 * j + 6)
                    dve.wait_ge(s_entry, 2 * j + 3)
                    dve.tensor_copy(slot_i[:], slot_t[:]).then_inc(s_slot, 1)

                def steps(i, first):
                    if not first:
                        centred(i - 1)
                    sums(i, 0)
                    heads(i, 0)
                    if not first:
                        normalised(i - 1)
                        residual_rows(i - 1)
                    sums(i, 1)
                    heads(i, 1)
                    if not first:
                        normalised_rows(i - 1)
                        best(i - 1)
                    sums(i, 2)
                    if not first:
                        choice(i - 1)
                    heads(i, 2)
                    if not first:
                        entries(i - 1)
                    sums(i, 3)
                    heads(i, 3)
                    residual(i)

                dve.memset(pad, 0.0).then_inc(s_set, 1)
                dve.memset(x2r[:, 0:2], 0.0).then_inc(s_set, 1)
                dve.memset(neg[:], -1.0).then_inc(s_set, 1)
                dve.wait_ge(l_r, 16 * 4)
                dve.wait_ge(s_set, 3)
                dve.tensor_copy(pad[:, :, 0:1].bitcast(U32), tok_no[:, TT:TT + 1].unsqueeze(1).to_broadcast([P, SPAN, 1])).then_inc(s_set, 1)
                dve.tensor_copy(base[:], region).then_inc(s_entry, 1)
                dve.tensor_tensor(ksq[:], keys[:], keys[:], ALU.mult).then_inc(s_pre, 1)
                dve.scalar_tensor_tensor(out=rt[:], in0=keys[:], scalar=2.0, in1=rw[:], op0=ALU.mult, op1=ALU.add).then_inc(s_pre, 1)
                dve.wait_ge(s_cps, 1)
                dve.tensor_tensor(cst[:], rb[:], psum[:, 7, 0:EXP], ALU.subtract).then_inc(s_pre, 1)
                dve.wait_ge(s_pre, 3)
                steps(0, True)
                with dve.Fori(1, NB) as i:
                    steps(i, False)
                centred(NB - 1)
                residual_rows(NB - 1)
                normalised(NB - 1)
                normalised_rows(NB - 1)
                best(NB - 1)
                choice(NB - 1)
                entries(NB - 1)
                dve.wait_ge(s_within, 5 * NB)
                dve.tensor_tensor(need[:], base[:], region, ALU.subtract).then_inc(s_etile, 1)
                dve.wait_ge(s_etile, 1)
                dve.tensor_scalar(need[:], need[:], float(P - 1), None, ALU.add).then_inc(s_etile, 1)
                dve.wait_ge(s_etile, 2)
                dve.tensor_copy(need_i[:], need[:]).then_inc(s_etile, 1)
                dve.wait_ge(s_etile, 3)
                dve.tensor_scalar(need_i[:], need_i[:], 7, None, ALU.arith_shift_right).then_inc(s_etile, 1)
                dve.wait_ge(s_etile, 4)
                dve.tensor_copy(need[:], need_i[:]).then_inc(s_etile, 1)
                dve.wait_ge(s_etile, 5)
                dve.tensor_tensor_scan(ends[:], ones[:, 0:EXP], need[:], 0.0, ALU.mult, ALU.add).then_inc(s_etile, 1)
                dve.wait_ge(s_etile, 6)
                dve.tensor_scalar(need[:], need[:], -1.0, float(TT), ALU.mult, ALU.add).then_inc(s_etile, 1)
                dve.tensor_tensor(cmp_e, tile_no.unsqueeze(2).to_broadcast([P, TILES, EXP]),
                                  ends[:].unsqueeze(1).to_broadcast([P, TILES, EXP]), ALU.is_ge).then_inc(s_etile, 1)
                dve.wait_ge(s_etile, 8)
                dve.tensor_reduce(e_tile[:], cmp_e, AX_X, ALU.add).then_inc(s_etile, 1)
                dve.wait_ge(s_etile, 9)
                dve.tensor_tensor(cmp_e, cmp_e, need[:].unsqueeze(1).to_broadcast([P, TILES, EXP]), ALU.mult).then_inc(s_etile, 1)
                dve.tensor_scalar(e_tile[:], e_tile[:], float(EXP - 1), None, ALU.min).then_inc(s_etile, 1)
                dve.wait_ge(s_etile, 11)
                dve.tensor_reduce(jump[:], cmp_e, AX_X, ALU.add).then_inc(s_etile, 1)
                dve.tensor_copy(e_int[:], e_tile[:]).then_inc(s_etile, 1)
                dve.tensor_tensor(fresh[:, 2:TILES], e_tile[:, 2:TILES], e_tile[:, 0:TILES - 2], ALU.is_gt).then_inc(s_etile, 1)
                dve.wait_ge(s_etile, 14)
                dve.tensor_tensor(jump[:], jump[:], tile_no, ALU.add).then_inc(s_etile, 1)
                dve.wait_ge(s_etile, 15)
                dve.tensor_scalar(jump[:], jump[:], float(EXP * TT), None, ALU.min).then_inc(s_etile, 1)
                dve.wait_ge(s_etile, 16)
                dve.tensor_scalar(place[:], jump[:], 2.0, None, ALU.mult).then_inc(s_etile, 1)
                dve.wait_ge(s_etile, 17)

            @block.tensor
            def _(pe):
                def scores(i, n):
                    g, kt = divmod(n, KT)
                    rows = min(P, KEYS - kt * P)
                    if kt == 0:
                        pe.wait_ge(s_qop[g], 16 * (NPR + 1) * (i + 1))
                    for e in range(2):
                        p = 2 * n + e
                        pe.wait_ge(s_ex, 2 * GR * i + max(p - 2, 0))
                        for j in range(2):
                            h = 4 * g + 2 * e + j
                            mm = pe.matmul(psum[0:rows, 2 * (p % 3) + j, :], k_op[0:SHIFT + 1, h, kt * P:kt * P + rows],
                                           q_op[0:SHIFT + 1, h, :], start=True, stop=True)
                        mm.then_inc(s_sc, 1)

                def weighted(i, n):
                    g, kt = divmod(n, KT)
                    rows = min(P, KEYS - kt * P)
                    pe.wait_ge(s_ex, 2 * GR * i + 2 * n + 2)
                    if kt == 0:
                        pe.wait_ge(s_os, 4 * i + g)
                    for j in range(4):
                        mm = pe.matmul(psum[32 * j:32 * j + 32, 6, :], v_pad[0:rows, kt, 4 * g + j, :], pr[0:rows, n % 3, j, :],
                                       start=kt == 0, stop=kt == KT - 1)
                    mm.then_inc(s_pv, 1)

                def denominators(i, g):
                    pe.wait_ge(s_os, 4 * i + g + 1)
                    if g == 0:
                        pe.wait_ge(s_pre, 3)
                        pe.wait_ge(s_cent, i)
                    elif g == 1:
                        pe.wait_ge(s_x2r, 2 * i)
                    elif g == 2:
                        pe.wait_ge(s_lg, i)
                    else:
                        pe.wait_ge(s_within, 5 * i)
                    pe.wait_ge(s_rd, 4 * i + g)
                    pe.matmul(psum[:, 7, :], den_sel, osb[:, g % 2, :], start=True, stop=True).then_inc(s_dn, 1)

                def output(i, t):
                    pe.wait_ge(s_on, 4 * i + 4)
                    pe.wait_ge(s_x2, KD * i + t)
                    for g in range(4):
                        mm = pe.matmul(psum[:, 7, :], x_wo[:, g, t * P:(t + 1) * P], on[:, g, :], start=g == 0, stop=g == 3)
                    mm.then_inc(s_wps, 1)

                def mean(j):
                    pe.wait_ge(s_x2, KD * j + KD)
                    for k in range(KD):
                        mm = pe.matmul(psum[:, 7, :], mean_w, x_t[:, k, bass.ds(j * BLK, BLK)], start=k == 0, stop=k == KD - 1)
                    mm.then_inc(s_mean, 1)

                def variance(j, reader, read):
                    pe.wait_ge(reader, read)
                    pe.wait_ge(s_sq, j + 1)
                    pe.matmul(psum[:, 7, :], mean_w, sq[:, 0, :], start=True, stop=True).then_inc(s_var, 1)

                def turned(j, u, src, done):
                    for c in range(2):
                        for k in range(KD):
                            mm = pe.transpose(psum[:, 7, c * D + k * P:c * D + (k + 1) * P],
                                              src[:, k, (2 * u + c) * P:(2 * u + c + 1) * P], ident)
                    mm.then_inc(done, 1)

                def residual_turned(j, u, reader=s_lnv):
                    pe.wait_ge(s_x2b, j + 1)
                    if u == 0:
                        pe.wait_ge(reader, j + 1)
                    else:
                        pe.wait_ge(s_x2r, 2 * j + 1)
                    turned(j, u, x2b, s_x2p)

                def normalised_turned(j, u, heads_read):
                    pe.wait_ge(s_xn, j + 1)
                    if u == 0:
                        pe.wait_ge(s_x2r, 2 * j + 2)
                        pe.wait_ge(s_rd, heads_read)
                    else:
                        pe.wait_ge(s_xr, 2 * j + 1)
                    turned(j, u, xn, s_xtp)

                def logits(j):
                    pe.wait_ge(s_xr, 2 * j + 2)
                    pe.wait_ge(s_xsq, j + 1)
                    for c in range(NC):
                        for k in range(KD):
                            pe.matmul(psum[:, 7, c * EXP:(c + 1) * EXP], xn[:, k, c * P:(c + 1) * P], rt[:, k, :], start=k == 0, stop=False)
                        mm = pe.matmul(psum[:, 7, c * EXP:(c + 1) * EXP], sq[:, 0, c * P:(c + 1) * P], neg[:], start=False, stop=True)
                    mm.then_inc(s_lps, 1)

                def counts(j, heads_read):
                    pe.wait_ge(s_rd, heads_read)
                    pe.wait_ge(s_oh, 3 * j + 3)
                    picked = chosen[:].rearrange("p e t -> p (e t)")
                    pe.matmul(psum[:, 7, 0:EXP * NC], ones[:, 0:P], picked, start=True, stop=True)
                    pe.matmul(psum[:, 7, EXP * NC:2 * EXP * NC], causal, picked, start=True, stop=True).then_inc(s_cnt, 1)

                def key_lengths():
                    pe.wait_ge(s_pre, 2)
                    for k in range(KD):
                        mm = pe.matmul(psum[:, 7, 0:EXP], ones[:, 0:P], ksq[:, k, :], start=k == 0, stop=k == KD - 1)
                    mm.then_inc(s_cps, 1)

                def steps(i, first):
                    for n in range(GR):
                        g, kt = divmod(n, KT)
                        scores(i, n)
                        if n > 0:
                            weighted(i, n - 1)
                        elif not first:
                            weighted(i - 1, GR - 1)
                        if kt == 3 and g > 0:
                            denominators(i, g - 1)
                        if first and n == 5:
                            key_lengths()
                        if first:
                            continue
                        j = i - 1
                        if n == 3:
                            denominators(j, 3)
                        elif n == 6:
                            output(j, 0)
                        elif n == 9:
                            output(j, 1)
                        elif n == 12:
                            mean(j)
                        elif n == 20:
                            variance(j, s_rd, 4 * i + 1)
                        elif n == 22:
                            residual_turned(j, 0)
                        elif n == 25:
                            residual_turned(j, 1)
                        elif n == 33:
                            normalised_turned(j, 0, 4 * i + 2)
                        elif n == 35:
                            normalised_turned(j, 1, 0)
                        elif n == 37:
                            logits(j)
                        elif n == 46:
                            counts(j, 4 * i + 3)

                pe.wait_ge(k_row, 16 * NPR)
                steps(0, True)
                with pe.Fori(1, NB) as i:
                    steps(i, False)
                weighted(NB - 1, GR - 1)
                denominators(NB - 1, 3)
                output(NB - 1, 0)
                output(NB - 1, 1)
                mean(NB - 1)
                residual_turned(NB - 1, 0, s_cent)
                residual_turned(NB - 1, 1)
                variance(NB - 1, s_x2r, 2 * NB)
                normalised_turned(NB - 1, 0, 4 * NB)
                normalised_turned(NB - 1, 1, 4 * NB)
                logits(NB - 1)
                counts(NB - 1, 4 * NB)

        with ExitStack() as st, nc.Block() as block:
            def sbe(name, shape, dt=F32):
                return st.enter_context(nc.sbuf_tensor(name, shape, dt))

            def seme(name):
                return sem("e_" + name)

            w1 = sbe("w1", [P, 2, KD * F + FF])
            w2 = sbe("w2", [P, 2, FF, D])
            b2 = sbe("b2", [P, EXP, D])
            slots = sbe("slots", [P, SPAN * 2])
            idx = sbe("idx", [P, 4], U32)
            xg = sbe("xg", [P, 4, D])
            xgt = sbe("xgt", [P, 2, KD, P])
            hid = sbe("hid", [P, 2, FF, P])
            yb = sbe("yb", [P, D])
            yt = sbe("yt", [P, 2, D])
            l_slots = seme("slots"); l_b2 = seme("ld_b2")
            l_w1 = [seme("ld_w1_0"), seme("ld_w1_1")]
            l_w2 = [seme("ld_w2_0"), seme("ld_w2_1")]
            l_xg = [seme("ld_xg_%d" % n) for n in range(4)]
            s_idx = seme("idx"); s_xt = seme("xt"); s_xgt = seme("xgt"); s_hp = seme("hp"); s_hid = seme("hid"); s_yp = seme("yp")
            s_yb = seme("yb"); s_y = seme("y"); s_add = seme("add")
            G = 4

            @block.sync
            def _(sp):
                sp.dma_start(slots[:], slot_rows.rearrange("(p t) c -> p (t c)", p=P)).then_inc(l_slots, 16)

                def expert(t):
                    return sp.value_load(e_int[0:1, bass.ds(t, 1)], min_val=0, max_val=EXP - 1)

                def load_w1(e, a, new=None):
                    sp.dma_start(w1[:, a], d["f_w1"][bass.ds(e, 1)].rearrange("o p f -> p (o f)"), cond=new).then_inc(l_w1[a], 16)

                def load_w2(e, a, new=None):
                    sp.dma_start(w2[:, a], d["f_w2"][bass.ds(e, 1)].rearrange("o p k f -> p (o k) f"), cond=new).then_inc(l_w2[a], 16)

                for t in range(2):
                    e = expert(t)
                    load_w1(e, t)
                    load_w2(e, t)
                sp.dma_start(b2[:], d["f_b2"].partition_broadcast(P)).then_inc(l_b2, 16)
                with sp.Fori(0, TILES // 2 - 1) as i:
                    for a in range(2):
                        t = 2 * i + a
                        e = expert(t + 2)
                        new = sp.value_load(fresh[0:1, bass.ds(t + 2, 1)], min_val=0, max_val=1)
                        sp.wait_ge(s_hid, FF * (t + 1))
                        load_w1(e, a, new)
                        sp.wait_ge(s_yp, t + 1)
                        load_w2(e, a, new)
                sp.wait_ge(s_add, 16 * TILES)
                sp.dma_start(d["out"].rearrange("o n c -> (o n) c"), y_rows[0:N]).then_inc(out_done, 16)
                sp.wait_ge(out_done, 16)

            @block.gpsimd
            def _(pool):
                def gather(t, a):
                    at = pool.value_load(place[0:1, bass.ds(t, 1)], min_val=0, max_val=2 * SPAN - 2)
                    pool.tensor_copy(idx[:, a:a + 1], slots[:, bass.ds(at, 1)].bitcast(U32)).then_inc(s_idx, 1)
                    count = pool.to_reg(t + 1)
                    pool.wait_ge(l_slots, 16)
                    pool.wait_ge(s_idx, count)
                    pool.indirect_dma_start(out=xg[:, a], out_offset=None, in_=xn_rows,
                                            in_offset=bass.IndirectOffsetOnAxis(ap=idx[:, a:a + 1], axis=0)).then_inc(l_xg[a], 16)

                def add(t, a):
                    count = pool.to_reg(t + 1)
                    pool.wait_ge(l_slots, 16)
                    pool.wait_ge(s_y, count)
                    pool.indirect_dma_start(out=y_rows, out_offset=bass.IndirectOffsetOnAxis(ap=idx[:, a:a + 1], axis=0),
                                            in_=yt[:, a % 2], in_offset=None, compute_op=ALU.add).then_inc(s_add, 16)

                pool.wait_ge(l_slots, 16)
                for a in range(G - 1):
                    gather(a, a)
                with pool.Fori(0, TILES // G - 1) as i:
                    for a in range(G):
                        t = G * i + a
                        pool.wait_ge(s_add, 16 * t)
                        pool.wait_ge(s_xt, t)
                        gather(t + G - 1, (a + G - 1) % G)
                        add(t, a)
                for t in range(TILES - G, TILES):
                    pool.wait_ge(s_add, 16 * t)
                    if t + G - 1 < TILES:
                        pool.wait_ge(s_xt, t)
                        gather(t + G - 1, (t + G - 1) % G)
                    add(t, t % G)

            @block.scalar
            def _(act):
                act.preload_act_table_set("gelu_and_others")
                with act.Fori(0, TILES // 2) as i:
                    for a in range(2):
                        t = 2 * i + a
                        for b in range(2):
                            act.wait_ge(s_hp, 2 * t + b + 1)
                            for f in range(FF // 2 * b, FF // 2 * (b + 1)):
                                act.activation(hid[:, a, f, :], psum[:, 2 * a + b, (f % 4) * P:(f % 4 + 1) * P], ACT.Gelu,
                                               bias=w1[:, a, KD * F + f:KD * F + f + 1]).then_inc(s_hid, 1)
                        act.wait_ge(s_yp, t)

            @block.vector
            def _(dve):
                def turn(t, a):
                    dve.wait_ge(s_xt, t + 1)
                    dve.tensor_copy(xgt[:, a], psum[:, 6 + a, 0:D].rearrange("p (k t) -> p k t", k=KD)).then_inc(s_xgt, 1)

                def result(t, a):
                    e = dve.value_load(e_int[0:1, bass.ds(t, 1)], min_val=0, max_val=EXP - 1)
                    at = dve.value_load(place[0:1, bass.ds(t, 1)], min_val=0, max_val=2 * SPAN - 2)
                    dve.wait_ge(s_yp, t + 1)
                    dve.wait_ge(s_y, t)
                    dve.tensor_tensor(yb[:], psum[:, 4 + a, 0:D], b2[:, bass.ds(e, 1), :].rearrange("p o n -> p (o n)"), ALU.add).then_inc(s_yb, 1)
                    dve.wait_ge(s_yb, t + 1)
                    dve.tensor_scalar(yt[:, a], yb[:], slots[:, bass.ds(at + 1, 1)], None, ALU.mult).then_inc(s_y, 1)
                    dve.wait_ge(s_add, 16 * t)

                dve.wait_ge(l_slots, 16)
                dve.wait_ge(l_b2, 16)
                turn(0, 0)
                turn(1, 1)
                with dve.Fori(0, TILES // 2 - 1) as i:
                    for a in range(2):
                        t = 2 * i + a
                        dve.wait_ge(s_hp, 2 * t + 2)
                        turn(t + 2, a)
                        result(t, a)
                result(TILES - 2, 0)
                result(TILES - 1, 1)

            @block.tensor
            def _(pe):
                def turned(t, s=None, rnd=None):
                    s, rnd = (t % G, t // G + 1) if s is None else (s, rnd)
                    pe.wait_ge(l_xg[s], 16 * rnd)
                    for k in range(KD):
                        mm = pe.transpose(psum[:, 6 + s % 2, k * P:(k + 1) * P], xg[:, s, k * P:(k + 1) * P], ident)
                    mm.then_inc(s_xt, 1)

                def first(t, a, rnd):
                    pe.wait_ge(s_xgt, t + 1)
                    pe.wait_ge(l_w1[a], 16 * rnd)
                    for b in range(2):
                        for f in range(FF // 2 * b, FF // 2 * (b + 1)):
                            for k in range(KD):
                                mm = pe.matmul(psum[:, 2 * a + b, (f % 4) * P:(f % 4 + 1) * P], w1[:, a, k * F + f * P:k * F + (f + 1) * P],
                                               xgt[:, a, k, :], start=k == 0, stop=k == KD - 1)
                        mm.then_inc(s_hp, 1)

                def second(t, a, rnd):
                    pe.wait_ge(l_w2[a], 16 * rnd)
                    pe.wait_ge(s_hid, FF * (t + 1))
                    for f in range(FF):
                        mm = pe.matmul(psum[:, 4 + a, 0:D], hid[:, a, f, :], w2[:, a, f, :], start=f == 0, stop=f == FF - 1)
                    mm.then_inc(s_yp, 1)
                    pe.wait_ge(s_y, t)

                turned(0)
                first(0, 0, 1)
                turned(1)
                with pe.Fori(0, TILES // G - 1) as i:
                    for a in range(G):
                        t = G * i + a
                        pe.wait_ge(s_hid, FF * t)
                        first(t + 1, (a + 1) % 2, 2 * i + 1 + (a + 1) // 2)
                        turned(t + 2, (a + 2) % G, i + 1 + (a + 2) // G)
                        second(t, a % 2, 2 * i + 1 + a // 2)
                for t in range(TILES - G, TILES):
                    if t + 1 < TILES:
                        pe.wait_ge(s_hid, FF * t)
                        first(t + 1, (t + 1) % 2, (t + 1) // 2 + 1)
                    if t + 2 < TILES:
                        turned(t + 2)
                    second(t, t % 2, t // 2 + 1)


def layouts(i):
    rope, const = constants()

    def rows(w):
        return np.ascontiguousarray(w.reshape(-1, P, w.shape[-1]).transpose(1, 0, 2))

    def doubled(w):
        w = w.reshape(D, H, 1, HD)
        return rows(np.concatenate([w, w], axis=2).reshape(D, 2 * D))

    def column(v):
        return np.ascontiguousarray(v.reshape(-1, P).T)

    def padded(w):
        w = w.reshape(H, HD, w.shape[-1])
        return rows(np.concatenate([w, np.zeros_like(w)], axis=1).reshape(2 * D, w.shape[-1]))

    return {
        "x_t": rows(i["x"][0].T), "const": const, "rope": rope,
        "a_wq": doubled(i["L0_attn_Wq"]), "a_wk": doubled(i["L0_attn_Wk"]), "a_wv": rows(i["L0_attn_Wv"]),
        "a_wo": rows(i["L0_attn_Wo"]), "a_wg1": rows(i["L0_attn_Wg1"]), "a_wg2": np.ascontiguousarray(i["L0_attn_Wg2"]),
        "a_nw": column(i["L0_attn_norm_w"]),
        "ctx_t": rows(np.pad(i["ctx_1024"][0].T, ((0, 0), (0, KEYP - KEYS)))),
        "x_wq": rows(i["L0_xattn_W_q"].T), "x_wk": rows(i["L0_xattn_W_k"].T), "x_wv": rows(i["L0_xattn_W_v"].T),
        "x_wo": padded(i["L0_xattn_W_o"].T), "x_bq": column(i["L0_xattn_b_q"]), "x_bk": column(i["L0_xattn_b_k"]),
        "x_bv": i["L0_xattn_b_v"].reshape(D), "x_bo": column(i["L0_xattn_b_o"]),
        "f_keys": rows(i["L0_ffn_keys"].T), "f_rw": rows(i["L0_ffn_rw"].T), "f_rb": i["L0_ffn_rb"].reshape(EXP),
        "f_b2": np.ascontiguousarray(i["L0_ffn_b2"]), "rconst": routing_constants(),
        "f_w1": np.concatenate([i["L0_ffn_w1"].transpose(0, 2, 1).reshape(EXP, KD, P, F).transpose(0, 2, 1, 3).reshape(EXP, P, KD * F),
                                i["L0_ffn_b1"].reshape(EXP, FF, P).transpose(0, 2, 1)], axis=2),
        "f_w2": np.ascontiguousarray(i["L0_ffn_w2"].transpose(0, 2, 1).reshape(EXP, FF, P, D).transpose(0, 2, 1, 3)),
    }


def kernel(**inputs):
    import numpy as _np
    import concourse.bacc as _bacc
    from concourse import mybir as _mybir
    from concourse.bass_utils import run_bass_kernel_spmd as _run

    laid_out = layouts({name: _np.asarray(a) for name, a in inputs.items()})
    nc = _bacc.Bacc("TRN2", target_bir_lowering=False, num_devices=1)
    arrays, d = {}, {}
    for name, a in laid_out.items():
        arrays[f"in_{name}_dram"] = _np.ascontiguousarray(a)
        d[name] = nc.dram_tensor(f"in_{name}_dram", a.shape, _mybir.dt.from_np(a.dtype), kind="ExternalInput").ap()
    d["out"] = nc.dram_tensor("out_0_dram", (1, N, D), F32, kind="ExternalOutput").ap()
    decoder_layer(nc, d)
    r = _run(nc, [arrays], core_ids=[0])
    return r.results[0]["out_0_dram"]
```
